# Optimizing a Trainium2 kernel written in Bass

```python
import numpy as np
import jax
import jax.numpy as jnp

def _softmax(x, axis=-1):
    return jax.nn.softmax(x, axis=axis)

def _gelu(x):
    return jax.nn.gelu(x, approximate=True)

def _silu(x):
    return jax.nn.silu(x)

def _sigmoid(x):
    return jax.nn.sigmoid(x)

def _layernorm(x, axis=-1, eps=1e-05):
    m = jnp.mean(x, axis=axis, keepdims=True)
    v = jnp.var(x, axis=axis, keepdims=True)
    return (x - m) / jnp.sqrt(v + eps)

def _scatter_add(tgt, idx, src, axis=0):
    return tgt.at[idx].add(src)

def _segment_sum(src, seg, n):
    return jax.ops.segment_sum(src, seg, n)
kernel_name = 'mk_perceiver_d1_seqx_r2_32679e'

def setup_inputs(seed: int=0):
    np.random.seed(seed)
    _w = jnp.asarray

    def _rec_inputs():
        import jax
        import jax.numpy as jnp
        _rk = jax.random.key(seed)
        x = -0.0002928 + 1 * jax.random.normal(jax.random.fold_in(_rk, 1), (8, 128, 512), jnp.float32)
        _lenS = 128 - jax.random.randint(jax.random.fold_in(_rk, 7), (8,), 0, max(1, 128 // 4) + 1, jnp.int32)
        _lenS2 = 2048 - jax.random.randint(jax.random.fold_in(_rk, 8), (8,), 0, max(1, 2048 // 4) + 1, jnp.int32)
        _ctx_1024P = jax.random.normal(jax.random.fold_in(_rk, 11), (8, 16, 512), jnp.float32)
        _ctx_1024c = jax.random.dirichlet(jax.random.fold_in(_rk, 511), 0.3 * jnp.ones((16,), jnp.float32), (8, 2048))
        _ctx_1024t = jnp.einsum('bsk,bkd->bsd', _ctx_1024c, _ctx_1024P)
        _ctx_1024t = _ctx_1024t * jax.lax.rsqrt(jnp.mean(jnp.square(_ctx_1024t)) + 1e-12) * 0.953939
        ctx_1024 = 4.13588e-05 + 0.999923 * (_ctx_1024t + 0.3 * jax.random.normal(jax.random.fold_in(_rk, 611), (8, 2048, 512), jnp.float32))
        return (x, ctx_1024)
    x, ctx_1024 = _rec_inputs()

    def _L0_xattn_setup():
        import jax, jax.numpy as jnp
        import numpy as np
        FEATURE_DIM = 512
        NUM_HEADS = 16
        HEAD_DIM = FEATURE_DIM // NUM_HEADS
        key = jax.random.key(seed)
        ks = jax.random.split(key, 11)
        B, SQ, SKV, D = (4, 512, 1024, FEATURE_DIM)
        s = 1.0 / np.sqrt(D)
        return {'query': jax.random.normal(ks[0], (B, SQ, D), jnp.float32), 'key': jax.random.normal(ks[1], (B, SKV, D), jnp.float32), 'value': jax.random.normal(ks[2], (B, SKV, D), jnp.float32), 'wq': jax.random.normal(ks[3], (D, D), jnp.float32) * s, 'bq': jnp.zeros((D,), jnp.float32), 'wk': jax.random.normal(ks[4], (D, D), jnp.float32) * s, 'bk': jnp.zeros((D,), jnp.float32), 'wv': jax.random.normal(ks[5], (D, D), jnp.float32) * s, 'bv': jnp.zeros((D,), jnp.float32), 'wo': jax.random.normal(ks[6], (D, D), jnp.float32) * s, 'bo': jnp.zeros((D,), jnp.float32)}
    _L0_xattn_all = _L0_xattn_setup()
    _L0_xattn_in = {k: v for k, v in _L0_xattn_all.items() if k in ('wq', 'bq', 'wk', 'bk', 'wv', 'bv', 'wo', 'bo')}
    del _L0_xattn_all

    def _L0_attn_setup():
        import jax, jax.numpy as jnp
        import numpy as np
        D_MODEL = 512
        NUM_HEADS = 16
        D_HEAD = D_MODEL // NUM_HEADS
        LAMBDA_INIT = 0.8
        EPS = 1e-05
        B, N = (4, 512)
        key = jax.random.key(seed)
        ks = jax.random.split(key, 10)
        w_scale = 1.0 / np.sqrt(D_MODEL)
        d2 = 2 * D_HEAD * NUM_HEADS
        return {'X': jax.random.normal(ks[0], (B, N, D_MODEL), jnp.float32), 'Wq': jax.random.normal(ks[1], (d2, D_MODEL), jnp.float32) * w_scale, 'Wk': jax.random.normal(ks[2], (d2, D_MODEL), jnp.float32) * w_scale, 'Wv': jax.random.normal(ks[3], (d2, D_MODEL), jnp.float32) * w_scale, 'Wo': jax.random.normal(ks[4], (D_MODEL, d2), jnp.float32) * w_scale, 'lq1': jax.random.normal(ks[5], (NUM_HEADS, D_HEAD), jnp.float32), 'lk1': jax.random.normal(ks[6], (NUM_HEADS, D_HEAD), jnp.float32), 'lq2': jax.random.normal(ks[7], (NUM_HEADS, D_HEAD), jnp.float32), 'lk2': jax.random.normal(ks[8], (NUM_HEADS, D_HEAD), jnp.float32), 'rms_scale': jnp.ones((2 * D_HEAD,), jnp.float32)}
    _L0_attn_all = _L0_attn_setup()
    _L0_attn_in = {k: v for k, v in _L0_attn_all.items() if k in ('Wq', 'Wk', 'Wv', 'Wo', 'lq1', 'lk1', 'lq2', 'lk2', 'rms_scale')}
    del _L0_attn_all

    def _L0_ffn_setup():
        import jax, jax.numpy as jnp
        import numpy as np
        THRESHOLD = 0.1
        key = jax.random.key(seed)
        k1, k2, k3 = jax.random.split(key, 3)
        B, S, D, E = (4, 2048, 512, 8)
        inputs = jax.random.normal(k1, (B, S, D), dtype=jnp.float32)
        gate_w = jax.random.normal(k2, (D, E), dtype=jnp.float32) * 0.02
        gate_b = jnp.zeros((E,), dtype=jnp.float32)
        expert_w = jax.random.normal(k3, (E, D, D), dtype=jnp.float32) * 0.02
        expert_b = jnp.zeros((E, D), dtype=jnp.float32)
        return {'inputs': inputs, 'gate_w': gate_w, 'gate_b': gate_b, 'expert_w': expert_w, 'expert_b': expert_b}
    _L0_ffn_all = _L0_ffn_setup()
    _L0_ffn_in = {k: v for k, v in _L0_ffn_all.items() if k in ('gate_w', 'gate_b', 'expert_w', 'expert_b')}
    del _L0_ffn_all
    return {'x': x, 'ctx_1024': ctx_1024, 'L0_xattn_wq': _L0_xattn_in['wq'], 'L0_xattn_bq': _L0_xattn_in['bq'], 'L0_xattn_wk': _L0_xattn_in['wk'], 'L0_xattn_bk': _L0_xattn_in['bk'], 'L0_xattn_wv': _L0_xattn_in['wv'], 'L0_xattn_bv': _L0_xattn_in['bv'], 'L0_xattn_wo': _L0_xattn_in['wo'], 'L0_xattn_bo': _L0_xattn_in['bo'], 'L0_attn_Wq': _L0_attn_in['Wq'], 'L0_attn_Wk': _L0_attn_in['Wk'], 'L0_attn_Wv': _L0_attn_in['Wv'], 'L0_attn_Wo': _L0_attn_in['Wo'], 'L0_attn_lq1': _L0_attn_in['lq1'], 'L0_attn_lk1': _L0_attn_in['lk1'], 'L0_attn_lq2': _L0_attn_in['lq2'], 'L0_attn_lk2': _L0_attn_in['lk2'], 'L0_attn_rms_scale': _L0_attn_in['rms_scale'], 'L0_ffn_gate_w': _L0_ffn_in['gate_w'], 'L0_ffn_gate_b': _L0_ffn_in['gate_b'], 'L0_ffn_expert_w': _L0_ffn_in['expert_w'], 'L0_ffn_expert_b': _L0_ffn_in['expert_b']}

def reference(x, ctx_1024, L0_xattn_wq, L0_xattn_bq, L0_xattn_wk, L0_xattn_bk, L0_xattn_wv, L0_xattn_bv, L0_xattn_wo, L0_xattn_bo, L0_attn_Wq, L0_attn_Wk, L0_attn_Wv, L0_attn_Wo, L0_attn_lq1, L0_attn_lk1, L0_attn_lq2, L0_attn_lk2, L0_attn_rms_scale, L0_ffn_gate_w, L0_ffn_gate_b, L0_ffn_expert_w, L0_ffn_expert_b):
    import jax
    import jax.numpy as jnp

    def _L0_xattn_ref(query, key, value, wq, bq, wk, bk, wv, bv, wo, bo):
        import jax, jax.numpy as jnp
        import numpy as np
        FEATURE_DIM = 512
        NUM_HEADS = 16
        HEAD_DIM = FEATURE_DIM // NUM_HEADS
        B, SQ, D = query.shape
        H, HD = (NUM_HEADS, HEAD_DIM)
        q = (query @ wq.T + bq).reshape(B, SQ, H, HD).transpose(0, 2, 1, 3)
        k = (key @ wk.T + bk).reshape(B, -1, H, HD).transpose(0, 2, 1, 3)
        v = (value @ wv.T + bv).reshape(B, -1, H, HD).transpose(0, 2, 1, 3)
        scores = jnp.einsum('bhqd,bhkd->bhqk', q, k) / jnp.sqrt(jnp.asarray(HD, q.dtype))
        attn = jax.nn.softmax(scores, axis=-1)
        ctx = jnp.einsum('bhqk,bhkd->bhqd', attn, v)
        ctx = ctx.transpose(0, 2, 1, 3).reshape(B, SQ, D)
        return ctx @ wo.T + bo

    def _L0_attn_ref(X, Wq, Wk, Wv, Wo, lq1, lk1, lq2, lk2, rms_scale):
        import jax, jax.numpy as jnp
        import numpy as np
        D_MODEL = 512
        NUM_HEADS = 16
        D_HEAD = D_MODEL // NUM_HEADS
        LAMBDA_INIT = 0.8
        EPS = 1e-05
        B, N = (4, 512)
        b, n, _ = X.shape
        H, dh = (NUM_HEADS, D_HEAD)

        def proj(W):
            return (X @ W.T).reshape(b, n, H, 2 * dh).transpose(0, 2, 1, 3)
        Q, K, V = (proj(Wq), proj(Wk), proj(Wv))
        Q1, Q2 = jnp.split(Q, 2, axis=-1)
        K1, K2 = jnp.split(K, 2, axis=-1)
        lam = jnp.exp(jnp.sum(lq1 * lk1, axis=-1)) - jnp.exp(jnp.sum(lq2 * lk2, axis=-1)) + LAMBDA_INIT
        lam = lam[None, :, None, None]
        scaling = 1.0 / np.sqrt(dh)
        causal = jnp.tril(jnp.ones((n, n), bool))
        A1 = jnp.where(causal, jnp.einsum('bhnd,bhmd->bhnm', Q1, K1) * scaling, -jnp.inf)
        A2 = jnp.where(causal, jnp.einsum('bhnd,bhmd->bhnm', Q2, K2) * scaling, -jnp.inf)
        attn = jax.nn.softmax(A1, axis=-1) - lam * jax.nn.softmax(A2, axis=-1)
        O = jnp.einsum('bhnm,bhmd->bhnd', attn, V)
        rms = jnp.sqrt(jnp.mean(O * O, axis=-1, keepdims=True) + EPS)
        O = O / rms * rms_scale * (1.0 - LAMBDA_INIT)
        Oc = O.transpose(0, 2, 1, 3).reshape(b, n, H * 2 * dh)
        return Oc @ Wo.T

    def _L0_ffn_ref(inputs, gate_w, gate_b, expert_w, expert_b):
        import jax, jax.numpy as jnp
        import numpy as np
        THRESHOLD = 0.1
        d = inputs.shape[-1]
        x = inputs.reshape(-1, d)
        gate_logits = jax.nn.softmax(x @ gate_w + gate_b, axis=-1)
        selected = (gate_logits >= THRESHOLD).astype(x.dtype)
        weights = gate_logits * selected
        wsum = jnp.sum(weights, axis=-1, keepdims=True)
        weights = weights / jnp.where(wsum == 0, jnp.ones_like(wsum), wsum)
        E = expert_w.shape[0]
        out = jnp.zeros((x.shape[0], expert_w.shape[-1]), dtype=x.dtype)
        for e in range(E):
            out = out + weights[:, e:e + 1] * (x @ expert_w[e] + expert_b[e])
        return out.reshape(*inputs.shape[:-1], out.shape[-1])
    x = x + _L0_xattn_ref(_layernorm(x, axis=-1), ctx_1024, ctx_1024, L0_xattn_wq, L0_xattn_bq, L0_xattn_wk, L0_xattn_bk, L0_xattn_wv, L0_xattn_bv, L0_xattn_wo, L0_xattn_bo)
    x = x + _L0_attn_ref(_layernorm(x, axis=-1), L0_attn_Wq, L0_attn_Wk, L0_attn_Wv, L0_attn_Wo, L0_attn_lq1, L0_attn_lk1, L0_attn_lq2, L0_attn_lk2, L0_attn_rms_scale)
    x = x + _L0_ffn_ref(_layernorm(x, axis=-1), L0_ffn_gate_w, L0_ffn_gate_b, L0_ffn_expert_w, L0_ffn_expert_b)
    return x

_drawn_inputs = setup_inputs


def setup_inputs(seed=0):
    import zlib

    import numpy as np

    out = dict(_drawn_inputs(seed))
    spreads = {'L0_xattn_bq': (0.0, 0.356),
     'L0_xattn_bk': (0.0, 0.8),
     'L0_xattn_bv': (0.0, 0.1),
     'L0_xattn_bo': (0.0, 0.1),
     'L0_attn_rms_scale': (1.0, 0.2),
     'L0_ffn_gate_b': (0.0, 0.1),
     'L0_ffn_expert_b': (0.0, 0.1)}
    factors = {}
    for name, (base, spread) in spreads.items():
        noise = np.random.default_rng([zlib.crc32(name.encode()), seed]).standard_normal(out[name].shape)
        drawn = base * np.exp(spread * noise) if base else spread * noise
        out[name] = jnp.asarray(drawn.astype(out[name].dtype))
    for name, factor in factors.items():
        out[name] = (out[name] * factor).astype(out[name].dtype)
    return out
```

```python
from contextlib import ExitStack

import numpy as np

import concourse.bass as bass
from concourse import mybir

F32 = mybir.dt.float32
F32R = mybir.dt.float32r
ALU = mybir.AluOpType
ACT = mybir.ActivationFunctionType
AX = mybir.AxisListType
RMAX = bass.bass_isa.ReduceOp.max

P = 128
B = 8
D = 512
KD = D // P
KV = 2048
NB = KV // P
HD = 32
G = D // P
HG = P // HD
TOK = B * P
EPS = 1e-5
SCALE = float(1.0 / np.sqrt(np.float32(HD)))
HEADS = 16
W2 = 2 * HD * HEADS
KB = W2 // P
LAMBDA_INIT = 0.8
NE = 8
THRESHOLD = 0.1
MASKED = -3.0e38



def product(nc, out, lhs, rhs, first, last):
    nc.tensor.matmul(out, lhs[0], rhs[0], start=first, stop=False)
    nc.tensor.matmul(out, lhs[0], rhs[1], start=False, stop=False)
    return nc.tensor.matmul(out, lhs[1], rhs[0], start=False, stop=last)


def f32(ap):
    return ap.bitcast(F32)


def make_identity(nc, pool, ident, step):
    nc.gpsimd.memset(ident[:, :], 0.0).then_inc(step, 1)
    pool.wait_ge(step, 1)
    nc.gpsimd.affine_select(out=ident[:, :], in_=ident[:, :], compare_op=ALU.not_equal, fill=1.0,
                            base=0, pattern=[[-1, P]], channel_multiplier=1).then_inc(step, 1)


class Norm:

    def __init__(self, nc, ctx, name):
        self.nc = nc
        self.stats = ctx.enter_context(nc.sbuf_tensor(f"{name}_stats", [P, B, 6], F32))
        self.mv = ctx.enter_context(nc.sbuf_tensor(f"{name}_mv", [P, B, 2], F32))
        self.veps = ctx.enter_context(nc.sbuf_tensor(f"{name}_veps", [P, B], F32))
        self.root = ctx.enter_context(nc.sbuf_tensor(f"{name}_root", [P, B], F32))
        self.rstd = ctx.enter_context(nc.sbuf_tensor(f"{name}_rstd", [P, B], F32))
        self.tmp = ctx.enter_context(nc.sbuf_tensor(f"{name}_tmp", [P, B], F32))
        self.step = ctx.enter_context(nc.semaphore(f"{name}_step"))
        self.root_ready = ctx.enter_context(nc.semaphore(f"{name}_root_ready"))

    STEPS_TO_VEPS = B + B + 1
    STEPS = STEPS_TO_VEPS + 5

    def vector(self, dve, x):
        nc = self.nc
        for t in range(B):
            nc.vector.bn_stats(self.stats[:, t, :], x[:, t, :]).then_inc(self.step, 1)
        for t in range(B):
            dve.wait_ge(self.step, t + 1)
            nc.vector.bn_aggr(self.mv[:, t, :], self.stats[:, t, :]).then_inc(self.step, 1)
        dve.wait_ge(self.step, 2 * B)
        nc.vector.tensor_scalar(self.veps[:, :], self.mv[:, :, 1], EPS, None, ALU.add).then_inc(self.step, 1)
        inv_root(nc, dve, self, self.STEPS_TO_VEPS)

    def scalar(self, act):
        act.wait_ge(self.step, self.STEPS_TO_VEPS)
        self.nc.scalar.activation(self.root[:, :], self.veps[:, :], ACT.Sqrt).then_inc(self.root_ready, 1)

    def apply(self, x, out, t):
        return self.nc.vector.tensor_scalar(out, x, self.mv[:, t, 0:1], self.rstd[:, t:t + 1],
                                            ALU.subtract, ALU.mult)


def inv_root(nc, dve, n, steps):
    dve.wait_ge(n.root_ready, 1)
    nc.vector.reciprocal(n.rstd[:, :], n.root[:, :]).then_inc(n.step, 1)
    dve.wait_ge(n.step, steps + 1)
    nc.vector.tensor_tensor(n.tmp[:, :], n.rstd[:, :], n.rstd[:, :], ALU.mult).then_inc(n.step, 1)
    dve.wait_ge(n.step, steps + 2)
    nc.vector.tensor_tensor(n.tmp[:, :], n.tmp[:, :], n.veps[:, :], ALU.mult).then_inc(n.step, 1)
    dve.wait_ge(n.step, steps + 3)
    nc.vector.tensor_scalar(n.tmp[:, :], n.tmp[:, :], -0.5, 1.5, ALU.mult, ALU.add).then_inc(n.step, 1)
    dve.wait_ge(n.step, steps + 4)
    nc.vector.tensor_tensor(n.rstd[:, :], n.rstd[:, :], n.tmp[:, :], ALU.mult).then_inc(n.step, 1)


def queries_and_weights(nc, x, w, q_d, wkT, wvT):
    with ExitStack() as ctx:
        def sb(name, shape, dt=F32):
            return ctx.enter_context(nc.sbuf_tensor(name, shape, dt))

        def sem(name):
            return ctx.enter_context(nc.semaphore(name))

        ident = sb("a_ident", [P, P])
        x_sb = sb("a_x", [P, B, D])
        xn = sb("a_xn", [P, B, D])
        w_sb = sb("a_w", [P, 3, KD, D])
        bq = sb("a_bq", [P, KD])
        wqT = [sb(f"a_wqT{i}", [P, KD, D], F32R) for i in range(2)]
        xT = [sb(f"a_xT{i}", [P, KD, TOK], F32R) for i in range(2)]
        q_st = sb("a_q", [P, 2, 2, TOK], F32R)
        bank = [ctx.enter_context(nc.psum_tensor(f"a_ps{i}", [P, 512], F32)) for i in range(4)]
        norm = Norm(nc, ctx, "a_norm")
        const = sem("a_const")
        x_in = sem("a_x_in")
        b_in = sem("a_b_in")
        w_in = [sem(f"a_w_in{i}") for i in range(3)]
        full = sem("a_full")
        hi_done = sem("a_hi")
        lo_done = sem("a_lo")
        normed = sem("a_normed")
        q_out = [sem(f"a_q_out{i}") for i in range(2)]
        weights = ((w["wk"], wkT), (w["wv"], wvT), (w["wq"], wqT))
        U_W, U_X, U_Q, U_END = 0, 12, 20, 28
        block = ctx.enter_context(nc.Block())

        @block.sync
        def _(sp):
            sp.dma_start(x_sb[:, :, :], x.rearrange("b p d -> p b d")).then_inc(x_in, 16)
            for i, (src, _) in enumerate(weights):
                sp.dma_start(w_sb[:, i, :, :], src.rearrange("(o p) d -> p o d", p=P)).then_inc(w_in[i], 16)
            with nc.allow_non_contiguous_dma(reason="512 numbers"):
                sp.dma_start(bq[:, :], w["bq"].rearrange("(g p) -> p g", p=P)).then_inc(b_in, 16)
            for g in range(G):
                sp.wait_ge(lo_done, U_Q + 2 * g + 2)
                for i in range(2):
                    sp.dma_start(f32(q_d[g, :, :, i, :]).rearrange("b p t -> p b t"),
                                 f32(q_st[:, g % 2, i, :]).rearrange("p (b t) -> p b t", b=B)
                                 ).then_inc(q_out[g % 2], 16)
            for i in range(2):
                sp.wait_ge(q_out[i], 16 * 2 * (G // 2))

        @block.gpsimd
        def _(pool):
            make_identity(nc, pool, ident, const)

        @block.tensor
        def _(pe):
            pe.wait_ge(const, 2)
            u = 0
            for i in range(3):
                pe.wait_ge(w_in[i], 16)
                for k in range(KD):
                    if u >= 4:
                        pe.wait_ge(lo_done, u - 3)
                    for o in range(KD):
                        last = nc.tensor.transpose(bank[u % 4][:, o * P:(o + 1) * P],
                                                   w_sb[:, i, o, k * P:(k + 1) * P], ident[:, :])
                    last.then_inc(full, 1)
                    u += 1
            for half in range(2):
                pe.wait_ge(normed, 4 * half + 4)
                for k in range(KD):
                    pe.wait_ge(lo_done, u - 3)
                    for t in range(4):
                        last = nc.tensor.transpose(bank[u % 4][:, t * P:(t + 1) * P],
                                                   xn[:, 4 * half + t, k * P:(k + 1) * P], ident[:, :])
                    last.then_inc(full, 1)
                    u += 1
            pe.wait_ge(lo_done, U_Q)
            for g in range(G):
                for half in range(2):
                    pe.wait_ge(lo_done, u - 3)
                    for k in range(KD):
                        last = product(nc, bank[u % 4][:, :], [a[:, k, g * P:(g + 1) * P] for a in wqT],
                                       [a[:, k, half * 512:(half + 1) * 512] for a in xT], k == 0, k == KD - 1)
                    last.then_inc(full, 1)
                    u += 1

        def places():
            for _, dst in weights:
                for k in range(KD):
                    yield [a[:, k, :] for a in dst]
            for half in range(2):
                for k in range(KD):
                    yield [a[:, k, half * 512:(half + 1) * 512] for a in xT]
            for g in range(G):
                for half in range(2):
                    yield [q_st[:, g % 2, i, half * 512:(half + 1) * 512] for i in range(2)]

        @block.scalar
        def _(act):
            for u, (hi, _) in enumerate(places()):
                if u == 4:
                    norm.scalar(act)
                act.wait_ge(full, u + 1)
                if u < U_Q:
                    nc.scalar.activation(hi, bank[u % 4][:, :], ACT.Copy).then_inc(hi_done, 1)
                else:
                    g = (u - U_Q) // 2
                    if u == U_Q:
                        act.wait_ge(b_in, 16)
                    if g >= 2:
                        act.wait_ge(q_out[g % 2], 32)
                    nc.scalar.activation(hi, bank[u % 4][:, :], ACT.Identity,
                                         bias=bq[:, g:g + 1]).then_inc(hi_done, 1)

        @block.vector
        def _(dve):
            dve.wait_ge(x_in, 16)
            for u, (hi, lo) in enumerate(places()):
                if u == 4:
                    norm.vector(dve, x_sb)
                    dve.wait_ge(norm.step, norm.STEPS)
                    for t in range(B):
                        norm.apply(x_sb[:, t, :], xn[:, t, :], t).then_inc(normed, 1)
                dve.wait_ge(hi_done, u + 1)
                if u < U_Q:
                    nc.vector.tensor_tensor(lo, bank[u % 4][:, :], f32(hi), ALU.subtract).then_inc(lo_done, 1)
                else:
                    g = (u - U_Q) // 2
                    if u == U_Q:
                        dve.wait_ge(b_in, 16)
                    nc.vector.scalar_tensor_tensor(out=lo, in0=bank[u % 4][:, :], scalar=bq[:, g:g + 1],
                                                   in1=f32(hi), op0=ALU.add, op1=ALU.subtract).then_inc(lo_done, 1)


def cross_attention(nc, ctx_in, w, q_d, o_d, wkT, wvT):
    with ExitStack() as ctx:
        def sb(name, shape, dt=F32):
            return ctx.enter_context(nc.sbuf_tensor(name, shape, dt))

        def sem(name):
            return ctx.enter_context(nc.semaphore(name))

        CH = 2
        NCH = NB // CH
        T_UNITS = NCH * 2
        K_UNITS = KV // 512
        V_UNITS = NB
        U_N = (G - 1) * K_UNITS
        U_V = U_N + T_UNITS + K_UNITS
        UNITS = U_V + V_UNITS
        PRE = T_UNITS + K_UNITS + V_UNITS
        SPLITS = U_V
        PRE_SPLITS = T_UNITS + K_UNITS
        SUMS = NB // 2 - 1
        PAIRS = NB // 2
        AHEAD = 4
        NEXT = ([("T", n) for n in range(4)]
                + [x for c in range(K_UNITS - 1) for x in [("T", 4 * c + 4 + n) for n in range(4)] + [("K", c)]]
                + [("K", K_UNITS - 1)])
        AT = {x: i for i, x in enumerate(NEXT)}
        SHARES = [0, 5, 8, 11, 14, 16, 18, 19, 20]
        KEYS_AT = {0: 0, 1: 1, 3: 2, 4: 3}

        ident = sb("b_ident", [P, P])
        ones = sb("b_ones", [P, HD])
        bk = sb("b_bk", [P, G])
        bv = sb("b_bv", [P, G])
        cin = sb("b_cin", [P, 2, CH, D])
        cT = [sb(f"b_cT{i}", [P, KD, KV], F32R) for i in range(2)]
        kT = [sb(f"b_kT{i}", [P, KV], F32R) for i in range(2)]
        v = sb("b_v", [P, NB, D])
        s = sb("b_s", [P, NB, HG * P])
        qbd = sb("b_qbd", [P, 2, 2, HG, P], F32R)
        mx = sb("b_mx", [P, 2, HG * P])
        mb = sb("b_mb", [P, HG * P])
        acc = sb("b_acc", [P, 2, HG * P])
        rD = sb("b_rD", [P, P])
        oq = sb("b_oq", [P, P])
        o_st = sb("b_o", [P, 2, P])
        work = [ctx.enter_context(nc.psum_tensor(f"b_work{i}", [P, 512], F32)) for i in range(2)]
        psS = [ctx.enter_context(nc.psum_tensor(f"b_psS{i}", [P, 512], F32)) for i in range(4)]
        psO = [ctx.enter_context(nc.psum_tensor(f"b_psO{i}", [P, 512], F32)) for i in range(2)]

        const = sem("b_const")
        bias_in = sem("b_bias_in")
        cin_in = [sem(f"b_cin_in{i}") for i in range(2)]
        q_in = [sem(f"b_q_in{i}") for i in range(2)]
        work_full = sem("b_work_full")
        hi_done = sem("b_hi_done")
        split_done = sem("b_split_done")
        v_done = sem("b_v_done")
        s_full = sem("b_s_full")
        mx_done = sem("b_mx_done")
        s_moved = sem("b_s_moved")
        fold_done = sem("b_fold_done")
        par_begun = sem("b_par_begun")
        par_done = sem("b_par_done")
        sub_done = sem("b_sub_done")
        exp_done = sem("b_exp_done")
        pv_done = sem("b_pv_done")
        sum_done = sem("b_sum_done")
        od_full = sem("b_od_full")
        rd_done = sem("b_rd_done")
        od_free = sem("b_od_free")
        o_out = sem("b_o_out")
        o_stored = sem("b_o_stored")
        block = ctx.enter_context(nc.Block())

        def split_no(b, i):
            return b * SPLITS + (PRE_SPLITS + i + 1)

        def full_no(b, i):
            return b * UNITS + (PRE + i + 1)

        def v_no(b, i):
            return b * V_UNITS + (V_UNITS + i - U_V + 1)

        @block.sync
        def _(sp):
            sp.sem_inc(o_stored, 2)
            with nc.allow_non_contiguous_dma(reason="512 numbers"):
                sp.dma_start(bk[:, :], w["bk"].rearrange("(g p) -> p g", p=P)).then_inc(bias_in, 16)
                sp.dma_start(bv[:, :], w["bv"].rearrange("(g p) -> p g", p=P)).then_inc(bias_in, 16)

            def load_context(b, c):
                sp.dma_start(cin[:, c % 2, :, :],
                             ctx_in[b, c * CH * P:(c + 1) * CH * P, :].rearrange("(o p) d -> p o d", p=P)
                             ).then_inc(cin_in[c % 2], 16)

            def load_queries(b, g):
                for j in range(HG):
                    sp.dma_start(f32(qbd[j * HD:(j + 1) * HD, g % 2, :, j, :]),
                                 f32(q_d[g, b, j * HD:(j + 1) * HD, :, :])).then_inc(q_in[g % 2], 16)

            def store_output(b, g):
                sp.wait_ge(od_free, b * G + (g + 1 + 2))
                sp.dma_start(o_d[g, b, :, :], o_st[:, g % 2, :]).then_inc(o_out, 16)
                sp.wait_ge(o_out, b * (16 * G) + 16 * (g + 1))
                sp.sem_inc(o_stored, 1)

            for c in range(NCH):
                if c >= 2:
                    sp.wait_ge(work_full, AT["T", 2 * (c - 2) + 1] + 1)
                load_context(0, c)
                if c == 1:
                    sp.wait_ge(const, 4)
                    load_queries(0, 0)
                    load_queries(0, 1)

            def batch(b, last):
                if not last:
                    sp.wait_ge(work_full, b * UNITS + PRE_SPLITS)
                    load_context(b + 1, 0)
                    load_context(b + 1, 1)
                for g in range(G):
                    if g < G - 2 or not last:
                        sp.wait_ge(s_full, b * (G * NB) + NB * (g + 1))
                        load_queries(b + (g + 2) // G, (g + 2) % G)
                    if g >= 1:
                        store_output(b, g - 1)
                if not last:
                    for c in range(2, NCH):
                        sp.wait_ge(work_full, full_no(b, U_N + AT["T", 2 * (c - 2) + 1]))
                        load_context(b + 1, c)
                store_output(b, G - 1)

            with sp.Fori(0, B - 1) as b:
                batch(b, False)
            batch(B - 1, True)

        @block.gpsimd
        def _(pool):
            pool.sem_inc(sum_done, SUMS)
            pool.sem_inc(par_done, 1)
            make_identity(nc, pool, ident, const)
            nc.gpsimd.memset(ones[:, :], 1.0).then_inc(const, 1)
            nc.gpsimd.memset(f32(qbd[:, :, :, :, :]), 0.0).then_inc(const, 1)

            def batch(b):
                for g in range(G):
                    pool.wait_ge(fold_done, b * G + (g + 1))
                    pool.sem_inc(par_begun, 1)
                    nc.gpsimd.partition_all_reduce(mb[:, :], mx[:, 0, :], P, RMAX).then_inc(par_done, 1)
                    for i in range(SUMS):
                        pool.wait_ge(exp_done, b * (G * PAIRS) + (g * PAIRS + i + 2))
                        if i == 0:
                            pool.wait_ge(od_full, b * G + (g + 1))
                            a = s[:, 0:2, :]
                        else:
                            pool.wait_ge(sum_done, b * (G * SUMS) + (SUMS + g * SUMS + i))
                            a = acc[:, :, :]
                        nc.gpsimd.tensor_tensor(acc[:, :, :], a, s[:, 2 * i + 2:2 * i + 4, :],
                                                ALU.add).then_inc(sum_done, 1)

            with pool.Fori(0, B) as b:
                batch(b)

        @block.tensor
        def _(pe):
            pe.sem_inc(od_full, 1)
            pe.sem_inc(pv_done, 1)
            pe.wait_ge(const, 4)

            def bank_free(b, i):
                if i - 2 < 0:
                    pe.wait_ge(v_done, v_no(b, U_V + V_UNITS + i - 2) - V_UNITS)
                elif i - 2 < U_V:
                    pe.wait_ge(split_done, split_no(b, i - 2))
                else:
                    pe.wait_ge(v_done, v_no(b, i - 2))

            def next_context(bn, first_unit, free, split_before):
                for i, (kind, n) in enumerate(NEXT):
                    bank = work[(first_unit + i) % 2]
                    free(first_unit + i)
                    if kind == "K":
                        pe.wait_ge(split_done, split_before + (AT["T", 4 * n + 3] + 1))
                        last = keys_bank(bank, 0, n)
                    else:
                        c, kk = n // 2, n % 2
                        if kk == 0:
                            pe.wait_ge(cin_in[c % 2], bn * (16 * NCH // 2) + 16 * (c // 2 + 1))
                        for k in range(2):
                            for o in range(CH):
                                last = nc.tensor.transpose(bank[:, (k * CH + o) * P:(k * CH + o + 1) * P],
                                                           cin[:, c % 2, o, (2 * kk + k) * P:(2 * kk + k + 1) * P],
                                                           ident[:, :])
                    last.then_inc(work_full, 1)

            def keys_bank(bank, g, c):
                for k in range(KD):
                    last = product(nc, bank[:, :], [a[:, k, g * P:(g + 1) * P] for a in wkT],
                                   [a[:, k, c * 512:(c + 1) * 512] for a in cT], k == 0, k == KD - 1)
                return last

            def keys(b, g):
                for c in range(K_UNITS):
                    i = (g - 1) * K_UNITS + c
                    bank_free(b, i)
                    keys_bank(work[i % 2], g, c).then_inc(work_full, 1)

            def values(first_unit, free):
                for t in range(V_UNITS):
                    i = first_unit + t
                    free(i)
                    for k in range(KD):
                        last = product(nc, work[i % 2][:, :], [a[:, k, t * P:(t + 1) * P] for a in cT],
                                       [a[:, k, :] for a in wvT], k == 0, k == KD - 1)
                    last.then_inc(work_full, 1)

            def scores(b, g, blocks):
                if 0 in blocks:
                    pe.wait_ge(q_in[g % 2], b * (16 * HG * 2) + 16 * HG * (g // 2 + 1))
                for t in blocks:
                    if t % 4 == 0:
                        pe.wait_ge(split_done, split_no(b, (g - 1) * K_UNITS + t // 4) if g
                                   else b * SPLITS + (AT["K", t // 4] + 1))
                    pe.wait_ge(s_moved, b * (G * NB) + (g * NB + t + 1))
                    product(nc, psS[t % 4][:, :], [a[:, t * P:(t + 1) * P] for a in kT],
                            [qbd[:, g % 2, i, :, :] for i in range(2)], True, True).then_inc(s_full, 1)

            def outputs(b, g):
                if g == 0:
                    pe.wait_ge(v_done, b * V_UNITS + V_UNITS)
                pe.wait_ge(od_free, b * G + (g + 1))
                for t in range(NB):
                    if t % 2 == 0:
                        pe.wait_ge(exp_done, b * (G * PAIRS) + (g * PAIRS + t // 2 + 1))
                    for j in range(HG):
                        h = slice(j * HD, (j + 1) * HD)
                        last = nc.tensor.matmul(psO[g % 2][h, 0:P], v[:, t, g * P + j * HD:g * P + (j + 1) * HD],
                                                s[:, t, j * P:(j + 1) * P], start=t == 0, stop=t == NB - 1)
                last.then_inc(pv_done, 1)

            def denominators(b, g):
                pe.wait_ge(sum_done, b * (G * SUMS) + (SUMS + (g + 1) * SUMS))
                for i in range(2):
                    for j in range(HG):
                        last = nc.tensor.matmul(psO[g % 2][j * HD:(j + 1) * HD, P:2 * P], ones[:, :],
                                                acc[:, i, j * P:(j + 1) * P], start=i == 0, stop=i == 1)
                last.then_inc(od_full, 1)

            def batch(b, last):
                for g in range(G):
                    scores(b, g, range(AHEAD, NB))
                    if g >= 1:
                        denominators(b, g - 1)
                    if g < G - 1:
                        keys(b, g + 1)
                        scores(b, g + 1, range(AHEAD))
                    elif not last:
                        next_context(b + 1, U_N, lambda i: bank_free(b, i), b * SPLITS + (PRE_SPLITS + U_N))
                        scores(b + 1, 0, range(AHEAD))
                    outputs(b, g)
                if not last:
                    values(U_V, lambda i: bank_free(b, i))
                denominators(b, G - 1)

            def pre_free(i):
                if i - 2 >= PRE_SPLITS:
                    pe.wait_ge(v_done, i - 2 - PRE_SPLITS + 1)
                elif i >= 2:
                    pe.wait_ge(split_done, i - 1)

            next_context(0, 0, pre_free, 0)
            values(PRE_SPLITS, pre_free)
            scores(0, 0, range(AHEAD))
            with pe.Fori(0, B - 1) as b:
                batch(b, False)
            batch(B - 1, True)

        def context_place(a, n):
            c, kk = n // 2, n % 2
            return a[:, 2 * kk:2 * kk + 2, c * CH * P:(c + 1) * CH * P]

        def share(q):
            return range(SHARES[q], SHARES[q + 1])

        def two(ps):
            return ps[:, :].rearrange("p (k t) -> p k t", k=2)

        @block.scalar
        def _(act):
            act.sem_inc(s_moved, 4)

            def context_hi(n, i, full):
                act.wait_ge(work_full, full)
                nc.scalar.activation(context_place(cT[0], n), two(work[i % 2]), ACT.Copy).then_inc(hi_done, 1)

            def keys_hi(g, c, i, full):
                act.wait_ge(work_full, full)
                nc.scalar.activation(kT[0][:, c * 512:(c + 1) * 512], work[i % 2][:, :], ACT.Identity,
                                     bias=bk[:, g:g + 1]).then_inc(hi_done, 1)

            def value_copy(t, i, full):
                act.wait_ge(work_full, full)
                nc.scalar.activation(v[:, t, :], work[i % 2][:, :], ACT.Copy).then_inc(v_done, 1)

            def next_hi(first_unit, full_before, units):
                for i in units:
                    kind, n = NEXT[i]
                    if kind == "T":
                        context_hi(n, first_unit + i, full_before + (i + 1))
                    else:
                        keys_hi(0, n, first_unit + i, full_before + (i + 1))

            def exps(b, g, q):
                act.wait_ge(sub_done, b * (G * PAIRS) + (g * PAIRS + q + 1))
                pair = s[:, 2 * q:2 * q + 2, :]
                nc.scalar.activation(pair, pair, ACT.Exp, scale=SCALE).then_inc(exp_done, 1)

            act.wait_ge(bias_in, 32)
            next_hi(0, 0, range(PRE_SPLITS))
            for t in range(V_UNITS):
                value_copy(t, PRE_SPLITS + t, PRE_SPLITS + t + 1)

            def batch(b, last):
                for g in range(G):
                    act.wait_ge(pv_done, b * G + (g + 1))
                    for t in range(NB):
                        act.wait_ge(mx_done, b * (G * NB) + (g * NB + t + 1))
                        if t % 2 == 0:
                            act.wait_ge(sum_done, b * (G * SUMS) + (g * SUMS + max(1, t // 2)))
                        nc.scalar.activation(s[:, t, :], psS[t % 4][:, :], ACT.Copy).then_inc(s_moved, 1)
                    for q in range(PAIRS + 1):
                        if q < PAIRS and g < G - 1:
                            if q in KEYS_AT:
                                i = g * K_UNITS + KEYS_AT[q]
                                keys_hi(g + 1, KEYS_AT[q], i, full_no(b, i))
                        elif q < PAIRS and not last:
                            next_hi(U_N, b * UNITS + (PRE + U_N), share(q))
                        if q >= 1:
                            exps(b, g, q - 1)
                if not last:
                    for t in range(V_UNITS):
                        value_copy(t, U_V + t, full_no(b, U_V + t))

            with act.Fori(0, B - 1) as b:
                batch(b, False)
            batch(B - 1, True)

        @block.vector
        def _(dve):
            dve.sem_inc(od_free, 2)

            def context_lo(n, i, split):
                dve.wait_ge(hi_done, split)
                nc.vector.tensor_tensor(context_place(cT[1], n), two(work[i % 2]), f32(context_place(cT[0], n)),
                                        ALU.subtract).then_inc(split_done, 1)

            def keys_lo(g, c, i, split):
                dve.wait_ge(hi_done, split)
                part = slice(c * 512, (c + 1) * 512)
                nc.vector.scalar_tensor_tensor(out=kT[1][:, part], in0=work[i % 2][:, :], scalar=bk[:, g:g + 1],
                                               in1=f32(kT[0][:, part]), op0=ALU.add,
                                               op1=ALU.subtract).then_inc(split_done, 1)

            def maximum(b, g):
                for t in range(NB):
                    dve.wait_ge(s_full, b * (G * NB) + (g * NB + t + 1))
                    if t < 2:
                        if t == 0:
                            dve.wait_ge(par_done, b * G + (g + 1))
                        nc.vector.tensor_copy(mx[:, t, :], psS[t % 4][:, :]).then_inc(mx_done, 1)
                    else:
                        dve.wait_ge(mx_done, b * (G * NB) + (g * NB + t - 1))
                        nc.vector.tensor_tensor(mx[:, t % 2, :], psS[t % 4][:, :], mx[:, t % 2, :],
                                                ALU.max).then_inc(mx_done, 1)
                dve.wait_ge(mx_done, b * (G * NB) + (g + 1) * NB)
                nc.vector.tensor_tensor(mx[:, 0, :], mx[:, 0, :], mx[:, 1, :], ALU.max).then_inc(fold_done, 1)

            def subtract(b, g, q):
                if q == 0:
                    dve.wait_ge(par_done, b * G + (g + 2))
                dve.wait_ge(s_moved, b * (G * NB) + (4 + g * NB + 2 * q + 2))
                pair = s[:, 2 * q:2 * q + 2, :]
                top = mb[:, :].rearrange("p (o n) -> p o n", o=1).broadcast_to([P, 2, HG * P])
                nc.vector.tensor_tensor(pair, pair, top, ALU.subtract).then_inc(sub_done, 1)

            def next_lo(first_unit, split_before, units):
                for i in units:
                    kind, n = NEXT[i]
                    if kind == "T":
                        context_lo(n, first_unit + i, split_before + (i + 1))
                    else:
                        keys_lo(0, n, first_unit + i, split_before + (i + 1))

            def normalise(b, g):
                dve.wait_ge(od_full, b * G + (g + 2))
                nc.vector.reciprocal(rD[:, :], psO[g % 2][:, P:2 * P]).then_inc(rd_done, 1)
                dve.wait_ge(rd_done, b * (2 * G) + (2 * g + 1))
                nc.vector.tensor_tensor(oq[:, :], psO[g % 2][:, 0:P], rD[:, :], ALU.mult).then_inc(rd_done, 1)
                dve.wait_ge(rd_done, b * (2 * G) + (2 * g + 2))
                dve.wait_ge(o_stored, b * G + (g + 1))
                nc.vector.tensor_scalar(o_st[:, g % 2, :], oq[:, :], bv[:, g:g + 1], None,
                                        ALU.add).then_inc(od_free, 1)

            dve.wait_ge(bias_in, 32)
            next_lo(0, 0, range(PRE_SPLITS))

            def batch(b, last):
                for g in range(G):
                    maximum(b, g)
                    if g >= 1:
                        normalise(b, g - 1)
                    for q in range(PAIRS):
                        if g < G - 1:
                            if q in KEYS_AT:
                                i = g * K_UNITS + KEYS_AT[q]
                                keys_lo(g + 1, KEYS_AT[q], i, split_no(b, i))
                        elif not last:
                            next_lo(U_N, b * SPLITS + (PRE_SPLITS + U_N), share(q))
                        subtract(b, g, q)
                normalise(b, G - 1)

            with dve.Fori(0, B - 1) as b:
                batch(b, False)
            batch(B - 1, True)


def transpose_units(nc, pe, bank, ident, src, blocks, u, full, lo_done):
    for k in range(src.shape[2] // P):
        for o4 in range(blocks // 4):
            if u >= len(bank):
                pe.wait_ge(lo_done, u - len(bank) + 1)
            for o in range(4):
                last = nc.tensor.transpose(bank[u % len(bank)][:, o * P:(o + 1) * P],
                                           src[:, 4 * o4 + o, k * P:(k + 1) * P], ident)
            last.then_inc(full, 1)
            u += 1
    return u


def output_projection(nc, x, w, o_d, x1, x1T):
    with ExitStack() as ctx:
        def sb(name, shape, dt=F32):
            return ctx.enter_context(nc.sbuf_tensor(name, shape, dt))

        def sem(name):
            return ctx.enter_context(nc.semaphore(name))

        ident = sb("c_ident", [P, P])
        o_sb = sb("c_o", [P, G, B, P])
        oT = [sb(f"c_oT{i}", [P, G, TOK], F32R) for i in range(2)]
        wo = sb("c_wo", [P, KD, D])
        woT = [sb(f"c_woT{i}", [P, KD, D], F32R) for i in range(2)]
        bo_row = sb("c_bo_row", [1, D])
        bo = sb("c_bo", [P, D])
        xn = sb("c_xn", [P, B, D])
        bank = [ctx.enter_context(nc.psum_tensor(f"c_ps{i}", [P, 512], F32)) for i in range(4)]
        norm = Norm(nc, ctx, "c_norm")
        const = sem("c_const")
        x_in = sem("c_x_in")
        o_in = sem("c_o_in")
        w_in = sem("c_w_in")
        b_in = sem("c_b_in")
        bo_ready = sem("c_bo_ready")
        full = sem("c_full")
        hi_done = sem("c_hi")
        lo_done = sem("c_lo")
        o_hi = sem("c_o_hi")
        o_lo = sem("c_o_lo")
        normed = sem("c_normed")
        U_O = KD
        U_X = U_O + B
        block = ctx.enter_context(nc.Block())

        @block.sync
        def _(sp):
            sp.dma_start(wo[:, :, :], w["wo"].rearrange("(o p) d -> p o d", p=P)).then_inc(w_in, 16)
            sp.dma_start(bo_row[:, :], w["bo"].rearrange("(a d) -> a d", a=1)).then_inc(b_in, 16)
            sp.dma_start(x1[:, :, :], x.rearrange("b p d -> p b d")).then_inc(x_in, 16)
            for g in range(G):
                sp.dma_start(o_sb[:, g, :, :], o_d[g].rearrange("b p t -> p b t")).then_inc(o_in, 16)

        @block.gpsimd
        def _(pool):
            make_identity(nc, pool, ident, const)
            pool.wait_ge(b_in, 16)
            nc.gpsimd.partition_broadcast(bo[:, :], bo_row[:, :], P).then_inc(bo_ready, 1)
            pool.wait_ge(bo_ready, 1)
            pool.wait_ge(x_in, 16)
            for t in range(B):
                nc.gpsimd.tensor_tensor(x1[:, t, :], x1[:, t, :], bo[:, :], ALU.add).then_inc(bo_ready, 1)

        @block.tensor
        def _(pe):
            pe.wait_ge(const, 2)
            pe.wait_ge(w_in, 16)
            u = transpose_units(nc, pe, bank, ident[:, :], wo, KD, 0, full, lo_done)
            pe.wait_ge(lo_done, U_O)
            pe.wait_ge(o_lo, G)
            for t in range(B):
                pe.wait_ge(lo_done, u - 3)
                for g in range(G):
                    last = product(nc, bank[u % 4][:, :], [a[:, g, t * P:(t + 1) * P] for a in oT],
                                   [a[:, g, :] for a in woT], g == 0, g == G - 1)
                last.then_inc(full, 1)
                u += 1
            for half in range(2):
                pe.wait_ge(normed, 4 * half + 4)
                u = transpose_units(nc, pe, bank, ident[:, :], xn[:, 4 * half:4 * half + 4, :], 4, u, full, lo_done)

        def places():
            for k in range(KD):
                yield k, [a[:, k, :] for a in woT]
            for half in range(2):
                for k in range(KD):
                    yield U_X + 4 * half + k, [a[:, k, half * 512:(half + 1) * 512] for a in x1T]

        @block.scalar
        def _(act):
            for g in range(G):
                act.wait_ge(o_in, 16 * G)
                nc.scalar.activation(oT[0][:, g, :], o_sb[:, g, :, :].rearrange("p b t -> p (b t)"),
                                     ACT.Copy).then_inc(o_hi, 1)
            for n, (u, (hi, _)) in enumerate(places()):
                if u == U_X:
                    norm.scalar(act)
                act.wait_ge(full, u + 1)
                nc.scalar.activation(hi, bank[u % 4][:, :], ACT.Copy).then_inc(hi_done, 1)

        @block.vector
        def _(dve):
            at = list(places())

            def lo(n):
                u, (hi, low) = at[n]
                dve.wait_ge(hi_done, n + 1)
                nc.vector.tensor_tensor(low, bank[u % 4][:, :], f32(hi), ALU.subtract).then_inc(lo_done, 1)

            for g in range(G):
                dve.wait_ge(o_hi, g + 1)
                nc.vector.tensor_tensor(oT[1][:, g, :], o_sb[:, g, :, :].rearrange("p b t -> p (b t)"),
                                        f32(oT[0][:, g, :]), ALU.subtract).then_inc(o_lo, 1)
            for n in range(KD):
                lo(n)
            for t in range(B):
                dve.wait_ge(bo_ready, t + 2)
                dve.wait_ge(full, U_O + t + 1)
                nc.vector.tensor_tensor(x1[:, t, :], bank[(U_O + t) % 4][:, :], x1[:, t, :],
                                        ALU.add).then_inc(lo_done, 1)
            dve.wait_ge(lo_done, U_X)
            norm.vector(dve, x1)
            dve.wait_ge(norm.step, norm.STEPS)
            for t in range(B):
                norm.apply(x1[:, t, :], xn[:, t, :], t).then_inc(normed, 1)
            for n in range(KD, KD + 2 * KD):
                lo(n)


def self_projections(nc, w, x1T, q2_d, k2_d, v2):
    with ExitStack() as ctx:
        def sb(name, shape, dt=F32):
            return ctx.enter_context(nc.sbuf_tensor(name, shape, dt))

        def sem(name):
            return ctx.enter_context(nc.semaphore(name))

        ident = sb("d_ident", [P, P])
        wn = sb("d_w", [P, 2, KB, D])
        wT = [[sb(f"d_wT{r}{i}", [P, KD, W2], F32R) for i in range(2)] for r in range(2)]
        st = sb("d_st", [P, 2, 2, 512], F32R)
        bank = [ctx.enter_context(nc.psum_tensor(f"d_ps{i}", [P, 512], F32)) for i in range(8)]
        const = sem("d_const")
        w_in = [sem(f"d_w_in{i}") for i in range(2)]
        full = sem("d_full")
        hi_done = sem("d_hi")
        done = sem("d_done")
        st_out = [sem(f"d_st_out{i}") for i in range(2)]
        TU = KD * KB // 4
        PU = KB * 2
        U_QT, U_KT, U_Q, U_VT, U_K, U_V = 0, TU, 2 * TU, 2 * TU + PU, 3 * TU + PU, 3 * TU + 2 * PU
        block = ctx.enter_context(nc.Block())
        weights = (w["Wq"], w["Wk"], w["Wv"])

        @block.sync
        def _(sp):
            def load(i):
                sp.dma_start(wn[:, i % 2, :, :], weights[i].rearrange("(o p) d -> p o d", p=P)
                             ).then_inc(w_in[i % 2], 16)

            load(0)
            load(1)
            sp.wait_ge(full, U_KT)
            load(2)
            for n in range(2 * PU):
                u = (U_Q if n < PU else U_K - PU) + n
                blk, half = (n % PU) // 2, n % 2
                dst = (q2_d, k2_d)[n // PU]
                sp.wait_ge(done, u + 1)
                for i in range(2):
                    sp.dma_start(f32(dst[4 * half:4 * half + 4, blk // 4, :, blk % 4, i, :]).rearrange("b p t -> p b t"),
                                 f32(st[:, n % 2, i, :]).rearrange("p (b t) -> p b t", b=4)
                                 ).then_inc(st_out[n % 2], 16)
            for i in range(2):
                sp.wait_ge(st_out[i], 32 * PU)

        @block.gpsimd
        def _(pool):
            make_identity(nc, pool, ident, const)

        @block.tensor
        def _(pe):
            pe.wait_ge(const, 2)

            def weight(i, u):
                pe.wait_ge(w_in[i % 2], 16 * (i // 2 + 1))
                return transpose_units(nc, pe, bank, ident[:, :], wn[:, i % 2, :, :], KB, u, full, done)

            def heads(r, u, first):
                pe.wait_ge(done, first)
                for blk in range(KB):
                    for half in range(2):
                        pe.wait_ge(done, u - len(bank) + 1)
                        for k in range(KD):
                            last = product(nc, bank[u % 8][:, :], [a[:, k, blk * P:(blk + 1) * P] for a in wT[r]],
                                           [a[:, k, half * 512:(half + 1) * 512] for a in x1T], k == 0, k == KD - 1)
                        last.then_inc(full, 1)
                        u += 1
                return u

            u = weight(0, 0)
            u = weight(1, u)
            u = heads(0, u, U_KT)
            u = weight(2, u)
            u = heads(1, u, U_Q)
            pe.wait_ge(done, U_K)
            for t in range(B):
                for half in range(2):
                    pe.wait_ge(done, u - len(bank) + 1)
                    for k in range(KD):
                        last = product(nc, bank[u % 8][:, :], [a[:, k, t * P:(t + 1) * P] for a in x1T],
                                       [a[:, k, half * 512:(half + 1) * 512] for a in wT[0]], k == 0, k == KD - 1)
                    last.then_inc(full, 1)
                    u += 1

        def places():
            u = n = 0
            for kind, r in (("w", 0), ("w", 1), ("h", 0), ("w", 0), ("h", 1)):
                for i in range(TU if kind == "w" else PU):
                    if kind == "w":
                        yield u, None, [a[:, i // 2, (i % 2) * 512:(i % 2 + 1) * 512] for a in wT[r]]
                    else:
                        yield u, n, [st[:, n % 2, j, :] for j in range(2)]
                        n += 1
                    u += 1

        @block.scalar
        def _(act):
            for u, n, (hi, _) in places():
                act.wait_ge(full, u + 1)
                if n is not None and n >= 2:
                    act.wait_ge(st_out[n % 2], 32 * (n // 2))
                nc.scalar.activation(hi, bank[u % 8][:, :], ACT.Copy).then_inc(hi_done, 1)

        @block.vector
        def _(dve):
            for u, _, (hi, lo) in places():
                dve.wait_ge(hi_done, u + 1)
                nc.vector.tensor_tensor(lo, bank[u % 8][:, :], f32(hi), ALU.subtract).then_inc(done, 1)
            for i in range(2 * B):
                u = U_V + i
                dve.wait_ge(full, u + 1)
                nc.vector.tensor_copy(v2[:, i // 2, (i % 2) * 512:(i % 2 + 1) * 512],
                                      bank[u % 8][:, :]).then_inc(done, 1)


def differential_attention(nc, w, q2_d, k2_d, v2, x1):
    with ExitStack() as ctx:
        def sb(name, shape, dt=F32):
            return ctx.enter_context(nc.sbuf_tensor(name, shape, dt))

        def sem(name):
            return ctx.enter_context(nc.semaphore(name))

        HALF = KB // 2
        ident = sb("e_ident", [P, P])
        mask = sb("e_mask", [P, P])
        wn = sb("e_w", [P, KD, W2])
        woT = [sb(f"e_woT{i}", [P, KB, D], F32R) for i in range(2)]
        lam_in_sb = sb("e_lam_in", [1, 4, HEADS * HD])
        lam_p = sb("e_lam_p", [1, 2, HEADS * HD])
        lam_s = sb("e_lam_s", [1, 2, HEADS])
        lam_e = sb("e_lam_e", [1, 2, HEADS])
        lam_d = sb("e_lam_d", [1, HEADS])
        coef_row = sb("e_coef_row", [1, HEADS, 2])
        coef = sb("e_coef", [P, HEADS, 2])
        rs = sb("e_rs", [P, 1])
        q2 = sb("e_q2", [P, 2, HALF, 2, P], F32R)
        k2 = sb("e_k2", [P, 2, HALF, 2, HG, P], F32R)
        sm = sb("e_sm", [P, 2, HG, P])
        top = sb("e_top", [P, 2, HG])
        ntop = sb("e_ntop", [P, 2, HG])
        sums = sb("e_sums", [P, 2, HG])
        rsum = sb("e_rsum", [P, 2, HG])
        cf = sb("e_cf", [P, 2, HG])
        at = sb("e_at", [P, 2, 2, P])
        aT = sb("e_aT", [P, 2, 2, P])
        o_sb = sb("e_o", [P, W2])
        sq = sb("e_sq", [P, W2])
        ms = sb("e_ms", [P, HEADS])
        expo = sb("e_expo", [P, HEADS])
        root = sb("e_root", [P, HEADS])
        nt = sb("e_nt", [P, HEADS])
        on = sb("e_on", [P, W2])
        oT = [sb(f"e_oT{i}", [P, KB, P], F32R) for i in range(2)]
        psS = [ctx.enter_context(nc.psum_tensor(f"e_psS{i}", [P, 512], F32)) for i in range(2)]
        psA = [ctx.enter_context(nc.psum_tensor(f"e_psA{i}", [P, 512], F32)) for i in range(2)]
        psO = [ctx.enter_context(nc.psum_tensor(f"e_psO{i}", [P, 512], F32)) for i in range(2)]
        psW = [ctx.enter_context(nc.psum_tensor(f"e_psW{i}", [P, 512], F32)) for i in range(2)]

        const = sem("e_const")
        w_in = sem("e_w_in")
        lam_in = sem("e_lam_in_s")
        lam_step = sem("e_lam_step")
        lam_exp = sem("e_lam_exp")
        coef_ready = sem("e_coef_ready")
        qk_in = [sem(f"e_qk_in{i}") for i in range(2)]
        w_full = sem("e_w_full")
        w_hi = sem("e_w_hi")
        w_lo = sem("e_w_lo")
        s_full = sem("e_s_full")
        sm_step = sem("e_sm_step")
        exp_done = sem("e_exp_done")
        a_step = sem("e_a_step")
        a_full = sem("e_a_full")
        aT_done = sem("e_aT_done")
        pv_done = sem("e_pv_done")
        o_copied = sem("e_o_copied")
        o_step = sem("e_o_step")
        root_done = sem("e_root_done")
        y_full = sem("e_y_full")
        x_done = sem("e_x_done")
        W_UNITS = KB
        O_STEPS = 7
        block = ctx.enter_context(nc.Block())

        @block.sync
        def _(sp):
            sp.dma_start(wn[:, :, :], w["Wo"].rearrange("(o p) d -> p o d", p=P)).then_inc(w_in, 16)
            for i, name in enumerate(("lq1", "lq2", "lk1", "lk2")):
                sp.dma_start(lam_in_sb[:, i, :], w[name].rearrange("(a h) d -> a (h d)", a=1)).then_inc(lam_in, 16)
            with nc.allow_non_contiguous_dma(reason="64 numbers"):
                for i in range(2):
                    sp.dma_start(rs[64 * i:64 * i + 64, :], w["rms_scale"].rearrange("(d a) -> d a", a=1)
                                 ).then_inc(lam_in, 16)
            sp.wait_ge(const, 6)

            with sp.Fori(0, B) as b:
                for hf in range(2):
                    sp.wait_ge(s_full, b * KB + (HALF + hf * HALF))
                    sp.dma_start(f32(q2[:, hf, :, :, :]), f32(q2_d[b, hf, :, :, :, :])).then_inc(qk_in[hf], 16)
                    for j in range(HG):
                        sp.dma_start(f32(k2[j * HD:(j + 1) * HD, hf, :, :, j, :]),
                                     f32(k2_d[b, hf, j * HD:(j + 1) * HD, :, :, :])).then_inc(qk_in[hf], 16)

        @block.gpsimd
        def _(pool):
            make_identity(nc, pool, ident, const)
            nc.gpsimd.memset(mask[:, :], 0.0).then_inc(const, 1)
            pool.wait_ge(const, 3)
            nc.gpsimd.affine_select(out=mask[:, :], in_=mask[:, :], compare_op=ALU.is_ge, fill=MASKED,
                                    base=0, pattern=[[-1, P]], channel_multiplier=1).then_inc(const, 1)
            nc.gpsimd.memset(f32(k2[:, :, :, :, :, :]), 0.0).then_inc(const, 1)
            nc.gpsimd.memset(expo[:, :], -0.5).then_inc(const, 1)
            pool.wait_ge(lam_step, 5)
            nc.gpsimd.partition_broadcast(coef[:, :, :].rearrange("p h s -> p (h s)"),
                                          coef_row[:, :, :].rearrange("p h s -> p (h s)"), P).then_inc(coef_ready, 1)
            pool.wait_ge(const, 6)
            with pool.Fori(0, B) as b:
                pool.wait_ge(o_step, b * O_STEPS + 3)
                nc.gpsimd.tensor_tensor(root[:, :], ms[:, :], expo[:, :], ALU.pow).then_inc(root_done, 1)

        @block.tensor
        def _(pe):
            pe.wait_ge(const, 2)
            pe.wait_ge(w_in, 16)
            for k in range(KB):
                if k >= 2:
                    pe.wait_ge(w_lo, k - 1)
                for o in range(KD):
                    last = nc.tensor.transpose(psW[k % 2][:, o * P:(o + 1) * P], wn[:, o, k * P:(k + 1) * P],
                                               ident[:, :])
                last.then_inc(w_full, 1)

            with pe.Fori(0, B) as b:
                for n in range(KB + 2):
                    if n < KB:
                        if n % HALF == 0:
                            hf = n // HALF
                            pe.wait_ge(qk_in[hf], b * (16 * 5) + 16 * 5)
                        pe.wait_ge(sm_step, b * (3 * KB) + 3 * n + 1)
                        product(nc, psS[n % 2][:, :], [q2[:, n // HALF, n % HALF, i, :] for i in range(2)],
                                [k2[:, n // HALF, n % HALF, i, :, :] for i in range(2)],
                                True, True).then_inc(s_full, 1)
                    if 1 <= n <= KB:
                        m = n - 1
                        pe.wait_ge(a_step, b * (6 * KB) + 6 * (m + 1))
                        pe.wait_ge(aT_done, b * KB + (m + 1))
                        for i in range(2):
                            last = nc.tensor.transpose(psA[m % 2][:, i * P:(i + 1) * P], at[:, m % 2, i, :],
                                                       ident[:, :])
                        last.then_inc(a_full, 1)
                    if n >= 2:
                        m = n - 2
                        pe.wait_ge(aT_done, b * KB + (m + 1 + 2))
                        if m == 0:
                            pe.wait_ge(o_copied, b + 1)
                        for i in range(2):
                            c = (m % HALF) * P + i * 2 * HD
                            last = nc.tensor.matmul(psO[m // HALF][:, c:c + 2 * HD], aT[:, m % 2, i, :],
                                                    v2[:, b, m * P + i * 2 * HD:m * P + (i + 1) * 2 * HD],
                                                    start=True, stop=True)
                        last.then_inc(pv_done, 1)
                pe.wait_ge(o_step, b * O_STEPS + O_STEPS)
                for i in range(2):
                    if i == 0:
                        pe.wait_ge(x_done, b + 1)
                    for j in range(4):
                        last = nc.tensor.transpose(psW[i][:, j * P:(j + 1) * P],
                                                   on[:, (4 * i + j) * P:(4 * i + j + 1) * P], ident[:, :])
                    last.then_inc(w_full, 1)
                pe.wait_ge(w_lo, b * 2 + (W_UNITS + 2))
                for k in range(KB):
                    last = product(nc, psW[0][:, :], [a[:, k, :] for a in oT], [a[:, k, :] for a in woT],
                                   k == 0, k == KB - 1)
                last.then_inc(y_full, 1)

        @block.scalar
        def _(act):
            act.sem_inc(aT_done, 2)
            act.wait_ge(lam_step, 2)
            nc.scalar.activation(lam_e[:, :, :], lam_s[:, :, :], ACT.Exp).then_inc(lam_exp, 1)
            for k in range(KB):
                act.wait_ge(w_full, k + 1)
                nc.scalar.activation(woT[0][:, k, :], psW[k % 2][:, :], ACT.Copy).then_inc(w_hi, 1)
            act.wait_ge(lam_step, 6)
            with act.Fori(0, B) as b:
                for n in range(KB + 1):
                    if n < KB:
                        act.wait_ge(sm_step, b * (3 * KB) + (2 + 3 * n + 3))
                        for j in range(HG):
                            last = nc.scalar.activation(sm[:, n % 2, j, :], sm[:, n % 2, j, :], ACT.Exp,
                                                        bias=ntop[:, n % 2, j:j + 1], scale=SCALE,
                                                        accum_out=sums[:, n % 2, j:j + 1])
                        last.then_inc(exp_done, 1)
                    if n >= 1:
                        m = n - 1
                        act.wait_ge(a_full, b * KB + (m + 1))
                        act.wait_ge(pv_done, b * KB + (m + 1))
                        nc.scalar.activation(aT[:, m % 2, :, :].rearrange("p i t -> p (i t)"), psA[m % 2][:, 0:2 * P],
                                             ACT.Copy).then_inc(aT_done, 1)
                act.wait_ge(pv_done, b * KB + (KB + 2))
                act.wait_ge(x_done, b + 1)
                for i in range(2):
                    last = nc.scalar.activation(o_sb[:, i * 512:(i + 1) * 512], psO[i][:, :], ACT.Copy)
                last.then_inc(o_copied, 1)
                for i in range(2):
                    act.wait_ge(w_full, b * 2 + (W_UNITS + i + 1))
                    nc.scalar.activation(oT[0][:, 4 * i:4 * i + 4, :].rearrange("p k t -> p (k t)"), psW[i][:, :],
                                         ACT.Copy, scale=rs[:, 0:1]).then_inc(w_hi, 1)

        @block.vector
        def _(dve):
            dve.sem_inc(sm_step, 2)
            dve.sem_inc(pv_done, 2)
            dve.sem_inc(s_full, HALF)
            dve.sem_inc(o_copied, 1)
            dve.sem_inc(x_done, 1)
            dve.wait_ge(lam_in, 16 * 6)
            nc.vector.tensor_tensor(lam_p[:, :, :], lam_in_sb[:, 0:2, :], lam_in_sb[:, 2:4, :],
                                    ALU.mult).then_inc(lam_step, 1)
            dve.wait_ge(lam_step, 1)
            nc.vector.tensor_reduce(lam_s[:, :, :], lam_p[:, :, :].rearrange("p i (h d) -> p i h d", d=HD),
                                    AX.X, ALU.add).then_inc(lam_step, 1)
            dve.wait_ge(lam_exp, 1)
            nc.vector.tensor_tensor(lam_d[:, :], lam_e[:, 1, :], lam_e[:, 0, :], ALU.subtract).then_inc(lam_step, 1)
            nc.vector.memset(coef_row[:, :, 0:1], 1.0).then_inc(lam_step, 1)
            dve.wait_ge(lam_step, 3)
            nc.vector.tensor_scalar(coef_row[:, :, 1], lam_d[:, :], -LAMBDA_INIT, None, ALU.add).then_inc(lam_step, 1)
            nc.vector.tensor_scalar(rs[:, :], rs[:, :], 1.0 - LAMBDA_INIT, None, ALU.mult).then_inc(lam_step, 1)
            for k in range(KB):
                dve.wait_ge(w_hi, k + 1)
                nc.vector.tensor_tensor(woT[1][:, k, :], psW[k % 2][:, :], f32(woT[0][:, k, :]),
                                        ALU.subtract).then_inc(w_lo, 1)
            dve.wait_ge(const, 4)
            dve.wait_ge(coef_ready, 1)
            dve.wait_ge(lam_step, 6)

            with dve.Fori(0, B) as b:
                for n in range(KB + 1):
                    if n < KB:
                        r = n % 2
                        s0 = b * (3 * KB)
                        dve.wait_ge(s_full, b * KB + (HALF + n + 1))
                        nc.vector.tensor_tensor(
                            sm[:, r, :, :], psS[r][:, :].rearrange("p (j k) -> p j k", j=HG),
                            mask[:, :].rearrange("p (o n) -> p o n", o=1).broadcast_to([P, HG, P]),
                            ALU.add).then_inc(sm_step, 1)
                        dve.wait_ge(sm_step, s0 + (2 + 3 * n + 1))
                        nc.vector.tensor_reduce(top[:, r, :], sm[:, r, :, :], AX.X, ALU.max).then_inc(sm_step, 1)
                        dve.wait_ge(sm_step, s0 + (2 + 3 * n + 2))
                        nc.vector.tensor_scalar(ntop[:, r, :], top[:, r, :], -SCALE, None,
                                                ALU.mult).then_inc(sm_step, 1)
                    if n >= 1:
                        m = n - 1
                        r = m % 2
                        a0 = b * (6 * KB)
                        dve.wait_ge(exp_done, b * KB + (m + 1))
                        nc.vector.reciprocal(rsum[:, r, :], sums[:, r, :]).then_inc(a_step, 1)
                        dve.wait_ge(a_step, a0 + (6 * m + 1))
                        nc.vector.tensor_tensor(cf[:, r, :], rsum[:, r, :],
                                                coef[:, 2 * m:2 * m + 2, :].rearrange("p h s -> p (h s)"),
                                                ALU.mult).then_inc(a_step, 1)
                        dve.wait_ge(a_step, a0 + (6 * m + 2))
                        for i in range(2):
                            nc.vector.tensor_scalar(at[:, r, i, :], sm[:, r, 2 * i, :], cf[:, r, 2 * i:2 * i + 1],
                                                    None, ALU.mult).then_inc(a_step, 1)
                        for i in range(2):
                            dve.wait_ge(a_step, a0 + (6 * m + 3 + i))
                            nc.vector.scalar_tensor_tensor(out=at[:, r, i, :], in0=sm[:, r, 2 * i + 1, :],
                                                           scalar=cf[:, r, 2 * i + 1:2 * i + 2], in1=at[:, r, i, :],
                                                           op0=ALU.mult, op1=ALU.add).then_inc(a_step, 1)
                o0 = b * O_STEPS
                dve.wait_ge(o_copied, b + 2)
                nc.vector.tensor_tensor(sq[:, :], o_sb[:, :], o_sb[:, :], ALU.mult).then_inc(o_step, 1)
                dve.wait_ge(o_step, o0 + 1)
                nc.vector.tensor_reduce(ms[:, :], sq[:, :].rearrange("p (h d) -> p h d", h=HEADS), AX.X,
                                        ALU.add).then_inc(o_step, 1)
                dve.wait_ge(o_step, o0 + 2)
                nc.vector.tensor_scalar(ms[:, :], ms[:, :], 1.0 / (2 * HD), EPS, ALU.mult, ALU.add).then_inc(o_step, 1)
                dve.wait_ge(root_done, b + 1)
                nc.vector.tensor_tensor(nt[:, :], root[:, :], root[:, :], ALU.mult).then_inc(o_step, 1)
                dve.wait_ge(o_step, o0 + 4)
                nc.vector.scalar_tensor_tensor(out=nt[:, :], in0=nt[:, :], scalar=-0.5, in1=ms[:, :],
                                               op0=ALU.mult, op1=ALU.mult).then_inc(o_step, 1)
                dve.wait_ge(o_step, o0 + 5)
                nc.vector.scalar_tensor_tensor(out=nt[:, :], in0=nt[:, :], scalar=1.5, in1=root[:, :],
                                               op0=ALU.add, op1=ALU.mult).then_inc(o_step, 1)
                dve.wait_ge(o_step, o0 + 6)
                nc.vector.tensor_tensor(
                    on[:, :].rearrange("p (h d) -> p h d", h=HEADS), o_sb[:, :].rearrange("p (h d) -> p h d", h=HEADS),
                    nt[:, :].rearrange("p (h o) -> p h o", o=1).broadcast_to([P, HEADS, 2 * HD]),
                    ALU.mult).then_inc(o_step, 1)
                for i in range(2):
                    dve.wait_ge(w_hi, b * 2 + (W_UNITS + i + 1))
                    nc.vector.scalar_tensor_tensor(
                        out=oT[1][:, 4 * i:4 * i + 4, :].rearrange("p k t -> p (k t)"), in0=psW[i][:, :],
                        scalar=rs[:, 0:1], in1=f32(oT[0][:, 4 * i:4 * i + 4, :]).rearrange("p k t -> p (k t)"),
                        op0=ALU.mult, op1=ALU.subtract).then_inc(w_lo, 1)
                dve.wait_ge(y_full, b + 1)
                nc.vector.tensor_tensor(x1[:, b, :], psW[0][:, :], x1[:, b, :], ALU.add).then_inc(x_done, 1)


def experts(nc, w, x2, out):
    with ExitStack() as ctx:
        def sb(name, shape, dt=F32):
            return ctx.enter_context(nc.sbuf_tensor(name, shape, dt))

        def sem(name):
            return ctx.enter_context(nc.semaphore(name))

        ident = sb("f_ident", [P, P])
        xn = sb("f_xn", [P, B, D])
        xT = [sb(f"f_xT{i}", [P, KD, TOK], F32R) for i in range(2)]
        gw = sb("f_gw", [P, KD, NE])
        gws = [sb(f"f_gws{i}", [P, KD, NE], F32R) for i in range(2)]
        gb_row = sb("f_gb_row", [1, NE])
        gb = sb("f_gb", [P, NE])
        z = sb("f_z", [P, B, NE])
        sel = sb("f_sel", [P, B, NE])
        r1 = sb("f_r1", [P, B])
        r2 = sb("f_r2", [P, B])
        gate = sb("f_gate", [P, NE, B])
        gateT = sb("f_gateT", [NE, TOK])
        eb = sb("f_eb", [NE, D])
        wn = sb("f_w", [P, 2, KD, D])
        ws = [sb(f"f_ws{i}", [P, 2, KD, D], F32R) for i in range(2)]
        bank = [ctx.enter_context(nc.psum_tensor(f"f_ps{i}", [P, 512], F32)) for i in range(6)]
        psG = ctx.enter_context(nc.psum_tensor("f_psG", [P, 512], F32))
        norm = Norm(nc, ctx, "f_norm")
        const = sem("f_const")
        s_in = sem("f_small_in")
        w_in = [sem(f"f_w_in{i}") for i in range(2)]
        gb_ready = sem("f_gb_ready")
        normed = sem("f_normed")
        x_full = sem("f_x_full")
        x_hi = sem("f_x_hi")
        x_lo = sem("f_x_lo")
        gw_hi = sem("f_gw_hi")
        gw_lo = sem("f_gw_lo")
        z_full = sem("f_z_full")
        z_step = sem("f_z_step")
        z_exp = sem("f_z_exp")
        t_full = sem("f_t_full")
        t_done = sem("f_t_done")
        y_full = sem("f_y_full")
        y_done = sem("f_y_done")
        w_hi = sem("f_w_hi")
        w_lo = sem("f_w_lo")
        out_sem = sem("f_out")
        Z_STEPS = 12
        NBANK = len(bank)
        assert B * NE % 2 == 0
        block = ctx.enter_context(nc.Block())

        @block.sync
        def _(sp):
            with nc.allow_non_contiguous_dma(reason="the gate's weights, 16 KB"):
                sp.dma_start(gw[:, :, :], w["gate_w"].rearrange("(k p) e -> p k e", p=P)).then_inc(s_in, 16)
            sp.dma_start(gb_row[:, :], w["gate_b"].rearrange("(a e) -> a e", a=1)).then_inc(s_in, 16)
            sp.dma_start(eb[:, :], w["expert_b"]).then_inc(s_in, 16)
            with sp.Fori(0, NE // 2) as i:
                for r in range(2):
                    sp.wait_ge(w_lo, i * 2 + r + 1)
                    sp.dma_start(wn[:, r, :, :], w["expert_w"][i * 2 + r].rearrange("(k p) d -> p k d", p=P)
                                 ).then_inc(w_in[r], 16)
            for t in range(B):
                sp.wait_ge(y_done, NE * B + t + 1)
                sp.dma_start(out[t], x2[:, t, :]).then_inc(out_sem, 16)
            sp.wait_ge(out_sem, 16 * B)

        @block.gpsimd
        def _(pool):
            pool.sem_inc(w_lo, 2)
            make_identity(nc, pool, ident, const)
            pool.wait_ge(s_in, 48)
            nc.gpsimd.partition_broadcast(gb[:, :], gb_row[:, :], P).then_inc(gb_ready, 1)
            with pool.Fori(0, NE // 2) as i:
                for r in range(2):
                    pool.wait_ge(w_hi, i * 2 + (r + 1))
                    nc.gpsimd.tensor_tensor(ws[1][:, r, :, :], wn[:, r, :, :], f32(ws[0][:, r, :, :]),
                                            ALU.subtract).then_inc(w_lo, 1)

        @block.tensor
        def _(pe):
            pe.wait_ge(const, 2)
            u = 0
            for half in range(2):
                pe.wait_ge(normed, 4 * half + 4)
                u = transpose_units(nc, pe, bank, ident[:, :], xn[:, 4 * half:4 * half + 4, :], 4, u, x_full, x_lo)
            pe.wait_ge(x_lo, 8)
            pe.wait_ge(gw_lo, 1)
            for t in range(B):
                for k in range(KD):
                    last = product(nc, psG[:, t * NE:(t + 1) * NE], [a[:, k, t * P:(t + 1) * P] for a in xT],
                                   [a[:, k, :] for a in gws], k == 0, k == KD - 1)
            last.then_inc(z_full, 1)
            pe.wait_ge(z_step, Z_STEPS)
            for half in range(2):
                for t in range(4):
                    last = nc.tensor.transpose(bank[half][0:NE, t * P:(t + 1) * P], gate[:, :, 4 * half + t],
                                               ident[:, :])
                last.then_inc(t_full, 1)
            pe.wait_ge(t_done, 2)
            for t in range(B):
                n = t
                if n >= NBANK:
                    pe.wait_ge(y_done, n - NBANK + 1)
                nc.tensor.matmul(bank[n % NBANK][:, :], gateT[:, t * P:(t + 1) * P], eb[:, :],
                                 start=True, stop=True).then_inc(y_full, 1)
            pe.wait_ge(y_done, B)
            with pe.Fori(0, NE // 2) as i:
                for r in range(2):
                    pe.wait_ge(w_lo, i * 2 + (r + 1 + 2))
                    for t in range(B):
                        n = r * B + t
                        pe.wait_ge(y_done, i * (2 * B) + (B + n - 4 + 1))
                        for k in range(KD):
                            last = product(nc, bank[n % 4][:, :], [a[:, k, t * P:(t + 1) * P] for a in xT],
                                           [a[:, r, k, :] for a in ws], k == 0, k == KD - 1)
                        last.then_inc(y_full, 1)

        @block.scalar
        def _(act):
            act.wait_ge(s_in, 48)
            nc.scalar.activation(gws[0][:, :, :], gw[:, :, :], ACT.Copy).then_inc(gw_hi, 1)
            norm.scalar(act)
            for u in range(8):
                act.wait_ge(x_full, u + 1)
                half, k = u // 4, u % 4
                nc.scalar.activation(xT[0][:, k, half * 512:(half + 1) * 512], bank[u % NBANK][:, :],
                                     ACT.Copy).then_inc(x_hi, 1)
            act.wait_ge(z_step, 3)
            nc.scalar.activation(z[:, :, :], z[:, :, :], ACT.Exp).then_inc(z_exp, 1)
            for half in range(2):
                act.wait_ge(t_full, half + 1)
                nc.scalar.activation(gateT[:, half * 512:(half + 1) * 512], bank[half][0:NE, :],
                                     ACT.Copy).then_inc(t_done, 1)
            with act.Fori(0, NE // 2) as i:
                for r in range(2):
                    act.wait_ge(w_in[r], i * 16 + 16)
                    act.wait_ge(y_full, i * (2 * B) + (r + 1) * B)
                    nc.scalar.activation(ws[0][:, r, :, :].rearrange("p k d -> p (k d)"),
                                         wn[:, r, :, :].rearrange("p k d -> p (k d)"), ACT.Copy).then_inc(w_hi, 1)

        @block.vector
        def _(dve):
            dve.sem_inc(y_full, B)
            dve.wait_ge(gw_hi, 1)
            nc.vector.tensor_tensor(gws[1][:, :, :], gw[:, :, :], f32(gws[0][:, :, :]),
                                    ALU.subtract).then_inc(gw_lo, 1)
            norm.vector(dve, x2)
            dve.wait_ge(norm.step, norm.STEPS)
            for t in range(B):
                norm.apply(x2[:, t, :], xn[:, t, :], t).then_inc(normed, 1)
            for u in range(8):
                dve.wait_ge(x_hi, u + 1)
                half, k = u // 4, u % 4
                part = slice(half * 512, (half + 1) * 512)
                nc.vector.tensor_tensor(xT[1][:, k, part], bank[u % NBANK][:, :], f32(xT[0][:, k, part]),
                                        ALU.subtract).then_inc(x_lo, 1)

            def over_experts(row):
                return row[:, :].rearrange("p (t o) -> p t o", o=1).broadcast_to([P, B, NE])

            dve.wait_ge(z_full, 1)
            dve.wait_ge(gb_ready, 1)
            nc.vector.tensor_tensor(z[:, :, :], psG[:, 0:B * NE].rearrange("p (t e) -> p t e", t=B),
                                    gb[:, :].rearrange("p (o e) -> p o e", o=1).broadcast_to([P, B, NE]),
                                    ALU.add).then_inc(z_step, 1)
            dve.wait_ge(z_step, 1)
            nc.vector.tensor_reduce(r1[:, :], z[:, :, :], AX.X, ALU.max).then_inc(z_step, 1)
            dve.wait_ge(z_step, 2)
            nc.vector.tensor_tensor(z[:, :, :], z[:, :, :], over_experts(r1), ALU.subtract).then_inc(z_step, 1)
            dve.wait_ge(z_exp, 1)
            nc.vector.tensor_reduce(r1[:, :], z[:, :, :], AX.X, ALU.add).then_inc(z_step, 1)
            dve.wait_ge(z_step, 4)
            nc.vector.reciprocal(r2[:, :], r1[:, :]).then_inc(z_step, 1)
            dve.wait_ge(z_step, 5)
            nc.vector.tensor_tensor(z[:, :, :], z[:, :, :], over_experts(r2), ALU.mult).then_inc(z_step, 1)
            dve.wait_ge(z_step, 6)
            nc.vector.scalar_tensor_tensor(out=sel[:, :, :], in0=z[:, :, :], scalar=THRESHOLD, in1=z[:, :, :],
                                           op0=ALU.is_ge, op1=ALU.mult).then_inc(z_step, 1)
            dve.wait_ge(z_step, 7)
            nc.vector.tensor_reduce(r1[:, :], sel[:, :, :], AX.X, ALU.add).then_inc(z_step, 1)
            dve.wait_ge(z_step, 8)
            nc.vector.tensor_scalar(r2[:, :], r1[:, :], 0.0, None, ALU.is_equal).then_inc(z_step, 1)
            dve.wait_ge(z_step, 9)
            nc.vector.tensor_tensor(r2[:, :], r2[:, :], r1[:, :], ALU.add).then_inc(z_step, 1)
            dve.wait_ge(z_step, 10)
            nc.vector.reciprocal(r1[:, :], r2[:, :]).then_inc(z_step, 1)
            dve.wait_ge(z_step, 11)
            nc.vector.tensor_tensor(gate[:, :, :].rearrange("p e t -> p t e"), sel[:, :, :], over_experts(r1),
                                    ALU.mult).then_inc(z_step, 1)
            for t in range(B):
                dve.wait_ge(y_full, B + t + 1)
                nc.vector.tensor_tensor(x2[:, t, :], bank[t % NBANK][:, :], x2[:, t, :], ALU.add).then_inc(y_done, 1)
            with dve.Fori(0, NE // 2) as i:
                for r in range(2):
                    for t in range(B):
                        n = r * B + t
                        dve.wait_ge(y_full, i * (2 * B) + (2 * B + n + 1))
                        dve.wait_ge(y_done, i * (2 * B) + (n + 1))
                        nc.vector.scalar_tensor_tensor(out=x2[:, t, :], in0=bank[n % 4][:, :],
                                                       scalar=gate[:, i * 2 + r, t:t + 1], in1=x2[:, t, :],
                                                       op0=ALU.mult, op1=ALU.add).then_inc(y_done, 1)


def perceiver_layer(nc, x, ctx_in, wx, wa, wf, out):
    q_d = nc.dram_tensor("q_scratch", [G, B, P, 2, P], F32R).ap()
    o_d = nc.dram_tensor("o_scratch", [G, B, P, P], F32).ap()
    q2_d = nc.dram_tensor("q2_scratch", [B, 2, P, KB // 2, 2, P], F32R).ap()
    k2_d = nc.dram_tensor("k2_scratch", [B, 2, P, KB // 2, 2, P], F32R).ap()
    with ExitStack() as ctx:
        wkT = [ctx.enter_context(nc.sbuf_tensor(f"wkT{i}", [P, KD, D], F32R)) for i in range(2)]
        wvT = [ctx.enter_context(nc.sbuf_tensor(f"wvT{i}", [P, KD, D], F32R)) for i in range(2)]
        queries_and_weights(nc, x, wx, q_d, wkT, wvT)
        cross_attention(nc, ctx_in, wx, q_d, o_d, wkT, wvT)
    with ExitStack() as ctx:
        x1 = ctx.enter_context(nc.sbuf_tensor("x1", [P, B, D], F32))
        v2 = ctx.enter_context(nc.sbuf_tensor("v2", [P, B, W2], F32))
        with ExitStack() as inner:
            x1T = [inner.enter_context(nc.sbuf_tensor(f"x1T{i}", [P, KD, TOK], F32R)) for i in range(2)]
            output_projection(nc, x, wx, o_d, x1, x1T)
            self_projections(nc, wa, x1T, q2_d, k2_d, v2)
        differential_attention(nc, wa, q2_d, k2_d, v2, x1)
        experts(nc, wf, x1, out)


_XATTN = ("wq", "bq", "wk", "bk", "wv", "bv", "wo", "bo")
_ATTN = ("Wq", "Wk", "Wv", "Wo", "lq1", "lk1", "lq2", "lk2", "rms_scale")
_FFN = ("gate_w", "gate_b", "expert_w", "expert_b")
_INS = (["x", "ctx_1024"] + [f"L0_xattn_{n}" for n in _XATTN] + [f"L0_attn_{n}" for n in _ATTN]
        + [f"L0_ffn_{n}" for n in _FFN])


def kernel(**inputs):
    import concourse.bacc as _bacc
    from concourse.bass_utils import run_bass_kernel_spmd as _run

    nc = _bacc.Bacc("TRN2", target_bir_lowering=False, num_devices=1)
    arrays, aps = {}, {}
    for name in _INS:
        a = np.ascontiguousarray(inputs[name])
        arrays[f"in_{name}"] = a
        aps[name] = nc.dram_tensor(f"in_{name}", a.shape, mybir.dt.from_np(a.dtype), kind="ExternalInput").ap()
    out = nc.dram_tensor("out_0", [B, P, D], F32, kind="ExternalOutput").ap()
    perceiver_layer(nc, aps["x"], aps["ctx_1024"], {n: aps[f"L0_xattn_{n}"] for n in _XATTN},
                    {n: aps[f"L0_attn_{n}"] for n in _ATTN}, {n: aps[f"L0_ffn_{n}"] for n in _FFN}, out)
    r = _run(nc, [arrays], core_ids=[0])
    return r.results[0]["out_0"]
```

```python
from contextlib import ExitStack

import numpy as np

import concourse.bass as bass
from concourse import mybir

F32 = mybir.dt.float32
F32R = mybir.dt.float32r
BF16 = mybir.dt.bfloat16
ALU = mybir.AluOpType
ACT = mybir.ActivationFunctionType
AX = mybir.AxisListType
RMAX = bass.bass_isa.ReduceOp.max

P = 128
B = 8
D = 512
KD = D // P
KV = 2048
NB = KV // P
HD = 32
G = D // P
HG = P // HD
TOK = B * P
EPS = 1e-5
SCALE = float(1.0 / np.sqrt(np.float32(HD)))
HEADS = 16
W2 = 2 * HD * HEADS
KB = W2 // P
LAMBDA_INIT = 0.8
NE = 8
THRESHOLD = 0.1
MASKED = -3.0e38



def product(nc, out, lhs, rhs, first, last):
    nc.tensor.matmul(out, lhs[0], rhs[0], start=first, stop=False)
    nc.tensor.matmul(out, lhs[0], rhs[1], start=False, stop=False)
    return nc.tensor.matmul(out, lhs[1], rhs[0], start=False, stop=last)


def f32(ap):
    return ap.bitcast(F32)


def reached(engine, sem, count):
    if not isinstance(count, int) or count > 0:
        engine.wait_ge(sem, count)


def make_identity(nc, pool, ident, step):
    nc.gpsimd.memset(ident[:, :], 0.0).then_inc(step, 1)
    pool.wait_ge(step, 1)
    nc.gpsimd.affine_select(out=ident[:, :], in_=ident[:, :], compare_op=ALU.not_equal, fill=1.0,
                            base=0, pattern=[[-1, P]], channel_multiplier=1).then_inc(step, 1)


class Norm:

    def __init__(self, nc, ctx, name):
        self.nc = nc
        self.stats = ctx.enter_context(nc.sbuf_tensor(f"{name}_stats", [P, B, 6], F32))
        self.mv = ctx.enter_context(nc.sbuf_tensor(f"{name}_mv", [P, B, 2], F32))
        self.veps = ctx.enter_context(nc.sbuf_tensor(f"{name}_veps", [P, B], F32))
        self.root = ctx.enter_context(nc.sbuf_tensor(f"{name}_root", [P, B], F32))
        self.rstd = ctx.enter_context(nc.sbuf_tensor(f"{name}_rstd", [P, B], F32))
        self.tmp = ctx.enter_context(nc.sbuf_tensor(f"{name}_tmp", [P, B], F32))
        self.step = ctx.enter_context(nc.semaphore(f"{name}_step"))
        self.root_ready = ctx.enter_context(nc.semaphore(f"{name}_root_ready"))

    STEPS_TO_VEPS = B + B + 1
    STEPS = STEPS_TO_VEPS + 5

    def tile_stats(self, x, t):
        self.nc.vector.bn_stats(self.stats[:, t, :], x[:, t, :]).then_inc(self.step, 1)

    def vector(self, dve):
        nc = self.nc
        for t in range(B):
            dve.wait_ge(self.step, t + 1)
            nc.vector.bn_aggr(self.mv[:, t, :], self.stats[:, t, :]).then_inc(self.step, 1)
        dve.wait_ge(self.step, 2 * B)
        nc.vector.tensor_scalar(self.veps[:, :], self.mv[:, :, 1], EPS, None, ALU.add).then_inc(self.step, 1)
        inv_root(nc, dve, self, self.STEPS_TO_VEPS)

    def scalar(self, act):
        act.wait_ge(self.step, self.STEPS_TO_VEPS)
        self.nc.scalar.activation(self.root[:, :], self.veps[:, :], ACT.Sqrt).then_inc(self.root_ready, 1)

    def apply(self, x, out, t):
        return self.nc.vector.tensor_scalar(out, x, self.mv[:, t, 0:1], self.rstd[:, t:t + 1],
                                            ALU.subtract, ALU.mult)


def inv_root(nc, dve, n, steps):
    dve.wait_ge(n.root_ready, 1)
    nc.vector.reciprocal(n.rstd[:, :], n.root[:, :]).then_inc(n.step, 1)
    dve.wait_ge(n.step, steps + 1)
    nc.vector.tensor_tensor(n.tmp[:, :], n.rstd[:, :], n.rstd[:, :], ALU.mult).then_inc(n.step, 1)
    dve.wait_ge(n.step, steps + 2)
    nc.vector.tensor_tensor(n.tmp[:, :], n.tmp[:, :], n.veps[:, :], ALU.mult).then_inc(n.step, 1)
    dve.wait_ge(n.step, steps + 3)
    nc.vector.tensor_scalar(n.tmp[:, :], n.tmp[:, :], -0.5, 1.5, ALU.mult, ALU.add).then_inc(n.step, 1)
    dve.wait_ge(n.step, steps + 4)
    nc.vector.tensor_tensor(n.rstd[:, :], n.rstd[:, :], n.tmp[:, :], ALU.mult).then_inc(n.step, 1)


def queries_and_weights(nc, x, w, q_d, wkT, wvT):
    with ExitStack() as ctx:
        def sb(name, shape, dt=F32):
            return ctx.enter_context(nc.sbuf_tensor(name, shape, dt))

        def sem(name):
            return ctx.enter_context(nc.semaphore(name))

        ident = sb("a_ident", [P, P])
        x_sb = sb("a_x", [P, B, D])
        xn = sb("a_xn", [P, B, D])
        w_sb = sb("a_w", [P, 3, KD, D])
        bq = sb("a_bq", [P, KD])
        wqT = [sb(f"a_wqT{i}", [P, KD, D], F32R) for i in range(2)]
        xT = [sb(f"a_xT{i}", [P, KD, TOK], F32R) for i in range(2)]
        q_st = sb("a_q", [P, 2, 2, TOK], F32R)
        bank = [ctx.enter_context(nc.psum_tensor(f"a_ps{i}", [P, 512], F32)) for i in range(4)]
        norm = Norm(nc, ctx, "a_norm")
        const = sem("a_const")
        x_in = sem("a_x_in")
        b_in = sem("a_b_in")
        w_in = [sem(f"a_w_in{i}") for i in range(3)]
        full = sem("a_full")
        hi_done = sem("a_hi")
        lo_done = sem("a_lo")
        normed = sem("a_normed")
        q_out = [sem(f"a_q_out{i}") for i in range(2)]
        weights = ((w["wk"], wkT), (w["wv"], wvT), (w["wq"], wqT))
        U_W, U_X, U_Q, U_END = 0, 12, 20, 28
        block = ctx.enter_context(nc.Block())

        @block.sync
        def _(sp):
            sp.dma_start(x_sb[:, :, :], x.rearrange("b p d -> p b d")).then_inc(x_in, 16)
            for i, (src, _) in enumerate(weights):
                sp.dma_start(w_sb[:, i, :, :], src.rearrange("(o p) d -> p o d", p=P)).then_inc(w_in[i], 16)
            with nc.allow_non_contiguous_dma(reason="512 numbers"):
                sp.dma_start(bq[:, :], w["bq"].rearrange("(g p) -> p g", p=P)).then_inc(b_in, 16)
            for g in range(G):
                sp.wait_ge(lo_done, U_Q + 2 * g + 2)
                for i in range(2):
                    sp.dma_start(f32(q_d[g, :, :, i, :]).rearrange("b p t -> p b t"),
                                 f32(q_st[:, g % 2, i, :]).rearrange("p (b t) -> p b t", b=B)
                                 ).then_inc(q_out[g % 2], 16)
            for i in range(2):
                sp.wait_ge(q_out[i], 16 * 2 * (G // 2))

        @block.gpsimd
        def _(pool):
            make_identity(nc, pool, ident, const)

        @block.tensor
        def _(pe):
            pe.wait_ge(const, 2)
            u = 0
            for i in range(3):
                pe.wait_ge(w_in[i], 16)
                for k in range(KD):
                    if u >= 4:
                        pe.wait_ge(lo_done, u - 3)
                    for o in range(KD):
                        last = nc.tensor.transpose(bank[u % 4][:, o * P:(o + 1) * P],
                                                   w_sb[:, i, o, k * P:(k + 1) * P], ident[:, :])
                    last.then_inc(full, 1)
                    u += 1
            for half in range(2):
                pe.wait_ge(normed, 4 * half + 4)
                for k in range(KD):
                    pe.wait_ge(lo_done, u - 3)
                    for t in range(4):
                        last = nc.tensor.transpose(bank[u % 4][:, t * P:(t + 1) * P],
                                                   xn[:, 4 * half + t, k * P:(k + 1) * P], ident[:, :])
                    last.then_inc(full, 1)
                    u += 1
            pe.wait_ge(lo_done, U_Q)
            for g in range(G):
                for half in range(2):
                    pe.wait_ge(lo_done, u - 3)
                    for k in range(KD):
                        last = product(nc, bank[u % 4][:, :], [a[:, k, g * P:(g + 1) * P] for a in wqT],
                                       [a[:, k, half * 512:(half + 1) * 512] for a in xT], k == 0, k == KD - 1)
                    last.then_inc(full, 1)
                    u += 1

        def places():
            for _, dst in weights:
                for k in range(KD):
                    yield [a[:, k, :] for a in dst]
            for half in range(2):
                for k in range(KD):
                    yield [a[:, k, half * 512:(half + 1) * 512] for a in xT]
            for g in range(G):
                for half in range(2):
                    yield [q_st[:, g % 2, i, half * 512:(half + 1) * 512] for i in range(2)]

        @block.scalar
        def _(act):
            for u, (hi, _) in enumerate(places()):
                if u == 4:
                    norm.scalar(act)
                act.wait_ge(full, u + 1)
                if u < U_Q:
                    nc.scalar.activation(hi, bank[u % 4][:, :], ACT.Copy).then_inc(hi_done, 1)
                else:
                    g = (u - U_Q) // 2
                    if u == U_Q:
                        act.wait_ge(b_in, 16)
                    if g >= 2:
                        act.wait_ge(q_out[g % 2], 32)
                    nc.scalar.activation(hi, bank[u % 4][:, :], ACT.Identity,
                                         bias=bq[:, g:g + 1]).then_inc(hi_done, 1)

        @block.vector
        def _(dve):
            dve.wait_ge(x_in, 16)
            for u, (hi, lo) in enumerate(places()):
                if u == 4:
                    for t in range(B):
                        norm.tile_stats(x_sb, t)
                    norm.vector(dve)
                    dve.wait_ge(norm.step, norm.STEPS)
                    for t in range(B):
                        norm.apply(x_sb[:, t, :], xn[:, t, :], t).then_inc(normed, 1)
                dve.wait_ge(hi_done, u + 1)
                if u < U_Q:
                    nc.vector.tensor_tensor(lo, bank[u % 4][:, :], f32(hi), ALU.subtract).then_inc(lo_done, 1)
                else:
                    g = (u - U_Q) // 2
                    if u == U_Q:
                        dve.wait_ge(b_in, 16)
                    nc.vector.scalar_tensor_tensor(out=lo, in0=bank[u % 4][:, :], scalar=bq[:, g:g + 1],
                                                   in1=f32(hi), op0=ALU.add, op1=ALU.subtract).then_inc(lo_done, 1)


def cross_attention(nc, ctx_in, w, q_d, o_d, wkT, wvT):
    with ExitStack() as ctx:
        def sb(name, shape, dt=F32):
            return ctx.enter_context(nc.sbuf_tensor(name, shape, dt))

        def sem(name):
            return ctx.enter_context(nc.semaphore(name))

        CH = 2
        NCH = NB // CH
        T_UNITS = NCH * 2
        K_UNITS = KV // 512
        V_UNITS = NB
        SUMS = NB // 2 - 1
        PAIRS = NB // 2
        QUARTERS = 4
        AHEAD = 4

        def items(text):
            return [(x[0], int(x[1:])) for x in text.split()]

        T_AT = {NB - 4: 0, NB - 3: 1, NB - 2: 2, NB - 1: 3}
        PLAN_T = items("T0 T1 T2 T3")
        PLAN_A = items("K0 T4 V0 T5 V1 T6 S0 S1 S2 S3")
        PLAN_B = items("T7 V2 V3 K1 V4 T8 S4 S5 V5 T9 S6 S7 V6 T10 D0 T11 V7 K2 V8 T12 S8 S9 V9 T13 S10 S11 "
                       "T14 V10 T15 V11 K3 V12 S12 S13 S14 S15 V13 V14 V15")
        PLAN = PLAN_T + PLAN_A + PLAN_B
        ACT_A = items("K0 T4 V0 T5 P0 P1 V1 T6 P2 P3 P4 P5 P6 P7 S0 S1 S2 S3")
        DVE_A = items("K0 T4 P0 P1 T5 P2 P3 T6 P4 P5 P6 P7 N0 S0 S1 S2 S3")
        KEYS_AT = [{3: 0, 4: 1, 5: 2, 7: 3}, {0: 0, 1: 1, 3: 2, 4: 3}, {0: 0, 1: 1, 3: 2, 4: 3}]

        UNIT = {x: i for i, x in enumerate(x for x in PLAN if x[0] in "TKV")}
        SPLIT = {x: i for i, x in enumerate(x for x in PLAN if x[0] in "TK")}
        assert len(SPLIT) == T_UNITS + K_UNITS and len(UNIT) == len(SPLIT) + V_UNITS
        SIDE = 2
        KEY_UNITS = (G - 1) * K_UNITS
        UNITS = len(UNIT) + KEY_UNITS
        SPLITS = len(SPLIT) + KEY_UNITS
        assert UNITS % 2 == 0

        ident = sb("b_ident", [P, P])
        ones = sb("b_ones", [P, HD])
        bk = sb("b_bk", [P, G])
        bv = sb("b_bv", [P, G])
        cin = sb("b_cin", [P, 2, CH, D])
        cT = [sb(f"b_cT{i}", [P, KD, KV], F32R) for i in range(2)]
        kT = [sb(f"b_kT{i}", [P, KV], F32R) for i in range(2)]
        v = sb("b_v", [P, NB, D])
        v_side = sb("b_v_side", [P, SIDE, P])
        s = sb("b_s", [P, NB, HG * P])
        qbd = sb("b_qbd", [P, 2, 2, HG, P], F32R)
        mx = sb("b_mx", [P, 2, HG * P])
        mb = sb("b_mb", [P, HG * P])
        acc = sb("b_acc", [P, 2, HG * P])
        rD = sb("b_rD", [P, P])
        oq = sb("b_oq", [P, P])
        o_st = sb("b_o", [P, 2, P])
        work = [ctx.enter_context(nc.psum_tensor(f"b_work{i}", [P, 512], F32)) for i in range(2)]
        psS = [ctx.enter_context(nc.psum_tensor(f"b_psS{i}", [P, 512], F32)) for i in range(4)]
        psO = [ctx.enter_context(nc.psum_tensor(f"b_psO{i}", [P, 512], F32)) for i in range(2)]

        const = sem("b_const")
        bias_in = sem("b_bias_in")
        cin_in = [sem(f"b_cin_in{i}") for i in range(2)]
        q_in = [sem(f"b_q_in{i}") for i in range(2)]
        work_full = sem("b_work_full")
        hi_done = sem("b_hi_done")
        split_done = sem("b_split_done")
        v_done = sem("b_v_done")
        s_full = sem("b_s_full")
        mx_done = sem("b_mx_done")
        s_moved = sem("b_s_moved")
        fold_done = sem("b_fold_done")
        par_begun = sem("b_par_begun")
        par_done = sem("b_par_done")
        sub_done = sem("b_sub_done")
        exp_done = sem("b_exp_done")
        pv_done = sem("b_pv_done")
        sum_done = sem("b_sum_done")
        od_full = sem("b_od_full")
        rd_done = sem("b_rd_done")
        od_free = sem("b_od_free")
        o_out = sem("b_o_out")
        o_stored = sem("b_o_stored")
        block = ctx.enter_context(nc.Block())

        def unit_full(bn, x):
            return bn * UNITS + (UNIT[x] + 1)

        def unit_split(bn, x):
            return bn * SPLITS + (SPLIT[x] + 1)

        def keys_full(b, i):
            return b * UNITS + (len(UNIT) + i + 1)

        def keys_split(b, i):
            return b * SPLITS + (len(SPLIT) + i + 1)

        @block.sync
        def _(sp):
            sp.sem_inc(o_stored, 2)
            with nc.allow_non_contiguous_dma(reason="512 numbers"):
                sp.dma_start(bk[:, :], w["bk"].rearrange("(g p) -> p g", p=P)).then_inc(bias_in, 16)
                sp.dma_start(bv[:, :], w["bv"].rearrange("(g p) -> p g", p=P)).then_inc(bias_in, 16)

            def load_context(b, c):
                sp.dma_start(cin[:, c % 2, :, :],
                             ctx_in[b, c * CH * P:(c + 1) * CH * P, :].rearrange("(o p) d -> p o d", p=P)
                             ).then_inc(cin_in[c % 2], 16)

            def load_queries(b, g):
                for j in range(HG):
                    sp.dma_start(f32(qbd[j * HD:(j + 1) * HD, g % 2, :, j, :]),
                                 f32(q_d[g, b, j * HD:(j + 1) * HD, :, :])).then_inc(q_in[g % 2], 16)

            def store_output(b, g):
                sp.wait_ge(od_free, b * G + (g + 1 + 2))
                sp.dma_start(o_d[g, b, :, :], o_st[:, g % 2, :]).then_inc(o_out, 16)
                sp.wait_ge(o_out, b * (16 * G) + 16 * (g + 1))
                sp.sem_inc(o_stored, 1)

            def rest_of_context(b, chunks):
                for c in chunks:
                    sp.wait_ge(work_full, unit_full(b, ("T", 2 * (c - 2) + 1)))
                    load_context(b, c)

            load_context(0, 0)
            load_context(0, 1)
            sp.wait_ge(const, 4)
            load_queries(0, 0)
            load_queries(0, 1)
            rest_of_context(0, range(2, NCH))

            def batch(b, last):
                if not last:
                    sp.wait_ge(work_full, unit_full(b, ("T", T_UNITS - 1)))
                    load_context(b + 1, 0)
                    load_context(b + 1, 1)
                for g in range(G):
                    if g == G - 1 and not last:
                        rest_of_context(b + 1, (2, 3))
                    if g < G - 2 or not last:
                        sp.wait_ge(s_full, b * (G * NB) + NB * (g + 1))
                        load_queries(b + (g + 2) // G, (g + 2) % G)
                    if g >= 1:
                        store_output(b, g - 1)
                if not last:
                    rest_of_context(b + 1, range(4, NCH))
                store_output(b, G - 1)

            with sp.Fori(0, B - 1) as b:
                batch(b, False)
            batch(B - 1, True)

        @block.gpsimd
        def _(pool):
            pool.sem_inc(sum_done, SUMS)
            pool.sem_inc(par_done, 1)
            make_identity(nc, pool, ident, const)
            nc.gpsimd.memset(ones[:, :], 1.0).then_inc(const, 1)
            nc.gpsimd.memset(f32(qbd[:, :, :, :, :]), 0.0).then_inc(const, 1)

            def batch(b):
                for g in range(G):
                    pool.wait_ge(fold_done, b * G + (g + 1))
                    pool.sem_inc(par_begun, 1)
                    nc.gpsimd.partition_all_reduce(mb[:, :], mx[:, 0, :], P, RMAX).then_inc(par_done, 1)
                    for i in range(SUMS):
                        pool.wait_ge(exp_done, b * (G * PAIRS) + (g * PAIRS + i + 2))
                        if i == 0:
                            pool.wait_ge(od_full, b * G + (g + 1))
                            a = s[:, 0:2, :]
                        else:
                            pool.wait_ge(sum_done, b * (G * SUMS) + (SUMS + g * SUMS + i))
                            a = acc[:, :, :]
                        nc.gpsimd.tensor_tensor(acc[:, :, :], a, s[:, 2 * i + 2:2 * i + 4, :],
                                                ALU.add).then_inc(sum_done, 1)

            with pool.Fori(0, B) as b:
                batch(b)

        @block.tensor
        def _(pe):
            pe.sem_inc(od_full, 1)
            pe.sem_inc(pv_done, QUARTERS)
            pe.wait_ge(const, 4)

            def plan_item(bn, x):
                kind, n = x
                if kind == "S":
                    scores(bn, 0, [n])
                elif kind == "D":
                    if not isinstance(bn, int):
                        denominators(bn - 1, G - 1)
                else:
                    i = UNIT[x]
                    bank = work[i % 2]
                    before = [y for y in UNIT if UNIT[y] == i - 2]
                    if not before:
                        reached(pe, split_done, bn * SPLITS + (i - 1))
                    elif before[0][0] == "V":
                        pe.wait_ge(v_done, bn * V_UNITS + (before[0][1] + 1))
                    else:
                        pe.wait_ge(split_done, unit_split(bn, before[0]))
                    if kind == "T":
                        c, kk = n // 2, n % 2
                        if kk == 0:
                            pe.wait_ge(cin_in[c % 2], bn * (16 * NCH // 2) + 16 * (c // 2 + 1))
                        for k in range(2):
                            for o in range(CH):
                                last = nc.tensor.transpose(bank[:, (k * CH + o) * P:(k * CH + o + 1) * P],
                                                           cin[:, c % 2, o, (2 * kk + k) * P:(2 * kk + k + 1) * P],
                                                           ident[:, :])
                    elif kind == "K":
                        pe.wait_ge(split_done, unit_split(bn, ("T", 4 * n + 3)))
                        last = keys_bank(bank, 0, n)
                    else:
                        for k in range(KD):
                            last = product(nc, bank[:, :], [a[:, k, n * P:(n + 1) * P] for a in cT],
                                           [a[:, k, :] for a in wvT], k == 0, k == KD - 1)
                    last.then_inc(work_full, 1)

            def keys_bank(bank, g, c):
                for k in range(KD):
                    last = product(nc, bank[:, :], [a[:, k, g * P:(g + 1) * P] for a in wkT],
                                   [a[:, k, c * 512:(c + 1) * 512] for a in cT], k == 0, k == KD - 1)
                return last

            def keys(b, g):
                for c in range(K_UNITS):
                    i = (g - 1) * K_UNITS + c
                    if i < 2:
                        pe.wait_ge(v_done, b * V_UNITS + (V_UNITS + i - 1))
                    else:
                        pe.wait_ge(split_done, keys_split(b, i - 2))
                    keys_bank(work[i % 2], g, c).then_inc(work_full, 1)

            def scores(b, g, blocks):
                if 0 in blocks:
                    pe.wait_ge(q_in[g % 2], b * (16 * HG * 2) + 16 * HG * (g // 2 + 1))
                for t in blocks:
                    if t % 4 == 0:
                        pe.wait_ge(split_done, keys_split(b, (g - 1) * K_UNITS + t // 4) if g
                                   else unit_split(b, ("K", t // 4)))
                    pe.wait_ge(s_moved, b * (G * NB) + (g * NB + t + 1))
                    product(nc, psS[t % 4][:, :], [a[:, t * P:(t + 1) * P] for a in kT],
                            [qbd[:, g % 2, i, :, :] for i in range(2)], True, True).then_inc(s_full, 1)

            def outputs(b, g):
                if g == 0:
                    pe.wait_ge(v_done, b * V_UNITS + V_UNITS)
                pe.wait_ge(od_free, b * G + (g + 1))
                for t in range(NB):
                    if t % 2 == 0:
                        pe.wait_ge(exp_done, b * (G * PAIRS) + (g * PAIRS + t // 2 + 1))
                    for j in range(HG):
                        h = slice(j * HD, (j + 1) * HD)
                        last = nc.tensor.matmul(psO[g % 2][h, 0:P], v[:, t, g * P + j * HD:g * P + (j + 1) * HD],
                                                s[:, t, j * P:(j + 1) * P], start=t == 0, stop=t == NB - 1)
                    if t % QUARTERS == QUARTERS - 1:
                        last.then_inc(pv_done, 1)

            def denominators(b, g):
                pe.wait_ge(sum_done, b * (G * SUMS) + (SUMS + (g + 1) * SUMS))
                for i in range(2):
                    for j in range(HG):
                        last = nc.tensor.matmul(psO[g % 2][j * HD:(j + 1) * HD, P:2 * P], ones[:, :],
                                                acc[:, i, j * P:(j + 1) * P], start=i == 0, stop=i == 1)
                last.then_inc(od_full, 1)

            def batch(b, last):
                for g in range(G):
                    if g >= 1:
                        for t in range(AHEAD, NB):
                            if g == G - 1 and t in T_AT and not last:
                                plan_item(b + 1, ("T", T_AT[t]))
                            scores(b, g, [t])
                        if g < G - 1 or last:
                            denominators(b, g - 1)
                    if g < G - 1:
                        keys(b, g + 1)
                        scores(b, g + 1, range(AHEAD))
                    elif not last:
                        for x in PLAN_A:
                            plan_item(b + 1, x)
                        denominators(b, g - 1)
                    outputs(b, g)
                if last:
                    denominators(b, G - 1)
                else:
                    for x in PLAN_B:
                        plan_item(b + 1, x)

            for x in PLAN:
                plan_item(0, x)
            with pe.Fori(0, B - 1) as b:
                batch(b, False)
            batch(B - 1, True)

        def context_place(a, n):
            c, kk = n // 2, n % 2
            return a[:, 2 * kk:2 * kk + 2, c * CH * P:(c + 1) * CH * P]

        def two(ps):
            return ps[:, :].rearrange("p (k t) -> p k t", k=2)

        @block.scalar
        def _(act):
            act.sem_inc(s_moved, 4)

            def plan_item(bn, x):
                kind, n = x
                if kind == "S":
                    move(bn, 0, n)
                elif kind == "P":
                    exps(bn - 1, G - 1, n)
                elif kind in "TKV":
                    act.wait_ge(work_full, unit_full(bn, x))
                    bank = work[UNIT[x] % 2]
                    if kind == "T":
                        nc.scalar.activation(context_place(cT[0], n), two(bank), ACT.Copy).then_inc(hi_done, 1)
                    elif kind == "K":
                        keys_hi(0, n, bank)
                    elif n < SIDE:
                        nc.scalar.activation(v[:, n, 0:D - P], bank[:, 0:D - P], ACT.Copy)
                        nc.scalar.activation(v_side[:, n, :], bank[:, D - P:D], ACT.Copy).then_inc(v_done, 1)
                    else:
                        if n == SIDE:
                            act.wait_ge(pv_done, bn * (G * QUARTERS) + QUARTERS)
                            act.wait_ge(v_done, bn * V_UNITS + SIDE)
                            nc.scalar.activation(v[:, 0:SIDE, D - P:D], v_side[:, :, :], ACT.Copy)
                        nc.scalar.activation(v[:, n, :], bank[:, :], ACT.Copy).then_inc(v_done, 1)

            def keys_hi(g, c, bank):
                nc.scalar.activation(kT[0][:, c * 512:(c + 1) * 512], bank[:, :], ACT.Identity,
                                     bias=bk[:, g:g + 1]).then_inc(hi_done, 1)

            def move(b, g, t):
                act.wait_ge(mx_done, b * (G * NB) + (g * NB + t + 1))
                if t % QUARTERS == 0:
                    act.wait_ge(pv_done, b * (G * QUARTERS) + (g * QUARTERS + t // QUARTERS + 1))
                if t % 2 == 0:
                    act.wait_ge(sum_done, b * (G * SUMS) + (g * SUMS + max(1, t // 2)))
                nc.scalar.activation(s[:, t, :], psS[t % 4][:, :], ACT.Copy).then_inc(s_moved, 1)

            def exps(b, g, q):
                act.wait_ge(sub_done, b * (G * PAIRS) + (g * PAIRS + q + 1))
                pair = s[:, 2 * q:2 * q + 2, :]
                nc.scalar.activation(pair, pair, ACT.Exp, scale=SCALE).then_inc(exp_done, 1)

            act.wait_ge(bias_in, 32)
            for x in PLAN:
                plan_item(0, x)

            def batch(b, last):
                for g in range(G):
                    if g >= 1:
                        for t in range(NB):
                            if g == G - 1 and t in T_AT and not last:
                                plan_item(b + 1, ("T", T_AT[t]))
                            move(b, g, t)
                    if g < G - 1:
                        for q in range(PAIRS + 1):
                            if q in KEYS_AT[g]:
                                c = KEYS_AT[g][q]
                                i = g * K_UNITS + c
                                act.wait_ge(work_full, keys_full(b, i))
                                keys_hi(g + 1, c, work[i % 2])
                            if q >= 1:
                                exps(b, g, q - 1)
                    elif last:
                        for q in range(PAIRS):
                            exps(b, g, q)
                    else:
                        for x in ACT_A + PLAN_B:
                            plan_item(b + 1, x)

            with act.Fori(0, B - 1) as b:
                batch(b, False)
            batch(B - 1, True)

        @block.vector
        def _(dve):
            dve.sem_inc(od_free, 2)

            def plan_item(bn, x):
                kind, n = x
                if kind == "S":
                    maximum(bn, 0, n)
                elif kind == "P":
                    subtract(bn - 1, G - 1, n)
                elif kind == "N":
                    normalise(bn - 1, G - 2)
                elif kind == "D":
                    if not isinstance(bn, int):
                        normalise(bn - 1, G - 1)
                elif kind in "TK":
                    dve.wait_ge(hi_done, unit_split(bn, x))
                    bank = work[UNIT[x] % 2]
                    if kind == "T":
                        nc.vector.tensor_tensor(context_place(cT[1], n), two(bank), f32(context_place(cT[0], n)),
                                                ALU.subtract).then_inc(split_done, 1)
                    else:
                        keys_lo(0, n, bank)

            def keys_lo(g, c, bank):
                part = slice(c * 512, (c + 1) * 512)
                nc.vector.scalar_tensor_tensor(out=kT[1][:, part], in0=bank[:, :], scalar=bk[:, g:g + 1],
                                               in1=f32(kT[0][:, part]), op0=ALU.add,
                                               op1=ALU.subtract).then_inc(split_done, 1)

            def maximum(b, g, t):
                dve.wait_ge(s_full, b * (G * NB) + (g * NB + t + 1))
                if t < 2:
                    if t == 0:
                        dve.wait_ge(par_done, b * G + (g + 1))
                    nc.vector.tensor_copy(mx[:, t, :], psS[t % 4][:, :]).then_inc(mx_done, 1)
                else:
                    dve.wait_ge(mx_done, b * (G * NB) + (g * NB + t - 1))
                    nc.vector.tensor_tensor(mx[:, t % 2, :], psS[t % 4][:, :], mx[:, t % 2, :],
                                            ALU.max).then_inc(mx_done, 1)
                if t == NB - 1:
                    dve.wait_ge(mx_done, b * (G * NB) + (g + 1) * NB)
                    nc.vector.tensor_tensor(mx[:, 0, :], mx[:, 0, :], mx[:, 1, :], ALU.max).then_inc(fold_done, 1)

            def subtract(b, g, q):
                if q == 0:
                    dve.wait_ge(par_done, b * G + (g + 2))
                dve.wait_ge(s_moved, b * (G * NB) + (4 + g * NB + 2 * q + 2))
                pair = s[:, 2 * q:2 * q + 2, :]
                top = mb[:, :].rearrange("p (o n) -> p o n", o=1).broadcast_to([P, 2, HG * P])
                nc.vector.tensor_tensor(pair, pair, top, ALU.subtract).then_inc(sub_done, 1)

            def normalise(b, g):
                dve.wait_ge(od_full, b * G + (g + 2))
                nc.vector.reciprocal(rD[:, :], psO[g % 2][:, P:2 * P]).then_inc(rd_done, 1)
                dve.wait_ge(rd_done, b * (2 * G) + (2 * g + 1))
                nc.vector.tensor_tensor(oq[:, :], psO[g % 2][:, 0:P], rD[:, :], ALU.mult).then_inc(rd_done, 1)
                dve.wait_ge(rd_done, b * (2 * G) + (2 * g + 2))
                dve.wait_ge(o_stored, b * G + (g + 1))
                nc.vector.tensor_scalar(o_st[:, g % 2, :], oq[:, :], bv[:, g:g + 1], None,
                                        ALU.add).then_inc(od_free, 1)

            dve.wait_ge(bias_in, 32)
            for x in PLAN:
                plan_item(0, x)

            def batch(b, last):
                for g in range(G):
                    if g >= 1:
                        for t in range(NB):
                            maximum(b, g, t)
                            if g == G - 1 and t in T_AT and not last:
                                plan_item(b + 1, ("T", T_AT[t]))
                        if g < G - 1 or last:
                            normalise(b, g - 1)
                    if g < G - 1 or last:
                        for q in range(PAIRS):
                            if g < G - 1 and q in KEYS_AT[g]:
                                c = KEYS_AT[g][q]
                                i = g * K_UNITS + c
                                dve.wait_ge(hi_done, keys_split(b, i))
                                keys_lo(g + 1, c, work[i % 2])
                            subtract(b, g, q)
                    else:
                        for x in DVE_A + PLAN_B:
                            plan_item(b + 1, x)
                if last:
                    normalise(b, G - 1)

            with dve.Fori(0, B - 1) as b:
                batch(b, False)
            batch(B - 1, True)


def transpose_units(nc, pe, bank, ident, src, blocks, u, full, lo_done):
    for k in range(src.shape[2] // P):
        for o4 in range(blocks // 4):
            if u >= len(bank):
                pe.wait_ge(lo_done, u - len(bank) + 1)
            for o in range(4):
                last = nc.tensor.transpose(bank[u % len(bank)][:, o * P:(o + 1) * P],
                                           src[:, 4 * o4 + o, k * P:(k + 1) * P], ident)
            last.then_inc(full, 1)
            u += 1
    return u


def output_projection(nc, x, w, o_d, x1, x1T):
    with ExitStack() as ctx:
        def sb(name, shape, dt=F32):
            return ctx.enter_context(nc.sbuf_tensor(name, shape, dt))

        def sem(name):
            return ctx.enter_context(nc.semaphore(name))

        ident = sb("c_ident", [P, P])
        o_sb = sb("c_o", [P, G, B, P])
        oT = [sb(f"c_oT{i}", [P, G, TOK], F32R) for i in range(2)]
        wo = sb("c_wo", [P, KD, D])
        woT = [sb(f"c_woT{i}", [P, KD, D], F32R) for i in range(2)]
        bo_row = sb("c_bo_row", [1, D])
        bo = sb("c_bo", [P, D])
        xn = sb("c_xn", [P, B, D])
        bank = [ctx.enter_context(nc.psum_tensor(f"c_ps{i}", [P, 512], F32)) for i in range(4)]
        norm = Norm(nc, ctx, "c_norm")
        const = sem("c_const")
        x_in = sem("c_x_in")
        o_in = sem("c_o_in")
        w_in = sem("c_w_in")
        b_in = sem("c_b_in")
        bo_ready = sem("c_bo_ready")
        full = sem("c_full")
        hi_done = sem("c_hi")
        lo_done = sem("c_lo")
        o_hi = sem("c_o_hi")
        o_lo = sem("c_o_lo")
        normed = sem("c_normed")
        U_O = KD
        U_X = U_O + B
        block = ctx.enter_context(nc.Block())

        @block.sync
        def _(sp):
            sp.dma_start(wo[:, :, :], w["wo"].rearrange("(o p) d -> p o d", p=P)).then_inc(w_in, 16)
            sp.dma_start(bo_row[:, :], w["bo"].rearrange("(a d) -> a d", a=1)).then_inc(b_in, 16)
            sp.dma_start(x1[:, :, :], x.rearrange("b p d -> p b d")).then_inc(x_in, 16)
            for g in range(G):
                sp.dma_start(o_sb[:, g, :, :], o_d[g].rearrange("b p t -> p b t")).then_inc(o_in, 16)

        @block.gpsimd
        def _(pool):
            make_identity(nc, pool, ident, const)
            pool.wait_ge(b_in, 16)
            nc.gpsimd.partition_broadcast(bo[:, :], bo_row[:, :], P).then_inc(bo_ready, 1)
            pool.wait_ge(bo_ready, 1)
            pool.wait_ge(x_in, 16)
            for t in range(B):
                nc.gpsimd.tensor_tensor(x1[:, t, :], x1[:, t, :], bo[:, :], ALU.add).then_inc(bo_ready, 1)

        @block.tensor
        def _(pe):
            pe.wait_ge(const, 2)
            pe.wait_ge(w_in, 16)
            u = transpose_units(nc, pe, bank, ident[:, :], wo, KD, 0, full, lo_done)
            pe.wait_ge(lo_done, U_O)
            pe.wait_ge(o_lo, G)
            for t in range(B):
                pe.wait_ge(lo_done, u - 3)
                for g in range(G):
                    last = product(nc, bank[u % 4][:, :], [a[:, g, t * P:(t + 1) * P] for a in oT],
                                   [a[:, g, :] for a in woT], g == 0, g == G - 1)
                last.then_inc(full, 1)
                u += 1
            for half in range(2):
                pe.wait_ge(normed, 4 * half + 4)
                u = transpose_units(nc, pe, bank, ident[:, :], xn[:, 4 * half:4 * half + 4, :], 4, u, full, lo_done)

        def places():
            for k in range(KD):
                yield k, [a[:, k, :] for a in woT]
            for half in range(2):
                for k in range(KD):
                    yield U_X + 4 * half + k, [a[:, k, half * 512:(half + 1) * 512] for a in x1T]

        @block.scalar
        def _(act):
            for g in range(G):
                act.wait_ge(o_in, 16 * G)
                nc.scalar.activation(oT[0][:, g, :], o_sb[:, g, :, :].rearrange("p b t -> p (b t)"),
                                     ACT.Copy).then_inc(o_hi, 1)
            for n, (u, (hi, _)) in enumerate(places()):
                if u == U_X:
                    norm.scalar(act)
                act.wait_ge(full, u + 1)
                nc.scalar.activation(hi, bank[u % 4][:, :], ACT.Copy).then_inc(hi_done, 1)

        @block.vector
        def _(dve):
            at = list(places())

            def lo(n):
                u, (hi, low) = at[n]
                dve.wait_ge(hi_done, n + 1)
                nc.vector.tensor_tensor(low, bank[u % 4][:, :], f32(hi), ALU.subtract).then_inc(lo_done, 1)

            for g in range(G):
                dve.wait_ge(o_hi, g + 1)
                nc.vector.tensor_tensor(oT[1][:, g, :], o_sb[:, g, :, :].rearrange("p b t -> p (b t)"),
                                        f32(oT[0][:, g, :]), ALU.subtract).then_inc(o_lo, 1)
            for n in range(KD):
                lo(n)
            for t in range(B):
                dve.wait_ge(bo_ready, t + 2)
                dve.wait_ge(full, U_O + t + 1)
                nc.vector.tensor_tensor(x1[:, t, :], bank[(U_O + t) % 4][:, :], x1[:, t, :],
                                        ALU.add).then_inc(lo_done, 1)
                dve.wait_ge(lo_done, U_O + t + 1)
                norm.tile_stats(x1, t)
            norm.vector(dve)
            dve.wait_ge(norm.step, norm.STEPS)
            for t in range(B):
                norm.apply(x1[:, t, :], xn[:, t, :], t).then_inc(normed, 1)
            for n in range(KD, KD + 2 * KD):
                lo(n)


def self_projections(nc, w, x1T, q2_d, k2_d, v2):
    with ExitStack() as ctx:
        def sb(name, shape, dt=F32):
            return ctx.enter_context(nc.sbuf_tensor(name, shape, dt))

        def sem(name):
            return ctx.enter_context(nc.semaphore(name))

        ident = sb("d_ident", [P, P])
        wn = sb("d_w", [P, 2, KB, D])
        wT = [[sb(f"d_wT{r}{i}", [P, KD, W2], F32R) for i in range(2)] for r in range(2)]
        st = sb("d_st", [P, 2, 2, 512], F32R)
        bank = [ctx.enter_context(nc.psum_tensor(f"d_ps{i}", [P, 512], F32)) for i in range(8)]
        const = sem("d_const")
        w_in = [sem(f"d_w_in{i}") for i in range(2)]
        full = sem("d_full")
        hi_done = sem("d_hi")
        done = sem("d_done")
        st_out = [sem(f"d_st_out{i}") for i in range(2)]
        TU = KD * KB // 4
        PU = KB * 2
        U_QT, U_KT, U_Q, U_VT, U_K, U_V = 0, TU, 2 * TU, 2 * TU + PU, 3 * TU + PU, 3 * TU + 2 * PU
        block = ctx.enter_context(nc.Block())
        weights = (w["Wq"], w["Wk"], w["Wv"])

        @block.sync
        def _(sp):
            def load(i):
                sp.dma_start(wn[:, i % 2, :, :], weights[i].rearrange("(o p) d -> p o d", p=P)
                             ).then_inc(w_in[i % 2], 16)

            load(0)
            load(1)
            sp.wait_ge(full, U_KT)
            load(2)
            for n in range(2 * PU):
                u = (U_Q if n < PU else U_K - PU) + n
                blk, half = (n % PU) // 2, n % 2
                dst = (q2_d, k2_d)[n // PU]
                sp.wait_ge(done, u + 1)
                for i in range(2):
                    sp.dma_start(f32(dst[4 * half:4 * half + 4, blk // 4, :, blk % 4, i, :]).rearrange("b p t -> p b t"),
                                 f32(st[:, n % 2, i, :]).rearrange("p (b t) -> p b t", b=4)
                                 ).then_inc(st_out[n % 2], 16)
            for i in range(2):
                sp.wait_ge(st_out[i], 32 * PU)

        @block.gpsimd
        def _(pool):
            make_identity(nc, pool, ident, const)

        @block.tensor
        def _(pe):
            pe.wait_ge(const, 2)

            def weight(i, u):
                pe.wait_ge(w_in[i % 2], 16 * (i // 2 + 1))
                return transpose_units(nc, pe, bank, ident[:, :], wn[:, i % 2, :, :], KB, u, full, done)

            def heads(r, u, first):
                pe.wait_ge(done, first)
                for blk in range(KB):
                    for half in range(2):
                        pe.wait_ge(done, u - len(bank) + 1)
                        for k in range(KD):
                            last = product(nc, bank[u % 8][:, :], [a[:, k, blk * P:(blk + 1) * P] for a in wT[r]],
                                           [a[:, k, half * 512:(half + 1) * 512] for a in x1T], k == 0, k == KD - 1)
                        last.then_inc(full, 1)
                        u += 1
                return u

            u = weight(0, 0)
            u = weight(1, u)
            u = heads(0, u, U_KT)
            u = weight(2, u)
            u = heads(1, u, U_Q)
            pe.wait_ge(done, U_K)
            for t in range(B):
                for half in range(2):
                    pe.wait_ge(done, u - len(bank) + 1)
                    for k in range(KD):
                        last = product(nc, bank[u % 8][:, :], [a[:, k, t * P:(t + 1) * P] for a in x1T],
                                       [a[:, k, half * 512:(half + 1) * 512] for a in wT[0]], k == 0, k == KD - 1)
                    last.then_inc(full, 1)
                    u += 1

        def places():
            u = n = 0
            for kind, r in (("w", 0), ("w", 1), ("h", 0), ("w", 0), ("h", 1)):
                for i in range(TU if kind == "w" else PU):
                    if kind == "w":
                        yield u, None, [a[:, i // 2, (i % 2) * 512:(i % 2 + 1) * 512] for a in wT[r]]
                    else:
                        yield u, n, [st[:, n % 2, j, :] for j in range(2)]
                        n += 1
                    u += 1

        @block.scalar
        def _(act):
            for u, n, (hi, _) in places():
                act.wait_ge(full, u + 1)
                if n is not None and n >= 2:
                    act.wait_ge(st_out[n % 2], 32 * (n // 2))
                nc.scalar.activation(hi, bank[u % 8][:, :], ACT.Copy).then_inc(hi_done, 1)

        @block.vector
        def _(dve):
            for u, _, (hi, lo) in places():
                dve.wait_ge(hi_done, u + 1)
                nc.vector.tensor_tensor(lo, bank[u % 8][:, :], f32(hi), ALU.subtract).then_inc(done, 1)
            for i in range(2 * B):
                u = U_V + i
                dve.wait_ge(full, u + 1)
                nc.vector.tensor_copy(v2[:, i // 2, (i % 2) * 512:(i % 2 + 1) * 512],
                                      bank[u % 8][:, :]).then_inc(done, 1)


def differential_attention(nc, w, q2_d, k2_d, v2, x1, norm):
    with ExitStack() as ctx:
        def sb(name, shape, dt=F32):
            return ctx.enter_context(nc.sbuf_tensor(name, shape, dt))

        def sem(name):
            return ctx.enter_context(nc.semaphore(name))

        HALF = KB // 2
        RING = 4
        LAG_T, LAG_PV, LAG_ADD = 3, 4, 2
        ident = sb("e_ident", [P, P])
        ident_b = sb("e_ident_b", [P, P], BF16)
        mask = sb("e_mask", [P, P])
        mask_b = sb("e_mask_b", [P, HG, P], BF16)
        wn = sb("e_w", [P, KD, W2])
        woT = [sb(f"e_woT{i}", [P, KB, D], F32R) for i in range(2)]
        lam_in_sb = sb("e_lam_in", [1, 4, HEADS * HD])
        lam_p = sb("e_lam_p", [1, 2, HEADS * HD])
        lam_s = sb("e_lam_s", [1, 2, HEADS])
        lam_e = sb("e_lam_e", [1, 2, HEADS])
        lam_d = sb("e_lam_d", [1, HEADS])
        coef_row = sb("e_coef_row", [1, HEADS, 2])
        coef = sb("e_coef", [P, HEADS, 2])
        rs = sb("e_rs", [P, 1])
        q2 = sb("e_q2", [P, 2, HALF, 2, P], F32R)
        k2 = sb("e_k2", [P, 2, HALF, 2, HG, P], F32R)
        sm = sb("e_sm", [P, RING, HG, P])
        top = sb("e_top", [P, RING, HG])
        ntop = sb("e_ntop", [P, RING, HG])
        sums = sb("e_sums", [P, RING, HG])
        rsum = sb("e_rsum", [P, RING, HG])
        cf = sb("e_cf", [P, RING, HG])
        at = sb("e_at", [P, RING, 2, P])
        aT = sb("e_aT", [P, 2, 2, P])
        o_sb = sb("e_o", [P, W2])
        sq = sb("e_sq", [P, W2])
        ms = sb("e_ms", [P, HEADS])
        expo = sb("e_expo", [P, HEADS])
        root = sb("e_root", [P, HEADS])
        nt = sb("e_nt", [P, HEADS])
        on = sb("e_on", [P, W2])
        oT = [sb(f"e_oT{i}", [P, KB, P], F32R) for i in range(2)]
        psS = [ctx.enter_context(nc.psum_tensor(f"e_psS{i}", [P, 512], F32)) for i in range(RING)]
        psA = ctx.enter_context(nc.psum_tensor("e_psA", [P, 2, P], F32))
        psO = [ctx.enter_context(nc.psum_tensor(f"e_psO{i}", [P, 512], F32)) for i in range(2)]
        psW = ctx.enter_context(nc.psum_tensor("e_psW", [P, 512], F32))

        const = sem("e_const")
        w_in = sem("e_w_in")
        lam_in = sem("e_lam_in_s")
        lam_step = sem("e_lam_step")
        lam_exp = sem("e_lam_exp")
        coef_ready = sem("e_coef_ready")
        qk_in = [sem(f"e_qk_in{i}") for i in range(2)]
        w_full = sem("e_w_full")
        w_hi = sem("e_w_hi")
        w_lo = sem("e_w_lo")
        s_full = sem("e_s_full")
        top_step = sem("e_top_step")
        exp_done = sem("e_exp_done")
        cf_step = sem("e_cf_step")
        mul_done = sem("e_mul_done")
        a_done = sem("e_a_done")
        a_full = sem("e_a_full")
        aT_done = sem("e_aT_done")
        pv_done = sem("e_pv_done")
        o_copied = sem("e_o_copied")
        o_step = sem("e_o_step")
        root_done = sem("e_root_done")
        on_done = sem("e_on_done")
        y_full = sem("e_y_full")
        x_done = sem("e_x_done")
        W_UNITS = KB
        O_STEPS = 6
        Y_FIRST, Y_STEPS = 4, 3
        block = ctx.enter_context(nc.Block())

        def batches(engine, batch):
            batch(0, True, False, False)
            batch(1, True, True, False)
            with engine.Fori(2, B) as b:
                batch(b, True, True, True)
            batch(B, False, True, True)
            batch(B + 1, False, False, True)

        def lagged(n, lag, front, back):
            if n >= lag:
                return (0, n - lag) if front else None
            return (-1, n - lag + KB) if back else None

        @block.sync
        def _(sp):
            sp.dma_start(wn[:, :, :], w["Wo"].rearrange("(o p) d -> p o d", p=P)).then_inc(w_in, 16)
            for i, name in enumerate(("lq1", "lq2", "lk1", "lk2")):
                sp.dma_start(lam_in_sb[:, i, :], w[name].rearrange("(a h) d -> a (h d)", a=1)).then_inc(lam_in, 16)
            with nc.allow_non_contiguous_dma(reason="64 numbers"):
                for i in range(2):
                    sp.dma_start(rs[64 * i:64 * i + 64, :], w["rms_scale"].rearrange("(d a) -> d a", a=1)
                                 ).then_inc(lam_in, 16)
            sp.wait_ge(const, 7)

            def load(b, hf):
                sp.dma_start(f32(q2[:, hf, :, :, :]), f32(q2_d[b, hf, :, :, :, :])).then_inc(qk_in[hf], 16)
                for j in range(HG):
                    sp.dma_start(f32(k2[j * HD:(j + 1) * HD, hf, :, :, j, :]),
                                 f32(k2_d[b, hf, j * HD:(j + 1) * HD, :, :, :])).then_inc(qk_in[hf], 16)

            load(0, 0)
            load(0, 1)
            with sp.Fori(1, B) as b:
                for hf in range(2):
                    sp.wait_ge(s_full, b * KB + (HALF + hf * HALF - KB))
                    load(b, hf)

        @block.gpsimd
        def _(pool):
            make_identity(nc, pool, ident, const)
            nc.gpsimd.memset(mask[:, :], 0.0).then_inc(const, 1)
            pool.wait_ge(const, 3)
            nc.gpsimd.affine_select(out=mask[:, :], in_=mask[:, :], compare_op=ALU.is_ge, fill=MASKED,
                                    base=0, pattern=[[-1, P]], channel_multiplier=1).then_inc(const, 1)
            nc.gpsimd.memset(f32(k2[:, 0, :, :, :, :]), 0.0).then_inc(const, 1)
            nc.gpsimd.memset(f32(k2[:, 1, :, :, :, :]), 0.0).then_inc(const, 1)
            nc.gpsimd.memset(expo[:, :], -0.5).then_inc(const, 1)
            pool.wait_ge(lam_step, 5)
            nc.gpsimd.partition_broadcast(coef[:, :, :].rearrange("p h s -> p (h s)"),
                                          coef_row[:, :, :].rearrange("p h s -> p (h s)"), P).then_inc(coef_ready, 1)
            pool.wait_ge(const, 7)

            def batch(b, front, back, out):
                for n in range(KB):
                    x = lagged(n, 1, front, back)
                    if x:
                        db, m = x
                        r = m % RING
                        pool.wait_ge(cf_step, b * (2 * KB) + (2 * KB * db + 2 * m + 2))
                        nc.gpsimd.tensor_tensor(
                            sm[:, r, :, :], sm[:, r, :, :],
                            cf[:, r, :].rearrange("p (j o) -> p j o", o=1).broadcast_to([P, HG, P]),
                            ALU.mult).then_inc(mul_done, 1)
                    if back and n == 5:
                        pool.wait_ge(o_step, b * O_STEPS + (3 - O_STEPS))
                        nc.gpsimd.tensor_tensor(root[:, :], ms[:, :], expo[:, :], ALU.pow).then_inc(root_done, 1)
                    for i in range(2 if back and n == KB - 1 else 0):
                        if i == 0:
                            pool.wait_ge(o_step, b * O_STEPS)
                        if out:
                            pool.wait_ge(w_full, b * 2 + (W_UNITS + i + 1 - 4))
                        nc.gpsimd.tensor_tensor(
                            on[:, i * 512:(i + 1) * 512].rearrange("p (h d) -> p h d", d=2 * HD),
                            o_sb[:, i * 512:(i + 1) * 512].rearrange("p (h d) -> p h d", d=2 * HD),
                            nt[:, i * 8:(i + 1) * 8].rearrange("p (h o) -> p h o", o=1).broadcast_to([P, 8, 2 * HD]),
                            ALU.mult).then_inc(on_done, 1)

            batches(pool, batch)

        @block.tensor
        def _(pe):
            pe.wait_ge(const, 2)
            pe.wait_ge(w_in, 16)
            for k in range(KB):
                if k >= 4:
                    pe.wait_ge(w_lo, k - 3)
                for o in range(KD):
                    last = nc.tensor.transpose(psS[k % 4][:, o * P:(o + 1) * P], wn[:, o, k * P:(k + 1) * P],
                                               ident[:, :])
                last.then_inc(w_full, 1)
            pe.wait_ge(w_lo, W_UNITS)
            pe.wait_ge(lam_step, 8)

            def batch(b, front, back, out):
                for n in range(KB):
                    if front:
                        reached(pe, exp_done, b * KB + (n + 1 - RING))
                        nc.tensor.matmul(psS[n % RING][:, :], ident_b[:, :], mask_b[:, :, :], start=True, stop=False)
                        if n % HALF == 0:
                            pe.wait_ge(qk_in[n // HALF], b * (16 * 5) + 16 * 5)
                        product(nc, psS[n % RING][:, :], [q2[:, n // HALF, n % HALF, i, :] for i in range(2)],
                                [k2[:, n // HALF, n % HALF, i, :, :] for i in range(2)],
                                False, True).then_inc(s_full, 1)
                    x = lagged(n, LAG_T, front, back)
                    if x:
                        db, m = x
                        pe.wait_ge(a_done, b * KB + (KB * db + m + 1))
                        reached(pe, aT_done, b * KB + (KB * db + m))
                        for i in range(2):
                            last = nc.tensor.transpose(psA[:, i, :], at[:, m % RING, i, :], ident[:, :])
                        last.then_inc(a_full, 1)
                    x = lagged(n, LAG_PV, front, back)
                    if x:
                        db, m = x
                        pe.wait_ge(aT_done, b * KB + (KB * db + m + 1))
                        if m % HALF == 0:
                            reached(pe, o_copied, b * 2 + (2 * db + m // HALF - 1))
                        for i in range(2):
                            c = (m % HALF) * P + i * 2 * HD
                            last = nc.tensor.matmul(psO[m // HALF][:, c:c + 2 * HD], aT[:, m % 2, i, :],
                                                    v2[:, b + db, m * P + i * 2 * HD:m * P + (i + 1) * 2 * HD],
                                                    start=True, stop=True)
                        last.then_inc(pv_done, 1)
                    if out and n in (0, 2):
                        i = n // 2
                        pe.wait_ge(on_done, b * 2 + (i + 1 - 4))
                        if n == 0:
                            reached(pe, x_done, b - 2)
                        else:
                            pe.wait_ge(w_lo, b * 2 + (W_UNITS + 1 - 4))
                        for j in range(4):
                            last = nc.tensor.transpose(psW[:, j * P:(j + 1) * P],
                                                       on[:, (4 * i + j) * P:(4 * i + j + 1) * P], ident[:, :])
                        last.then_inc(w_full, 1)
                    if out and Y_FIRST <= n < Y_FIRST + Y_STEPS:
                        if n == Y_FIRST:
                            pe.wait_ge(w_lo, b * 2 + (W_UNITS + 2 - 4))
                        for k in range((n - Y_FIRST) * KB // Y_STEPS, (n - Y_FIRST + 1) * KB // Y_STEPS):
                            last = product(nc, psW[:, :], [a[:, k, :] for a in oT], [a[:, k, :] for a in woT],
                                           k == 0, k == KB - 1)
                        if n == Y_FIRST + Y_STEPS - 1:
                            last.then_inc(y_full, 1)

            batches(pe, batch)

        @block.scalar
        def _(act):
            act.wait_ge(lam_step, 2)
            nc.scalar.activation(lam_e[:, :, :], lam_s[:, :, :], ACT.Exp).then_inc(lam_exp, 1)
            for k in range(KB):
                act.wait_ge(w_full, k + 1)
                nc.scalar.activation(woT[0][:, k, :], psS[k % 4][:, :], ACT.Copy).then_inc(w_hi, 1)
            act.wait_ge(lam_step, 6)

            def batch(b, front, back, out):
                for n in range(KB):
                    if out and n in (1, 3):
                        i = n // 2
                        act.wait_ge(w_full, b * 2 + (W_UNITS + i + 1 - 4))
                        reached(act, y_full, b - 2)
                        nc.scalar.activation(oT[0][:, 4 * i:4 * i + 4, :].rearrange("p k t -> p (k t)"), psW[:, :],
                                             ACT.Copy, scale=rs[:, 0:1]).then_inc(w_hi, 1)
                    x = lagged(n, LAG_T, front, back)
                    if x:
                        db, m = x
                        act.wait_ge(a_full, b * KB + (KB * db + m + 1))
                        reached(act, pv_done, b * KB + (KB * db + m - 1))
                        nc.scalar.activation(aT[:, m % 2, :, :], psA[:, :, :], ACT.Copy).then_inc(aT_done, 1)
                    if front:
                        act.wait_ge(top_step, b * (2 * KB) + (2 * n + 2))
                        reached(act, a_done, b * KB + (n + 1 - RING))
                        for j in range(HG):
                            last = nc.scalar.activation(sm[:, n % RING, j, :], psS[n % RING][:, j * P:(j + 1) * P],
                                                        ACT.Exp, bias=ntop[:, n % RING, j:j + 1], scale=SCALE,
                                                        accum_out=sums[:, n % RING, j:j + 1])
                        last.then_inc(exp_done, 1)
                    if back and n in (1, 4):
                        i = n // 4
                        part = slice(i * 512, (i + 1) * 512)
                        act.wait_ge(pv_done, b * KB + (HALF * (i + 1) - KB))
                        reached(act, on_done, b * 2 + (i + 1 - 4))
                        nc.scalar.activation(o_sb[:, part], psO[i][:, :], ACT.Copy)
                        nc.scalar.activation(sq[:, part], psO[i][:, :], ACT.Square).then_inc(o_copied, 1)

            batches(act, batch)

        @block.vector
        def _(dve):
            dve.wait_ge(lam_in, 16 * 6)
            nc.vector.tensor_tensor(lam_p[:, :, :], lam_in_sb[:, 0:2, :], lam_in_sb[:, 2:4, :],
                                    ALU.mult).then_inc(lam_step, 1)
            dve.wait_ge(lam_step, 1)
            nc.vector.tensor_reduce(lam_s[:, :, :], lam_p[:, :, :].rearrange("p i (h d) -> p i h d", d=HD),
                                    AX.X, ALU.add).then_inc(lam_step, 1)
            dve.wait_ge(lam_exp, 1)
            nc.vector.tensor_tensor(lam_d[:, :], lam_e[:, 1, :], lam_e[:, 0, :], ALU.subtract).then_inc(lam_step, 1)
            nc.vector.memset(coef_row[:, :, 0:1], 1.0).then_inc(lam_step, 1)
            dve.wait_ge(lam_step, 3)
            nc.vector.tensor_scalar(coef_row[:, :, 1], lam_d[:, :], -LAMBDA_INIT, None, ALU.add).then_inc(lam_step, 1)
            nc.vector.tensor_scalar(rs[:, :], rs[:, :], 1.0 - LAMBDA_INIT, None, ALU.mult).then_inc(lam_step, 1)
            dve.wait_ge(const, 4)
            nc.vector.tensor_copy(ident_b[:, :], ident[:, :]).then_inc(lam_step, 1)
            nc.vector.tensor_copy(mask_b[:, :, :], mask[:, :].rearrange("p (o n) -> p o n", o=1)
                                  .broadcast_to([P, HG, P])).then_inc(lam_step, 1)
            for k in range(KB):
                dve.wait_ge(w_hi, k + 1)
                nc.vector.tensor_tensor(woT[1][:, k, :], psS[k % 4][:, :], f32(woT[0][:, k, :]),
                                        ALU.subtract).then_inc(w_lo, 1)
            dve.wait_ge(coef_ready, 1)
            dve.wait_ge(lam_step, 6)

            def batch(b, front, back, out):
                for n in range(KB):
                    if front:
                        r = n % RING
                        dve.wait_ge(s_full, b * KB + (n + 1))
                        nc.vector.tensor_reduce(top[:, r, :], psS[r][:, :].rearrange("p (j k) -> p j k", j=HG),
                                                AX.X, ALU.max).then_inc(top_step, 1)
                        dve.wait_ge(top_step, b * (2 * KB) + (2 * n + 1))
                        nc.vector.tensor_scalar(ntop[:, r, :], top[:, r, :], -SCALE, None,
                                                ALU.mult).then_inc(top_step, 1)
                    x = lagged(n, 1, front, back)
                    if x:
                        db, m = x
                        r = m % RING
                        dve.wait_ge(exp_done, b * KB + (KB * db + m + 1))
                        nc.vector.reciprocal(rsum[:, r, :], sums[:, r, :]).then_inc(cf_step, 1)
                        dve.wait_ge(cf_step, b * (2 * KB) + (2 * KB * db + 2 * m + 1))
                        nc.vector.tensor_tensor(cf[:, r, :], rsum[:, r, :],
                                                coef[:, 2 * m:2 * m + 2, :].rearrange("p h s -> p (h s)"),
                                                ALU.mult).then_inc(cf_step, 1)
                    x = lagged(n, LAG_ADD, front, back)
                    if x:
                        db, m = x
                        r = m % RING
                        dve.wait_ge(mul_done, b * KB + (KB * db + m + 1))
                        reached(dve, a_full, b * KB + (KB * db + m + 1 - RING))
                        nc.vector.tensor_tensor(at[:, r, :, :], sm[:, r, 0:HG:2, :], sm[:, r, 1:HG:2, :],
                                                ALU.add).then_inc(a_done, 1)
                    if out and n in (1, 3):
                        i = n // 2
                        dve.wait_ge(w_hi, b * 2 + (W_UNITS + i + 1 - 4))
                        nc.vector.scalar_tensor_tensor(
                            out=oT[1][:, 4 * i:4 * i + 4, :].rearrange("p k t -> p (k t)"), in0=psW[:, :],
                            scalar=rs[:, 0:1], in1=f32(oT[0][:, 4 * i:4 * i + 4, :]).rearrange("p k t -> p (k t)"),
                            op0=ALU.mult, op1=ALU.subtract).then_inc(w_lo, 1)
                    o0 = b * O_STEPS
                    if back and n in (3, 5):
                        i = n // 4
                        dve.wait_ge(o_copied, b * 2 + (i + 1 - 2))
                        nc.vector.tensor_reduce(ms[:, i * 8:(i + 1) * 8], sq[:, i * 512:(i + 1) * 512]
                                                .rearrange("p (h d) -> p h d", d=2 * HD), AX.X,
                                                ALU.add).then_inc(o_step, 1)
                    if back and n == 5:
                        dve.wait_ge(o_step, o0 + (2 - O_STEPS))
                        nc.vector.tensor_scalar(ms[:, :], ms[:, :], 1.0 / (2 * HD), EPS, ALU.mult,
                                                ALU.add).then_inc(o_step, 1)
                    if out and n == Y_FIRST + Y_STEPS:
                        dve.wait_ge(y_full, b - 1)
                        nc.vector.tensor_tensor(x1[:, b - 2, :], psW[:, :], x1[:, b - 2, :], ALU.add).then_inc(x_done, 1)
                        dve.wait_ge(x_done, b - 1)
                        norm.tile_stats(x1, b - 2)
                    if back and n == 6:
                        dve.wait_ge(root_done, b)
                        nc.vector.tensor_tensor(nt[:, :], root[:, :], root[:, :], ALU.mult).then_inc(o_step, 1)
                        dve.wait_ge(o_step, o0 + (4 - O_STEPS))
                        nc.vector.scalar_tensor_tensor(out=nt[:, :], in0=nt[:, :], scalar=-0.5, in1=ms[:, :],
                                                       op0=ALU.mult, op1=ALU.mult).then_inc(o_step, 1)
                        dve.wait_ge(o_step, o0 + (5 - O_STEPS))
                        nc.vector.scalar_tensor_tensor(out=nt[:, :], in0=nt[:, :], scalar=1.5, in1=root[:, :],
                                                       op0=ALU.add, op1=ALU.mult).then_inc(o_step, 1)

            batches(dve, batch)


def experts(nc, w, x2, out, norm):
    with ExitStack() as ctx:
        def sb(name, shape, dt=F32):
            return ctx.enter_context(nc.sbuf_tensor(name, shape, dt))

        def sem(name):
            return ctx.enter_context(nc.semaphore(name))

        ident = sb("f_ident", [P, P])
        xn = sb("f_xn", [P, B, D])
        xT = [sb(f"f_xT{i}", [P, KD, TOK], F32R) for i in range(2)]
        gw = sb("f_gw", [P, KD, NE])
        gws = [sb(f"f_gws{i}", [P, KD, NE], F32R) for i in range(2)]
        gb_row = sb("f_gb_row", [1, NE])
        gb = sb("f_gb", [P, NE])
        zT = sb("f_zT", [NE, TOK])
        z = sb("f_z", [P, B, NE])
        sel = sb("f_sel", [P, B, NE])
        r1 = sb("f_r1", [P, B])
        r2 = sb("f_r2", [P, B])
        gate = sb("f_gate", [P, NE, B])
        gateT = sb("f_gateT", [NE, TOK])
        eb = sb("f_eb", [NE, D])
        wn = sb("f_w", [P, 2, KD, D])
        ws = [sb(f"f_ws{i}", [P, 2, KD, D], F32R) for i in range(2)]
        bank = [ctx.enter_context(nc.psum_tensor(f"f_ps{i}", [P, 512], F32)) for i in range(6)]
        psG = ctx.enter_context(nc.psum_tensor("f_psG", [P, 512], F32))
        const = sem("f_const")
        s_in = sem("f_small_in")
        w_in = [sem(f"f_w_in{i}") for i in range(2)]
        gb_ready = sem("f_gb_ready")
        normed = sem("f_normed")
        x_full = sem("f_x_full")
        x_hi = sem("f_x_hi")
        x_lo = sem("f_x_lo")
        gw_hi = sem("f_gw_hi")
        gw_lo = sem("f_gw_lo")
        zT_full = sem("f_zT_full")
        zT_done = sem("f_zT_done")
        z_full = sem("f_z_full")
        z_step = sem("f_z_step")
        z_exp = sem("f_z_exp")
        t_full = sem("f_t_full")
        t_done = sem("f_t_done")
        y_full = sem("f_y_full")
        y_done = sem("f_y_done")
        w_hi = sem("f_w_hi")
        w_lo = sem("f_w_lo")
        out_sem = sem("f_out")
        Z_STEPS = 12
        NBANK = len(bank)
        assert B * NE % 2 == 0
        block = ctx.enter_context(nc.Block())

        @block.sync
        def _(sp):
            def load_expert(i, r):
                sp.wait_ge(w_lo, i * 2 + r + 1)
                sp.dma_start(wn[:, r, :, :], w["expert_w"][i * 2 + r].rearrange("(k p) d -> p k d", p=P)
                             ).then_inc(w_in[r], 16)

            load_expert(0, 0)
            with nc.allow_non_contiguous_dma(reason="the gate's weights, 16 KB"):
                sp.dma_start(gw[:, :, :], w["gate_w"].rearrange("(k p) e -> p k e", p=P)).then_inc(s_in, 16)
            sp.dma_start(gb_row[:, :], w["gate_b"].rearrange("(a e) -> a e", a=1)).then_inc(s_in, 16)
            sp.dma_start(eb[:, :], w["expert_b"]).then_inc(s_in, 16)
            load_expert(0, 1)
            with sp.Fori(1, NE // 2) as i:
                for r in range(2):
                    load_expert(i, r)
            for t in range(B):
                sp.wait_ge(y_done, (1 + NE) * B + t + 1)
                sp.dma_start(out[t], x2[:, t, :]).then_inc(out_sem, 16)
            sp.wait_ge(out_sem, 16 * B)

        @block.gpsimd
        def _(pool):
            pool.sem_inc(w_lo, 2)
            make_identity(nc, pool, ident, const)
            pool.wait_ge(s_in, 48)
            nc.gpsimd.partition_broadcast(gb[:, :], gb_row[:, :], P).then_inc(gb_ready, 1)
            with pool.Fori(0, NE // 2) as i:
                for r in range(2):
                    pool.wait_ge(w_hi, i * 2 + (r + 1))
                    nc.gpsimd.tensor_tensor(ws[1][:, r, :, :], wn[:, r, :, :], f32(ws[0][:, r, :, :]),
                                            ALU.subtract).then_inc(w_lo, 1)

        @block.tensor
        def _(pe):
            pe.wait_ge(const, 2)
            u = 0
            for half in range(2):
                pe.wait_ge(normed, 4 * half + 4)
                u = transpose_units(nc, pe, bank, ident[:, :], xn[:, 4 * half:4 * half + 4, :], 4, u, x_full, x_lo)
            pe.wait_ge(x_lo, 8)
            pe.wait_ge(gw_lo, 1)
            for half in range(2):
                for k in range(KD):
                    last = product(nc, bank[2 + half][0:NE, :], [a[:, k, :] for a in gws],
                                   [a[:, k, half * 512:(half + 1) * 512] for a in xT], k == 0, k == KD - 1)
                last.then_inc(zT_full, 1)
            pe.wait_ge(zT_done, 2)
            for t in range(B):
                last = nc.tensor.transpose(psG[:, t * NE:(t + 1) * NE], zT[:, t * P:(t + 1) * P], ident[0:NE, 0:NE])
            last.then_inc(z_full, 1)
            with pe.Fori(0, NE // 2) as i:
                for r in range(2):
                    pe.wait_ge(w_lo, i * 2 + (r + 1 + 2))
                    for t in range(B):
                        n = r * B + t
                        pe.wait_ge(y_done, i * (2 * B) + (B + n - 4 + 1))
                        for k in range(KD):
                            last = product(nc, bank[n % 4][:, :], [a[:, k, t * P:(t + 1) * P] for a in xT],
                                           [a[:, r, k, :] for a in ws], k == 0, k == KD - 1)
                        last.then_inc(y_full, 1)
            for half in range(2):
                for t in range(4):
                    last = nc.tensor.transpose(bank[4 + half][0:NE, t * P:(t + 1) * P], gate[:, :, 4 * half + t],
                                               ident[:, :])
                last.then_inc(t_full, 1)
            for t in range(B):
                pe.wait_ge(y_done, (NE + 1) * B + t - 4 + 1)
                pe.wait_ge(t_done, t // 4 + 1)
                nc.tensor.matmul(bank[t % 4][:, :], gateT[:, t * P:(t + 1) * P], eb[:, :],
                                 start=True, stop=True).then_inc(y_full, 1)

        @block.scalar
        def _(act):
            norm.scalar(act)
            def weights_hi(i, r):
                act.wait_ge(w_in[r], i * 16 + 16)
                act.wait_ge(y_full, i * (2 * B) + (r + 1) * B)
                nc.scalar.activation(ws[0][:, r, :, :].rearrange("p k d -> p (k d)"),
                                     wn[:, r, :, :].rearrange("p k d -> p (k d)"), ACT.Copy).then_inc(w_hi, 1)

            act.wait_ge(s_in, 48)
            nc.scalar.activation(gws[0][:, :, :], gw[:, :, :], ACT.Copy).then_inc(gw_hi, 1)
            for u in range(8):
                if u == 4:
                    weights_hi(0, 0)
                act.wait_ge(x_full, u + 1)
                half, k = u // 4, u % 4
                nc.scalar.activation(xT[0][:, k, half * 512:(half + 1) * 512], bank[u % NBANK][:, :],
                                     ACT.Copy).then_inc(x_hi, 1)
            for half in range(2):
                act.wait_ge(zT_full, half + 1)
                nc.scalar.activation(zT[:, half * 512:(half + 1) * 512], bank[2 + half][0:NE, :],
                                     ACT.Copy).then_inc(zT_done, 1)
            act.wait_ge(z_step, 3)
            nc.scalar.activation(z[:, :, :], z[:, :, :], ACT.Exp).then_inc(z_exp, 1)
            weights_hi(0, 1)
            with act.Fori(1, NE // 2) as i:
                for r in range(2):
                    weights_hi(i, r)
            for half in range(2):
                act.wait_ge(t_full, half + 1)
                nc.scalar.activation(gateT[:, half * 512:(half + 1) * 512], bank[4 + half][0:NE, :],
                                     ACT.Copy).then_inc(t_done, 1)

        @block.vector
        def _(dve):
            dve.sem_inc(y_full, 2 * B)
            dve.sem_inc(y_done, B)
            norm.vector(dve)
            dve.wait_ge(norm.step, norm.STEPS)
            for t in range(B):
                norm.apply(x2[:, t, :], xn[:, t, :], t).then_inc(normed, 1)
            dve.wait_ge(gw_hi, 1)
            nc.vector.tensor_tensor(gws[1][:, :, :], gw[:, :, :], f32(gws[0][:, :, :]),
                                    ALU.subtract).then_inc(gw_lo, 1)
            for u in range(8):
                dve.wait_ge(x_hi, u + 1)
                half, k = u // 4, u % 4
                part = slice(half * 512, (half + 1) * 512)
                nc.vector.tensor_tensor(xT[1][:, k, part], bank[u % NBANK][:, :], f32(xT[0][:, k, part]),
                                        ALU.subtract).then_inc(x_lo, 1)

            def over_experts(row):
                return row[:, :].rearrange("p (t o) -> p t o", o=1).broadcast_to([P, B, NE])

            dve.wait_ge(z_full, 1)
            dve.wait_ge(gb_ready, 1)
            nc.vector.tensor_tensor(z[:, :, :], psG[:, 0:B * NE].rearrange("p (t e) -> p t e", t=B),
                                    gb[:, :].rearrange("p (o e) -> p o e", o=1).broadcast_to([P, B, NE]),
                                    ALU.add).then_inc(z_step, 1)
            dve.wait_ge(z_step, 1)
            nc.vector.tensor_reduce(r1[:, :], z[:, :, :], AX.X, ALU.max).then_inc(z_step, 1)
            dve.wait_ge(z_step, 2)
            nc.vector.tensor_tensor(z[:, :, :], z[:, :, :], over_experts(r1), ALU.subtract).then_inc(z_step, 1)
            dve.wait_ge(z_exp, 1)
            nc.vector.tensor_reduce(r1[:, :], z[:, :, :], AX.X, ALU.add).then_inc(z_step, 1)
            dve.wait_ge(z_step, 4)
            nc.vector.reciprocal(r2[:, :], r1[:, :]).then_inc(z_step, 1)
            dve.wait_ge(z_step, 5)
            nc.vector.tensor_tensor(z[:, :, :], z[:, :, :], over_experts(r2), ALU.mult).then_inc(z_step, 1)
            dve.wait_ge(z_step, 6)
            nc.vector.scalar_tensor_tensor(out=sel[:, :, :], in0=z[:, :, :], scalar=THRESHOLD, in1=z[:, :, :],
                                           op0=ALU.is_ge, op1=ALU.mult).then_inc(z_step, 1)
            dve.wait_ge(z_step, 7)
            nc.vector.tensor_reduce(r1[:, :], sel[:, :, :], AX.X, ALU.add).then_inc(z_step, 1)
            dve.wait_ge(z_step, 8)
            nc.vector.tensor_scalar(r2[:, :], r1[:, :], 0.0, None, ALU.is_equal).then_inc(z_step, 1)
            dve.wait_ge(z_step, 9)
            nc.vector.tensor_tensor(r2[:, :], r2[:, :], r1[:, :], ALU.add).then_inc(z_step, 1)
            dve.wait_ge(z_step, 10)
            nc.vector.reciprocal(r1[:, :], r2[:, :]).then_inc(z_step, 1)
            dve.wait_ge(z_step, 11)
            nc.vector.tensor_tensor(gate[:, :, :].rearrange("p e t -> p t e"), sel[:, :, :], over_experts(r1),
                                    ALU.mult).then_inc(z_step, 1)
            dve.wait_ge(z_step, Z_STEPS)
            with dve.Fori(0, NE // 2) as i:
                for r in range(2):
                    for t in range(B):
                        n = r * B + t
                        dve.wait_ge(y_full, i * (2 * B) + (2 * B + n + 1))
                        dve.wait_ge(y_done, i * (2 * B) + (n + 1))
                        nc.vector.scalar_tensor_tensor(out=x2[:, t, :], in0=bank[n % 4][:, :],
                                                       scalar=gate[:, i * 2 + r, t:t + 1], in1=x2[:, t, :],
                                                       op0=ALU.mult, op1=ALU.add).then_inc(y_done, 1)
            for t in range(B):
                dve.wait_ge(y_full, (2 + NE) * B + t + 1)
                dve.wait_ge(y_done, NE * B + t + 1)
                nc.vector.tensor_tensor(x2[:, t, :], bank[t % 4][:, :], x2[:, t, :], ALU.add).then_inc(y_done, 1)


def perceiver_layer(nc, x, ctx_in, wx, wa, wf, out):
    q_d = nc.dram_tensor("q_scratch", [G, B, P, 2, P], F32R).ap()
    o_d = nc.dram_tensor("o_scratch", [G, B, P, P], F32).ap()
    q2_d = nc.dram_tensor("q2_scratch", [B, 2, P, KB // 2, 2, P], F32R).ap()
    k2_d = nc.dram_tensor("k2_scratch", [B, 2, P, KB // 2, 2, P], F32R).ap()
    with ExitStack() as ctx:
        wkT = [ctx.enter_context(nc.sbuf_tensor(f"wkT{i}", [P, KD, D], F32R)) for i in range(2)]
        wvT = [ctx.enter_context(nc.sbuf_tensor(f"wvT{i}", [P, KD, D], F32R)) for i in range(2)]
        queries_and_weights(nc, x, wx, q_d, wkT, wvT)
        cross_attention(nc, ctx_in, wx, q_d, o_d, wkT, wvT)
    with ExitStack() as ctx:
        x1 = ctx.enter_context(nc.sbuf_tensor("x1", [P, B, D], F32))
        v2 = ctx.enter_context(nc.sbuf_tensor("v2", [P, B, W2], F32))
        with ExitStack() as inner:
            x1T = [inner.enter_context(nc.sbuf_tensor(f"x1T{i}", [P, KD, TOK], F32R)) for i in range(2)]
            output_projection(nc, x, wx, o_d, x1, x1T)
            self_projections(nc, wa, x1T, q2_d, k2_d, v2)
        ffn_norm = Norm(nc, ctx, "ffn_norm")
        differential_attention(nc, wa, q2_d, k2_d, v2, x1, ffn_norm)
        experts(nc, wf, x1, out, ffn_norm)


_XATTN = ("wq", "bq", "wk", "bk", "wv", "bv", "wo", "bo")
_ATTN = ("Wq", "Wk", "Wv", "Wo", "lq1", "lk1", "lq2", "lk2", "rms_scale")
_FFN = ("gate_w", "gate_b", "expert_w", "expert_b")
_INS = (["x", "ctx_1024"] + [f"L0_xattn_{n}" for n in _XATTN] + [f"L0_attn_{n}" for n in _ATTN]
        + [f"L0_ffn_{n}" for n in _FFN])


def kernel(**inputs):
    import concourse.bacc as _bacc
    from concourse.bass_utils import run_bass_kernel_spmd as _run

    nc = _bacc.Bacc("TRN2", target_bir_lowering=False, num_devices=1)
    arrays, aps = {}, {}
    for name in _INS:
        a = np.ascontiguousarray(inputs[name])
        arrays[f"in_{name}"] = a
        aps[name] = nc.dram_tensor(f"in_{name}", a.shape, mybir.dt.from_np(a.dtype), kind="ExternalInput").ap()
    out = nc.dram_tensor("out_0", [B, P, D], F32, kind="ExternalOutput").ap()
    perceiver_layer(nc, aps["x"], aps["ctx_1024"], {n: aps[f"L0_xattn_{n}"] for n in _XATTN},
                    {n: aps[f"L0_attn_{n}"] for n in _ATTN}, {n: aps[f"L0_ffn_{n}"] for n in _FFN}, out)
    r = _run(nc, [arrays], core_ids=[0])
    return r.results[0]["out_0"]
```

```python
from contextlib import ExitStack

import numpy as np

import concourse.bass as bass
from concourse import mybir

F32 = mybir.dt.float32
F32R = mybir.dt.float32r
BF16 = mybir.dt.bfloat16
ALU = mybir.AluOpType
ACT = mybir.ActivationFunctionType
AX = mybir.AxisListType
RMAX = bass.bass_isa.ReduceOp.max

P = 128
B = 8
D = 512
KD = D // P
KV = 2048
NB = KV // P
HD = 32
G = D // P
HG = P // HD
TOK = B * P
EPS = 1e-5
SCALE = float(1.0 / np.sqrt(np.float32(HD)))
HEADS = 16
W2 = 2 * HD * HEADS
KB = W2 // P
LAMBDA_INIT = 0.8
NE = 8
THRESHOLD = 0.1
MASKED = -3.0e38



def product(nc, out, lhs, rhs, first, last):
    nc.tensor.matmul(out, lhs[0], rhs[0], start=first, stop=False)
    nc.tensor.matmul(out, lhs[0], rhs[1], start=False, stop=False)
    return nc.tensor.matmul(out, lhs[1], rhs[0], start=False, stop=last)


def f32(ap):
    return ap.bitcast(F32)


def reached(engine, sem, count):
    if not isinstance(count, int) or count > 0:
        engine.wait_ge(sem, count)


def make_identity(nc, pool, ident, step):
    nc.gpsimd.memset(ident[:, :], 0.0).then_inc(step, 1)
    pool.wait_ge(step, 1)
    nc.gpsimd.affine_select(out=ident[:, :], in_=ident[:, :], compare_op=ALU.not_equal, fill=1.0,
                            base=0, pattern=[[-1, P]], channel_multiplier=1).then_inc(step, 1)


class Shared:

    def __init__(self, nc, ctx):
        def sem(name):
            return ctx.enter_context(nc.semaphore(name))

        self.ident = ctx.enter_context(nc.sbuf_tensor("ident", [P, P], F32))
        base = nc.sbuf_base
        ctx.enter_context(nc.sbuf_tensor("arena", [P, 2 * KD * KV], F32))

        def at(start, name, *shape, dt=F32):
            return nc.alloc_sbuf_tensor_at(name, [P, *shape], dt, offset=base + 4 * start)[(slice(None),) * (len(shape) + 1)]

        QUARTER = KD * KV // 2
        assert QUARTER == B * D == KD * W2 == 2 * KD * D == KD * TOK
        self.x_sb = at(0, "x_sb", B, D)
        self.w_sb = [at(QUARTER + i * KD * D, f"w_sb{i}", KD, D) for i in range(3)]
        self.cT = [at(2 * i * QUARTER, f"cT{i}", KD, KV, dt=F32R) for i in range(2)]
        self.x1 = at(0, "x1", B, D)
        self.o_sb = at(QUARTER, "o_sb", G, B, P)
        self.wo = at(2 * QUARTER, "wo_sb", KD, D)
        self.x1T = [at((2 + i) * QUARTER, f"x1T{i}", KD, TOK, dt=F32R) for i in range(2)]
        self.Wo = at(QUARTER, "Wo_sb", KD, W2)
        self.k2 = at(2 * QUARTER, "k2_sb", 2, KB // 2, 2, HG, P, dt=F32R)
        self.experts = at(QUARTER, "experts_sb", 2, KD, D)
        self.q_out = [sem(f"q_out{i}") for i in range(2)]
        self.o_out = sem("o_out")
        self.cin_in = [sem(f"cin_in{i}") for i in range(2)]
        self.x_in = sem("x_in")
        self.wo_in = sem("wo_in")
        self.o_in = [sem(f"o_in{i}") for i in range(2)]
        self.wqk_in = [sem(f"wqk_in{i}") for i in range(2)]
        self.Wo_in = sem("Wo_in_s")
        self.expert_in = [sem(f"expert_in{i}") for i in range(2)]


class Norm:

    def __init__(self, nc, ctx, name, parts=((0, B),)):
        self.nc = nc
        self.parts = parts
        self.stats = ctx.enter_context(nc.sbuf_tensor(f"{name}_stats", [P, B, 6], F32))
        self.mv = ctx.enter_context(nc.sbuf_tensor(f"{name}_mv", [P, B, 2], F32))
        self.veps = ctx.enter_context(nc.sbuf_tensor(f"{name}_veps", [P, B], F32))
        self.root = ctx.enter_context(nc.sbuf_tensor(f"{name}_root", [P, B], F32))
        self.rstd = ctx.enter_context(nc.sbuf_tensor(f"{name}_rstd", [P, B], F32))
        self.tmp = ctx.enter_context(nc.sbuf_tensor(f"{name}_tmp", [P, B], F32))
        self.step = ctx.enter_context(nc.semaphore(f"{name}_step"))
        self.root_ready = ctx.enter_context(nc.semaphore(f"{name}_root_ready"))

    def first_step(self, part):
        return sum(2 * (t1 - t0) + 6 for t0, t1 in self.parts[:part])

    def tile_stats(self, x, t):
        self.nc.vector.bn_stats(self.stats[:, t, :], x[:, t, :]).then_inc(self.step, 1)

    def vector(self, dve, part=0):
        nc = self.nc
        t0, t1 = self.parts[part]
        cols = slice(t0, t1)
        n = self.first_step(part)
        for t in range(t0, t1):
            n += 1
            dve.wait_ge(self.step, n)
            nc.vector.bn_aggr(self.mv[:, t, :], self.stats[:, t, :]).then_inc(self.step, 1)
        n += t1 - t0
        dve.wait_ge(self.step, n)
        nc.vector.tensor_scalar(self.veps[:, cols], self.mv[:, cols, 1], EPS, None, ALU.add).then_inc(self.step, 1)
        dve.wait_ge(self.root_ready, part + 1)
        nc.vector.reciprocal(self.rstd[:, cols], self.root[:, cols]).then_inc(self.step, 1)
        dve.wait_ge(self.step, n + 2)
        nc.vector.tensor_tensor(self.tmp[:, cols], self.rstd[:, cols], self.rstd[:, cols],
                                ALU.mult).then_inc(self.step, 1)
        dve.wait_ge(self.step, n + 3)
        nc.vector.tensor_tensor(self.tmp[:, cols], self.tmp[:, cols], self.veps[:, cols],
                                ALU.mult).then_inc(self.step, 1)
        dve.wait_ge(self.step, n + 4)
        nc.vector.tensor_scalar(self.tmp[:, cols], self.tmp[:, cols], -0.5, 1.5, ALU.mult,
                                ALU.add).then_inc(self.step, 1)
        dve.wait_ge(self.step, n + 5)
        nc.vector.tensor_tensor(self.rstd[:, cols], self.rstd[:, cols], self.tmp[:, cols],
                                ALU.mult).then_inc(self.step, 1)

    def done(self, dve, part=0):
        dve.wait_ge(self.step, self.first_step(part + 1))

    def scalar(self, act, part=0):
        t0, t1 = self.parts[part]
        act.wait_ge(self.step, self.first_step(part + 1) - 5)
        self.nc.scalar.activation(self.root[:, t0:t1], self.veps[:, t0:t1], ACT.Sqrt).then_inc(self.root_ready, 1)

    def apply(self, x, out, t):
        return self.nc.vector.tensor_scalar(out, x, self.mv[:, t, 0:1], self.rstd[:, t:t + 1],
                                            ALU.subtract, ALU.mult)


def queries_and_weights(nc, x, ctx_in, w, q_d, wkT, wvT, cin, shared):
    with ExitStack() as ctx:
        def sb(name, shape, dt=F32):
            return ctx.enter_context(nc.sbuf_tensor(name, shape, dt))

        def sem(name):
            return ctx.enter_context(nc.semaphore(name))

        ident, x_sb, w_sb = shared.ident, shared.x_sb, shared.w_sb
        xn = sb("a_xn", [P, B, D])
        bq = sb("a_bq", [P, KD])
        wqT = [sb(f"a_wqT{i}", [P, KD, D], F32R) for i in range(2)]
        xT = [sb(f"a_xT{i}", [P, KD, TOK], F32R) for i in range(2)]
        q_st = sb("a_q", [P, 2, 2, TOK], F32R)
        bank = [ctx.enter_context(nc.psum_tensor(f"a_ps{i}", [P, 512], F32)) for i in range(4)]
        norm = Norm(nc, ctx, "a_norm")
        const = sem("a_const")
        x_in = [sem(f"a_x_in{i}") for i in range(2)]
        b_in = sem("a_b_in")
        w_in = [sem(f"a_w_in{i}") for i in range(3)]
        full = sem("a_full")
        hi_done = sem("a_hi")
        lo_done = sem("a_lo")
        normed = sem("a_normed")
        q_out = shared.q_out
        weights = ((w["wk"], wkT), (w["wv"], wvT), (w["wq"], wqT))
        order = ([("w", 2, k) for k in range(KD)] + [("x", half, k) for half in range(2) for k in range(KD)]
                 + [u for n in range(2 * G) for u in (("q", n // 2, n % 2), ("w", n // KD, n % KD))])
        place = {u: i for i, u in enumerate(order)}
        RING = len(bank)
        block = ctx.enter_context(nc.Block())

        @block.sync
        def _(sp):
            for i in range(2):
                part = slice(i * (B // 2), (i + 1) * (B // 2))
                sp.dma_start(x_sb[:, part, :], x[part].rearrange("b p d -> p b d")).then_inc(x_in[i], 16)
            with nc.allow_non_contiguous_dma(reason="512 numbers"):
                sp.dma_start(bq[:, :], w["bq"].rearrange("(g p) -> p g", p=P)).then_inc(b_in, 16)
            for i in (2, 0, 1):
                sp.dma_start(w_sb[i], weights[i][0].rearrange("(o p) d -> p o d", p=P)).then_inc(w_in[i], 16)
            for c in range(2):
                sp.dma_start(cin[:, c, :, :], ctx_in[0, c * 2 * P:(c + 1) * 2 * P, :]
                             .rearrange("(o p) d -> p o d", p=P)).then_inc(shared.cin_in[c], 16)
            for g in range(G):
                sp.wait_ge(lo_done, place["q", g, 1] + 1)
                for i in range(2):
                    sp.dma_start(f32(q_d[g, :, :, i, :]).rearrange("b p t -> p b t"),
                                 f32(q_st[:, g % 2, i, :]).rearrange("p (b t) -> p b t", b=B)
                                 ).then_inc(q_out[g % 2], 16)
        @block.gpsimd
        def _(pool):
            make_identity(nc, pool, ident, const)

        @block.tensor
        def _(pe):
            pe.wait_ge(const, 2)
            for u, (kind, i, j) in enumerate(order):
                if u >= RING:
                    pe.wait_ge(lo_done, u - RING + 1)
                out = bank[u % RING]
                if kind == "w":
                    if j == 0:
                        pe.wait_ge(w_in[i], 16)
                    for o in range(KD):
                        last = nc.tensor.transpose(out[:, o * P:(o + 1) * P], w_sb[i][:, o, j * P:(j + 1) * P],
                                                   ident[:, :])
                elif kind == "x":
                    if j == 0:
                        pe.wait_ge(normed, 4 * i + 4)
                    for t in range(4):
                        last = nc.tensor.transpose(out[:, t * P:(t + 1) * P], xn[:, 4 * i + t, j * P:(j + 1) * P],
                                                   ident[:, :])
                else:
                    if (i, j) == (0, 0):
                        pe.wait_ge(lo_done, u)
                    for k in range(KD):
                        last = product(nc, out[:, :], [a[:, k, i * P:(i + 1) * P] for a in wqT],
                                       [a[:, k, j * 512:(j + 1) * 512] for a in xT], k == 0, k == KD - 1)
                last.then_inc(full, 1)

        def to(u):
            kind, i, j = u
            if kind == "w":
                return [a[:, j, :] for a in weights[i][1]]
            if kind == "x":
                return [a[:, j, i * 512:(i + 1) * 512] for a in xT]
            return [q_st[:, i % 2, n, j * 512:(j + 1) * 512] for n in range(2)]

        @block.scalar
        def _(act):
            norm.scalar(act)
            act.wait_ge(b_in, 16)
            for u, unit in enumerate(order):
                kind, g, _ = unit
                act.wait_ge(full, u + 1)
                if kind == "q":
                    if g >= 2:
                        act.wait_ge(q_out[g % 2], 32)
                    nc.scalar.activation(to(unit)[0], bank[u % RING][:, :], ACT.Identity,
                                         bias=bq[:, g:g + 1]).then_inc(hi_done, 1)
                else:
                    nc.scalar.activation(to(unit)[0], bank[u % RING][:, :], ACT.Copy).then_inc(hi_done, 1)

        @block.vector
        def _(dve):
            for t in range(B):
                if t % 4 == 0:
                    dve.wait_ge(x_in[t // 4], 16)
                norm.tile_stats(x_sb, t)
            norm.vector(dve)
            norm.done(dve)
            for t in range(4):
                norm.apply(x_sb[:, t, :], xn[:, t, :], t).then_inc(normed, 1)
            dve.wait_ge(b_in, 16)
            for u, unit in enumerate(order):
                kind, g, _ = unit
                if u == KD:
                    for t in range(4, B):
                        norm.apply(x_sb[:, t, :], xn[:, t, :], t).then_inc(normed, 1)
                hi, lo = to(unit)
                dve.wait_ge(hi_done, u + 1)
                if kind == "q":
                    nc.vector.scalar_tensor_tensor(out=lo, in0=bank[u % RING][:, :], scalar=bq[:, g:g + 1],
                                                   in1=f32(hi), op0=ALU.add, op1=ALU.subtract).then_inc(lo_done, 1)
                else:
                    nc.vector.tensor_tensor(lo, bank[u % RING][:, :], f32(hi), ALU.subtract).then_inc(lo_done, 1)


def cross_attention(nc, x, ctx_in, w, q_d, o_d, wkT, wvT, cin, shared):
    with ExitStack() as ctx:
        def sb(name, shape, dt=F32):
            return ctx.enter_context(nc.sbuf_tensor(name, shape, dt))

        def sem(name):
            return ctx.enter_context(nc.semaphore(name))

        CH = 2
        NCH = NB // CH
        T_UNITS = NCH * 2
        K_UNITS = KV // 512
        V_UNITS = NB
        SUMS = NB // 2 - 1
        PAIRS = NB // 2
        LAST_SUMS = 3
        QUARTERS = 4
        AHEAD = 4

        def items(text):
            return [(x[0], int(x[1:])) for x in text.split()]

        T_AT = {NB - 8 + n: n for n in range(4)}
        PLAN_T = items("T0 T1 T2 T3")
        PLAN_A = items("K0 T4 V0 T5 V1 T6 S0 S1 S2 S3")
        PLAN_B = items("T7 V2 V3 K1 V4 T8 S4 S5 V5 T9 S6 S7 V6 T10 D0 T11 V7 K2 V8 T12 S8 S9 V9 T13 S10 S11 "
                       "T14 V10 T15 V11 K3 V12 S12 S13 S14 S15 V13 V14 V15")
        PLAN = PLAN_T + PLAN_A + PLAN_B
        ACT_A = items("K0 T4 V0 T5 P0 P1 V1 T6 P2 P3 P4 P5 P6 P7 S0 S1 S2 S3")
        DVE_A = items("K0 T4 P0 P1 T5 P2 P3 T6 P4 P5 P6 P7 N0 S0 S1 S2 S3")
        KEYS_AT = [{3: 0, 4: 1, 5: 2, 7: 3}, {0: 0, 1: 1, 3: 2, 4: 3}, {0: 0, 1: 1, 3: 2, 4: 3}]

        UNIT = {x: i for i, x in enumerate(x for x in PLAN if x[0] in "TKV")}
        SPLIT = {x: i for i, x in enumerate(x for x in PLAN if x[0] in "TK")}
        assert len(SPLIT) == T_UNITS + K_UNITS and len(UNIT) == len(SPLIT) + V_UNITS
        SIDE = 2
        KEY_UNITS = (G - 1) * K_UNITS
        UNITS = len(UNIT) + KEY_UNITS
        SPLITS = len(SPLIT) + KEY_UNITS
        assert UNITS % 2 == 0

        ident, cT, cin_in = shared.ident, shared.cT, shared.cin_in
        ones = sb("b_ones", [P, HD])
        bk = sb("b_bk", [P, G])
        bv = sb("b_bv", [P, G])
        kT = [sb(f"b_kT{i}", [P, KV], F32R) for i in range(2)]
        v = sb("b_v", [P, NB, D])
        v_side = sb("b_v_side", [P, SIDE, P])
        s = sb("b_s", [P, NB, HG * P])
        qbd = sb("b_qbd", [P, 2, 2, HG, P], F32R)
        mx = sb("b_mx", [P, 2, HG * P])
        mb = sb("b_mb", [P, HG * P])
        acc = sb("b_acc", [P, 2, HG * P])
        rD = sb("b_rD", [P, P])
        oq = sb("b_oq", [P, P])
        o_st = sb("b_o", [P, 2, P])
        work = [ctx.enter_context(nc.psum_tensor(f"b_work{i}", [P, 512], F32)) for i in range(2)]
        psS = [ctx.enter_context(nc.psum_tensor(f"b_psS{i}", [P, 512], F32)) for i in range(4)]
        psO = [ctx.enter_context(nc.psum_tensor(f"b_psO{i}", [P, 512], F32)) for i in range(2)]

        const = sem("b_const")
        bias_in = sem("b_bias_in")
        q_in = [sem(f"b_q_in{i}") for i in range(2)]
        work_full = sem("b_work_full")
        hi_done = sem("b_hi_done")
        split_done = sem("b_split_done")
        v_done = sem("b_v_done")
        s_full = sem("b_s_full")
        mx_done = sem("b_mx_done")
        s_moved = sem("b_s_moved")
        fold_done = sem("b_fold_done")
        par_begun = sem("b_par_begun")
        par_done = sem("b_par_done")
        sub_done = sem("b_sub_done")
        exp_done = sem("b_exp_done")
        pv_done = sem("b_pv_done")
        sum_done = sem("b_sum_done")
        od_full = sem("b_od_full")
        rd_done = sem("b_rd_done")
        od_free = sem("b_od_free")
        o_out = shared.o_out
        o_stored = sem("b_o_stored")
        block = ctx.enter_context(nc.Block())

        def unit_full(bn, x):
            return bn * UNITS + (UNIT[x] + 1)

        def unit_split(bn, x):
            return bn * SPLITS + (SPLIT[x] + 1)

        def keys_full(b, i):
            return b * UNITS + (len(UNIT) + i + 1)

        def keys_split(b, i):
            return b * SPLITS + (len(SPLIT) + i + 1)

        @block.sync
        def _(sp):
            sp.sem_inc(o_stored, 2)
            with nc.allow_non_contiguous_dma(reason="512 numbers"):
                sp.dma_start(bk[:, :], w["bk"].rearrange("(g p) -> p g", p=P)).then_inc(bias_in, 16)
                sp.dma_start(bv[:, :], w["bv"].rearrange("(g p) -> p g", p=P)).then_inc(bias_in, 16)

            def load_context(b, c):
                sp.dma_start(cin[:, c % 2, :, :],
                             ctx_in[b, c * CH * P:(c + 1) * CH * P, :].rearrange("(o p) d -> p o d", p=P)
                             ).then_inc(cin_in[c % 2], 16)

            def load_queries(b, g):
                for j in range(HG):
                    sp.dma_start(f32(qbd[j * HD:(j + 1) * HD, g % 2, :, j, :]),
                                 f32(q_d[g, b, j * HD:(j + 1) * HD, :, :])).then_inc(q_in[g % 2], 16)

            def store_output(b, g):
                sp.wait_ge(od_free, b * G + (g + 1 + 2))
                sp.dma_start(o_d[g, b, :, :], o_st[:, g % 2, :]).then_inc(o_out, 16)
                sp.wait_ge(o_out, b * (16 * G) + 16 * (g + 1))
                sp.sem_inc(o_stored, 1)

            def rest_of_context(b, chunks):
                for c in chunks:
                    sp.wait_ge(work_full, unit_full(b, ("T", 2 * (c - 2) + 1)))
                    load_context(b, c)

            sp.wait_ge(const, 2)
            for i in range(2):
                sp.wait_ge(shared.q_out[i], 16 * 2 * (G // 2))
            load_queries(0, 0)
            load_queries(0, 1)
            rest_of_context(0, range(2, NCH))

            def batch(b, last):
                if not last:
                    sp.wait_ge(work_full, unit_full(b, ("T", T_UNITS - 1)))
                    load_context(b + 1, 0)
                    load_context(b + 1, 1)
                for g in range(G):
                    if g == G - 1 and not last:
                        rest_of_context(b + 1, (2, 3))
                    if g < G - 2 or not last:
                        sp.wait_ge(s_full, b * (G * NB) + NB * (g + 1))
                        load_queries(b + (g + 2) // G, (g + 2) % G)
                    if g >= 1:
                        store_output(b, g - 1)
                if not last:
                    rest_of_context(b + 1, range(4, NCH))
                else:
                    sp.wait_ge(work_full, keys_full(b, KEY_UNITS - 1))
                    sp.dma_start(shared.wo, w["wo"].rearrange("(o p) d -> p o d", p=P)).then_inc(shared.wo_in, 16)
                    for g in range(G):
                        sp.dma_start(shared.o_sb[:, g, 0:B - 1, :], o_d[g, 0:B - 1].rearrange("b p t -> p b t")
                                     ).then_inc(shared.o_in[0], 16)
                    sp.dma_start(shared.x1, x.rearrange("b p d -> p b d")).then_inc(shared.x_in, 16)
                    for g in range(G - 1):
                        sp.dma_start(shared.o_sb[:, g, B - 1, :], o_d[g, B - 1]).then_inc(shared.o_in[1], 16)
                if not last:
                    store_output(b, G - 1)
                else:
                    sp.wait_ge(od_free, b * G + (G + 2))
                    sp.dma_start(o_d[G - 1, b, :, :], o_st[:, (G - 1) % 2, :]).then_inc(o_out, 16)

            with sp.Fori(0, B - 1) as b:
                batch(b, False)
            batch(B - 1, True)

        @block.gpsimd
        def _(pool):
            pool.sem_inc(sum_done, SUMS)
            pool.sem_inc(par_done, 1)
            nc.gpsimd.memset(ones[:, :], 1.0).then_inc(const, 1)
            nc.gpsimd.memset(f32(qbd[:, :, :, :, :]), 0.0).then_inc(const, 1)

            def batch(b, last):
                for g in range(G):
                    pool.wait_ge(fold_done, b * G + (g + 1))
                    pool.sem_inc(par_begun, 1)
                    nc.gpsimd.partition_all_reduce(mb[:, :], mx[:, 0, :], P, RMAX).then_inc(par_done, 1)
                    for i in range(LAST_SUMS if last and g == G - 1 else SUMS):
                        pool.wait_ge(exp_done, b * (G * PAIRS) + (g * PAIRS + i + 2))
                        if i == 0:
                            pool.wait_ge(od_full, b * G + (g + 1))
                            a = s[:, 0:2, :]
                        else:
                            pool.wait_ge(sum_done, b * (G * SUMS) + (SUMS + g * SUMS + i))
                            a = acc[:, :, :]
                        nc.gpsimd.tensor_tensor(acc[:, :, :], a, s[:, 2 * i + 2:2 * i + 4, :],
                                                ALU.add).then_inc(sum_done, 1)

            with pool.Fori(0, B - 1) as b:
                batch(b, False)
            batch(B - 1, True)

        @block.tensor
        def _(pe):
            pe.sem_inc(od_full, 1)
            pe.sem_inc(pv_done, QUARTERS)
            pe.wait_ge(const, 2)

            def plan_item(bn, x):
                kind, n = x
                if kind == "S":
                    scores(bn, 0, [n])
                elif kind == "D":
                    if not isinstance(bn, int):
                        denominators(bn - 1, G - 1)
                else:
                    i = UNIT[x]
                    bank = work[i % 2]
                    before = [y for y in UNIT if UNIT[y] == i - 2]
                    if not before:
                        reached(pe, split_done, bn * SPLITS + (i - 1))
                    elif before[0][0] == "V":
                        pe.wait_ge(v_done, bn * V_UNITS + (before[0][1] + 1))
                    else:
                        pe.wait_ge(split_done, unit_split(bn, before[0]))
                    if kind == "T":
                        c, kk = n // 2, n % 2
                        if kk == 0:
                            pe.wait_ge(cin_in[c % 2], bn * (16 * NCH // 2) + 16 * (c // 2 + 1))
                        for k in range(2):
                            for o in range(CH):
                                last = nc.tensor.transpose(bank[:, (k * CH + o) * P:(k * CH + o + 1) * P],
                                                           cin[:, c % 2, o, (2 * kk + k) * P:(2 * kk + k + 1) * P],
                                                           ident[:, :])
                    elif kind == "K":
                        pe.wait_ge(split_done, unit_split(bn, ("T", 4 * n + 3)))
                        last = keys_bank(bank, 0, n)
                    else:
                        for k in range(KD):
                            last = product(nc, bank[:, :], [a[:, k, n * P:(n + 1) * P] for a in cT],
                                           [a[:, k, :] for a in wvT], k == 0, k == KD - 1)
                    last.then_inc(work_full, 1)

            def keys_bank(bank, g, c):
                for k in range(KD):
                    last = product(nc, bank[:, :], [a[:, k, g * P:(g + 1) * P] for a in wkT],
                                   [a[:, k, c * 512:(c + 1) * 512] for a in cT], k == 0, k == KD - 1)
                return last

            def keys(b, g):
                for c in range(K_UNITS):
                    i = (g - 1) * K_UNITS + c
                    if i < 2:
                        pe.wait_ge(v_done, b * V_UNITS + (V_UNITS + i - 1))
                    else:
                        pe.wait_ge(split_done, keys_split(b, i - 2))
                    keys_bank(work[i % 2], g, c).then_inc(work_full, 1)

            def scores(b, g, blocks):
                if 0 in blocks:
                    pe.wait_ge(q_in[g % 2], b * (16 * HG * 2) + 16 * HG * (g // 2 + 1))
                for t in blocks:
                    if t % 4 == 0:
                        pe.wait_ge(split_done, keys_split(b, (g - 1) * K_UNITS + t // 4) if g
                                   else unit_split(b, ("K", t // 4)))
                    pe.wait_ge(s_moved, b * (G * NB) + (g * NB + t + 1))
                    product(nc, psS[t % 4][:, :], [a[:, t * P:(t + 1) * P] for a in kT],
                            [qbd[:, g % 2, i, :, :] for i in range(2)], True, True).then_inc(s_full, 1)

            def outputs(b, g, with_sums=False):
                if g == 0:
                    pe.wait_ge(v_done, b * V_UNITS + V_UNITS)
                pe.wait_ge(od_free, b * G + (g + 1))
                for t in range(NB):
                    if t % 2 == 0:
                        pe.wait_ge(exp_done, b * (G * PAIRS) + (g * PAIRS + t // 2 + 1))
                    for j in range(HG):
                        h = slice(j * HD, (j + 1) * HD)
                        last = nc.tensor.matmul(psO[g % 2][h, 0:P], v[:, t, g * P + j * HD:g * P + (j + 1) * HD],
                                                s[:, t, j * P:(j + 1) * P], start=t == 0, stop=t == NB - 1)
                    if with_sums and t >= 2 * (LAST_SUMS + 1):
                        for j in range(HG):
                            nc.tensor.matmul(work[0][j * HD:(j + 1) * HD, P:2 * P], ones[:, :],
                                             s[:, t, j * P:(j + 1) * P], start=t == 2 * (LAST_SUMS + 1), stop=False)
                    if t % QUARTERS == QUARTERS - 1:
                        last.then_inc(pv_done, 1)
                if with_sums:
                    pe.wait_ge(sum_done, b * (G * SUMS) + (SUMS + g * SUMS + LAST_SUMS))
                    for i in range(2):
                        for j in range(HG):
                            last = nc.tensor.matmul(work[0][j * HD:(j + 1) * HD, P:2 * P], ones[:, :],
                                                    acc[:, i, j * P:(j + 1) * P], start=False, stop=i == 1)
                    last.then_inc(od_full, 1)

            def denominators(b, g):
                pe.wait_ge(sum_done, b * (G * SUMS) + (SUMS + (g + 1) * SUMS))
                for i in range(2):
                    for j in range(HG):
                        last = nc.tensor.matmul(psO[g % 2][j * HD:(j + 1) * HD, P:2 * P], ones[:, :],
                                                acc[:, i, j * P:(j + 1) * P], start=i == 0, stop=i == 1)
                last.then_inc(od_full, 1)

            def batch(b, last):
                for g in range(G):
                    if g >= 1:
                        for t in range(AHEAD, NB):
                            if g == G - 1 and t in T_AT and not last:
                                plan_item(b + 1, ("T", T_AT[t]))
                            scores(b, g, [t])
                        if g < G - 1 or last:
                            denominators(b, g - 1)
                    if g < G - 1:
                        keys(b, g + 1)
                        scores(b, g + 1, range(AHEAD))
                    elif not last:
                        for x in PLAN_A:
                            plan_item(b + 1, x)
                        denominators(b, g - 1)
                    outputs(b, g, with_sums=last and g == G - 1)
                if not last:
                    for x in PLAN_B:
                        plan_item(b + 1, x)

            for x in PLAN:
                plan_item(0, x)
            with pe.Fori(0, B - 1) as b:
                batch(b, False)
            batch(B - 1, True)

        def context_place(a, n):
            c, kk = n // 2, n % 2
            return a[:, 2 * kk:2 * kk + 2, c * CH * P:(c + 1) * CH * P]

        def two(ps):
            return ps[:, :].rearrange("p (k t) -> p k t", k=2)

        @block.scalar
        def _(act):
            act.sem_inc(s_moved, 4)

            def plan_item(bn, x):
                kind, n = x
                if kind == "S":
                    move(bn, 0, n)
                elif kind == "P":
                    exps(bn - 1, G - 1, n)
                elif kind in "TKV":
                    act.wait_ge(work_full, unit_full(bn, x))
                    bank = work[UNIT[x] % 2]
                    if kind == "T":
                        nc.scalar.activation(context_place(cT[0], n), two(bank), ACT.Copy).then_inc(hi_done, 1)
                    elif kind == "K":
                        keys_hi(0, n, bank)
                    elif n < SIDE:
                        nc.scalar.activation(v[:, n, 0:D - P], bank[:, 0:D - P], ACT.Copy)
                        nc.scalar.activation(v_side[:, n, :], bank[:, D - P:D], ACT.Copy).then_inc(v_done, 1)
                    else:
                        if n == SIDE:
                            act.wait_ge(pv_done, bn * (G * QUARTERS) + QUARTERS)
                            act.wait_ge(v_done, bn * V_UNITS + SIDE)
                            nc.scalar.activation(v[:, 0:SIDE, D - P:D], v_side[:, :, :], ACT.Copy)
                        nc.scalar.activation(v[:, n, :], bank[:, :], ACT.Copy).then_inc(v_done, 1)

            def keys_hi(g, c, bank):
                nc.scalar.activation(kT[0][:, c * 512:(c + 1) * 512], bank[:, :], ACT.Identity,
                                     bias=bk[:, g:g + 1]).then_inc(hi_done, 1)

            def move(b, g, t):
                act.wait_ge(mx_done, b * (G * NB) + (g * NB + t + 1))
                if t % QUARTERS == 0:
                    act.wait_ge(pv_done, b * (G * QUARTERS) + (g * QUARTERS + t // QUARTERS + 1))
                if t % 2 == 0:
                    act.wait_ge(sum_done, b * (G * SUMS) + (g * SUMS + max(1, t // 2)))
                nc.scalar.activation(s[:, t, :], psS[t % 4][:, :], ACT.Copy).then_inc(s_moved, 1)

            def exps(b, g, q):
                act.wait_ge(sub_done, b * (G * PAIRS) + (g * PAIRS + q + 1))
                pair = s[:, 2 * q:2 * q + 2, :]
                nc.scalar.activation(pair, pair, ACT.Exp, scale=SCALE).then_inc(exp_done, 1)

            act.wait_ge(bias_in, 32)
            for x in PLAN:
                plan_item(0, x)

            def batch(b, last):
                for g in range(G):
                    if g >= 1:
                        for t in range(NB):
                            if g == G - 1 and t in T_AT and not last:
                                plan_item(b + 1, ("T", T_AT[t]))
                            move(b, g, t)
                    if g < G - 1:
                        for q in range(PAIRS + 1):
                            if q in KEYS_AT[g]:
                                c = KEYS_AT[g][q]
                                i = g * K_UNITS + c
                                act.wait_ge(work_full, keys_full(b, i))
                                keys_hi(g + 1, c, work[i % 2])
                            if q >= 1:
                                exps(b, g, q - 1)
                    elif last:
                        for q in range(PAIRS):
                            exps(b, g, q)
                    else:
                        for x in ACT_A + PLAN_B:
                            plan_item(b + 1, x)

            with act.Fori(0, B - 1) as b:
                batch(b, False)
            batch(B - 1, True)

        @block.vector
        def _(dve):
            dve.sem_inc(od_free, 2)

            def plan_item(bn, x):
                kind, n = x
                if kind == "S":
                    maximum(bn, 0, n)
                elif kind == "P":
                    subtract(bn - 1, G - 1, n)
                elif kind == "N":
                    normalise(bn - 1, G - 2)
                elif kind == "D":
                    if not isinstance(bn, int):
                        normalise(bn - 1, G - 1)
                elif kind in "TK":
                    dve.wait_ge(hi_done, unit_split(bn, x))
                    bank = work[UNIT[x] % 2]
                    if kind == "T":
                        nc.vector.tensor_tensor(context_place(cT[1], n), two(bank), f32(context_place(cT[0], n)),
                                                ALU.subtract).then_inc(split_done, 1)
                    else:
                        keys_lo(0, n, bank)

            def keys_lo(g, c, bank):
                part = slice(c * 512, (c + 1) * 512)
                nc.vector.scalar_tensor_tensor(out=kT[1][:, part], in0=bank[:, :], scalar=bk[:, g:g + 1],
                                               in1=f32(kT[0][:, part]), op0=ALU.add,
                                               op1=ALU.subtract).then_inc(split_done, 1)

            def maximum(b, g, t):
                dve.wait_ge(s_full, b * (G * NB) + (g * NB + t + 1))
                if t < 2:
                    if t == 0:
                        dve.wait_ge(par_done, b * G + (g + 1))
                    nc.vector.tensor_copy(mx[:, t, :], psS[t % 4][:, :]).then_inc(mx_done, 1)
                else:
                    dve.wait_ge(mx_done, b * (G * NB) + (g * NB + t - 1))
                    nc.vector.tensor_tensor(mx[:, t % 2, :], psS[t % 4][:, :], mx[:, t % 2, :],
                                            ALU.max).then_inc(mx_done, 1)
                if t == NB - 1:
                    dve.wait_ge(mx_done, b * (G * NB) + (g + 1) * NB)
                    nc.vector.tensor_tensor(mx[:, 0, :], mx[:, 0, :], mx[:, 1, :], ALU.max).then_inc(fold_done, 1)

            def subtract(b, g, q):
                if q == 0:
                    dve.wait_ge(par_done, b * G + (g + 2))
                dve.wait_ge(s_moved, b * (G * NB) + (4 + g * NB + 2 * q + 2))
                pair = s[:, 2 * q:2 * q + 2, :]
                top = mb[:, :].rearrange("p (o n) -> p o n", o=1).broadcast_to([P, 2, HG * P])
                nc.vector.tensor_tensor(pair, pair, top, ALU.subtract).then_inc(sub_done, 1)

            def normalise(b, g, sums=None):
                dve.wait_ge(od_full, b * G + (g + 2))
                nc.vector.reciprocal(rD[:, :], (sums or psO[g % 2])[:, P:2 * P]).then_inc(rd_done, 1)
                dve.wait_ge(rd_done, b * (2 * G) + (2 * g + 1))
                nc.vector.tensor_tensor(oq[:, :], psO[g % 2][:, 0:P], rD[:, :], ALU.mult).then_inc(rd_done, 1)
                dve.wait_ge(rd_done, b * (2 * G) + (2 * g + 2))
                dve.wait_ge(o_stored, b * G + (g + 1))
                nc.vector.tensor_scalar(o_st[:, g % 2, :], oq[:, :], bv[:, g:g + 1], None,
                                        ALU.add).then_inc(od_free, 1)

            dve.wait_ge(bias_in, 32)
            for x in PLAN:
                plan_item(0, x)

            def batch(b, last):
                for g in range(G):
                    if g >= 1:
                        for t in range(NB):
                            maximum(b, g, t)
                            if g == G - 1 and t in T_AT and not last:
                                plan_item(b + 1, ("T", T_AT[t]))
                        if g < G - 1 or last:
                            normalise(b, g - 1)
                    if g < G - 1 or last:
                        for q in range(PAIRS):
                            if g < G - 1 and q in KEYS_AT[g]:
                                c = KEYS_AT[g][q]
                                i = g * K_UNITS + c
                                dve.wait_ge(hi_done, keys_split(b, i))
                                keys_lo(g + 1, c, work[i % 2])
                            subtract(b, g, q)
                    else:
                        for x in DVE_A + PLAN_B:
                            plan_item(b + 1, x)
                if last:
                    normalise(b, G - 1, work[0])

            with dve.Fori(0, B - 1) as b:
                batch(b, False)
            batch(B - 1, True)


def transpose_units(nc, pe, bank, ident, src, blocks, u, full, lo_done):
    for k in range(src.shape[2] // P):
        for o4 in range(blocks // 4):
            if u >= len(bank):
                pe.wait_ge(lo_done, u - len(bank) + 1)
            for o in range(4):
                last = nc.tensor.transpose(bank[u % len(bank)][:, o * P:(o + 1) * P],
                                           src[:, 4 * o4 + o, k * P:(k + 1) * P], ident)
            last.then_inc(full, 1)
            u += 1
    return u


def output_projection(nc, w, w_next, o_d, wn, shared):
    with ExitStack() as ctx:
        def sb(name, shape, dt=F32):
            return ctx.enter_context(nc.sbuf_tensor(name, shape, dt))

        def sem(name):
            return ctx.enter_context(nc.semaphore(name))

        ident, o_sb, wo, x1, x1T = shared.ident, shared.o_sb, shared.wo, shared.x1, shared.x1T
        oT = [sb(f"c_oT{i}", [P, G, TOK], F32R) for i in range(2)]
        woT = [sb(f"c_woT{i}", [P, KD, D], F32R) for i in range(2)]
        bo_row = sb("c_bo_row", [1, D])
        bo = sb("c_bo", [P, D])
        xn = sb("c_xn", [P, B, D])
        bank = [ctx.enter_context(nc.psum_tensor(f"c_ps{i}", [P, 512], F32)) for i in range(4)]
        norm = Norm(nc, ctx, "c_norm", ((0, B // 2), (B // 2, B)))
        b_in = sem("c_b_in")
        bo_ready = sem("c_bo_ready")
        full = sem("c_full")
        hi_done = sem("c_hi")
        lo_done = sem("c_lo")
        o_hi = sem("c_o_hi")
        o_lo = sem("c_o_lo")
        normed = sem("c_normed")
        U_O = KD
        U_X = U_O + B
        batches = [(slice(b0 * P, b1 * P), b0, b1, i) for b0, b1, i in ((0, 2, 0), (2, B - 1, 0), (B - 1, B, 1))]
        block = ctx.enter_context(nc.Block())

        @block.sync
        def _(sp):
            sp.wait_ge(shared.o_out, 16 * G * B)
            sp.dma_start(o_sb[:, G - 1, B - 1, :], o_d[G - 1, B - 1]).then_inc(shared.o_in[1], 16)
            sp.dma_start(bo_row[:, :], w["bo"].rearrange("(a d) -> a d", a=1)).then_inc(b_in, 16)
            for i, name in enumerate(("Wq", "Wk")):
                sp.dma_start(wn[:, i, :, :], w_next[name].rearrange("(o p) d -> p o d", p=P)
                             ).then_inc(shared.wqk_in[i], 16)

        @block.gpsimd
        def _(pool):
            pool.wait_ge(b_in, 16)
            nc.gpsimd.partition_broadcast(bo[:, :], bo_row[:, :], P).then_inc(bo_ready, 1)
            pool.wait_ge(bo_ready, 1)
            pool.wait_ge(shared.x_in, 16)
            for t in range(B):
                nc.gpsimd.tensor_tensor(x1[:, t, :], x1[:, t, :], bo[:, :], ALU.add).then_inc(bo_ready, 1)

        @block.tensor
        def _(pe):
            pe.wait_ge(shared.wo_in, 16)
            u = transpose_units(nc, pe, bank, ident[:, :], wo, KD, 0, full, lo_done)
            pe.wait_ge(lo_done, U_O)
            for t in range(B):
                for i, (_, b0, _, _) in enumerate(batches):
                    if t == b0:
                        pe.wait_ge(o_lo, (i + 1) * G)
                pe.wait_ge(lo_done, u - 3)
                for g in range(G):
                    last = product(nc, bank[u % 4][:, :], [a[:, g, t * P:(t + 1) * P] for a in oT],
                                   [a[:, g, :] for a in woT], g == 0, g == G - 1)
                last.then_inc(full, 1)
                u += 1
            for half in range(2):
                pe.wait_ge(normed, 4 * half + 4)
                u = transpose_units(nc, pe, bank, ident[:, :], xn[:, 4 * half:4 * half + 4, :], 4, u, full, lo_done)

        def places():
            for k in range(KD):
                yield k, [a[:, k, :] for a in woT]
            for half in range(2):
                for k in range(KD):
                    yield U_X + 4 * half + k, [a[:, k, half * 512:(half + 1) * 512] for a in x1T]

        @block.scalar
        def _(act):
            for n, (u, (hi, _)) in enumerate(places()):
                if u == U_X:
                    for part, b0, b1, i in batches:
                        act.wait_ge(shared.o_in[i], 16 * G)
                        for g in range(G):
                            nc.scalar.activation(oT[0][:, g, part], o_sb[:, g, b0:b1, :].rearrange("p b t -> p (b t)"),
                                                 ACT.Copy).then_inc(o_hi, 1)
                    norm.scalar(act, 0)
                act.wait_ge(full, u + 1)
                nc.scalar.activation(hi, bank[u % 4][:, :], ACT.Copy).then_inc(hi_done, 1)
                if u == U_X + 1:
                    norm.scalar(act, 1)

        @block.vector
        def _(dve):
            at = list(places())

            def lo(n):
                u, (hi, low) = at[n]
                dve.wait_ge(hi_done, n + 1)
                nc.vector.tensor_tensor(low, bank[u % 4][:, :], f32(hi), ALU.subtract).then_inc(lo_done, 1)

            for n in range(KD):
                lo(n)
            for i, (part, b0, b1, _) in enumerate(batches):
                for g in range(G):
                    dve.wait_ge(o_hi, i * G + g + 1)
                    nc.vector.tensor_tensor(oT[1][:, g, part], o_sb[:, g, b0:b1, :].rearrange("p b t -> p (b t)"),
                                            f32(oT[0][:, g, part]), ALU.subtract).then_inc(o_lo, 1)
            for t in range(B):
                dve.wait_ge(bo_ready, t + 2)
                dve.wait_ge(full, U_O + t + 1)
                nc.vector.tensor_tensor(x1[:, t, :], bank[(U_O + t) % 4][:, :], x1[:, t, :],
                                        ALU.add).then_inc(lo_done, 1)
                dve.wait_ge(lo_done, U_O + t + 1)
                norm.tile_stats(x1, t)
                if t == B // 2 - 1:
                    norm.vector(dve, 0)
                    norm.done(dve, 0)
                if t == B // 2 + 1:
                    for t2 in range(B // 2):
                        norm.apply(x1[:, t2, :], xn[:, t2, :], t2).then_inc(normed, 1)
            norm.vector(dve, 1)
            norm.done(dve, 1)
            for t in range(B // 2, B):
                norm.apply(x1[:, t, :], xn[:, t, :], t).then_inc(normed, 1)
            for n in range(KD, KD + 2 * KD):
                lo(n)


def self_projections(nc, w, q2_d, k2_d, v2, wn, shared):
    with ExitStack() as ctx:
        def sb(name, shape, dt=F32):
            return ctx.enter_context(nc.sbuf_tensor(name, shape, dt))

        def sem(name):
            return ctx.enter_context(nc.semaphore(name))

        ident, x1T = shared.ident, shared.x1T
        wT = [[sb(f"d_wT{r}{i}", [P, KD, W2], F32R) for i in range(2)] for r in range(2)]
        st = sb("d_st", [P, 2, 2, 512], F32R)
        bank = [ctx.enter_context(nc.psum_tensor(f"d_ps{i}", [P, 512], F32)) for i in range(8)]
        w_in = shared.wqk_in
        full = sem("d_full")
        hi_done = sem("d_hi")
        done = sem("d_done")
        st_out = [sem(f"d_st_out{i}") for i in range(2)]
        TU = KD * KB // 4
        PU = KB * 2
        U_QT, U_KT, U_Q, U_VT, U_K, U_V = 0, TU, 2 * TU, 2 * TU + PU, 3 * TU + PU, 3 * TU + 2 * PU
        block = ctx.enter_context(nc.Block())
        weights = (w["Wq"], w["Wk"], w["Wv"])

        @block.sync
        def _(sp):
            def load(i):
                sp.dma_start(wn[:, i % 2, :, :], weights[i].rearrange("(o p) d -> p o d", p=P)
                             ).then_inc(w_in[i % 2], 16)

            sp.dma_start(shared.Wo, w["Wo"].rearrange("(o p) d -> p o d", p=P)).then_inc(shared.Wo_in, 16)
            sp.wait_ge(full, U_KT)
            load(2)
            for n in range(2 * PU):
                u = (U_Q if n < PU else U_K - PU) + n
                blk, half = (n % PU) // 2, n % 2
                dst = (q2_d, k2_d)[n // PU]
                sp.wait_ge(done, u + 1)
                for i in range(2):
                    sp.dma_start(f32(dst[4 * half:4 * half + 4, blk // 4, :, blk % 4, i, :]).rearrange("b p t -> p b t"),
                                 f32(st[:, n % 2, i, :]).rearrange("p (b t) -> p b t", b=4)
                                 ).then_inc(st_out[n % 2], 16)
            for i in range(2):
                sp.wait_ge(st_out[i], 32 * PU)

        @block.tensor
        def _(pe):
            def weight(i, u):
                pe.wait_ge(w_in[i % 2], 16 * (i // 2 + 1))
                return transpose_units(nc, pe, bank, ident[:, :], wn[:, i % 2, :, :], KB, u, full, done)

            def heads(r, u, first):
                pe.wait_ge(done, first)
                for blk in range(KB):
                    for half in range(2):
                        pe.wait_ge(done, u - len(bank) + 1)
                        for k in range(KD):
                            last = product(nc, bank[u % 8][:, :], [a[:, k, blk * P:(blk + 1) * P] for a in wT[r]],
                                           [a[:, k, half * 512:(half + 1) * 512] for a in x1T], k == 0, k == KD - 1)
                        last.then_inc(full, 1)
                        u += 1
                return u

            u = weight(0, 0)
            u = weight(1, u)
            u = heads(0, u, U_KT)
            u = weight(2, u)
            u = heads(1, u, U_Q)
            pe.wait_ge(done, U_K)
            for t in range(B):
                for half in range(2):
                    pe.wait_ge(done, u - len(bank) + 1)
                    for k in range(KD):
                        last = product(nc, bank[u % 8][:, :], [a[:, k, t * P:(t + 1) * P] for a in x1T],
                                       [a[:, k, half * 512:(half + 1) * 512] for a in wT[0]], k == 0, k == KD - 1)
                    last.then_inc(full, 1)
                    u += 1

        def places():
            u = n = 0
            for kind, r in (("w", 0), ("w", 1), ("h", 0), ("w", 0), ("h", 1)):
                for i in range(TU if kind == "w" else PU):
                    if kind == "w":
                        yield u, None, [a[:, i // 2, (i % 2) * 512:(i % 2 + 1) * 512] for a in wT[r]]
                    else:
                        yield u, n, [st[:, n % 2, j, :] for j in range(2)]
                        n += 1
                    u += 1

        @block.scalar
        def _(act):
            for u, n, (hi, _) in places():
                act.wait_ge(full, u + 1)
                if n is not None and n >= 2:
                    act.wait_ge(st_out[n % 2], 32 * (n // 2))
                nc.scalar.activation(hi, bank[u % 8][:, :], ACT.Copy).then_inc(hi_done, 1)

        @block.vector
        def _(dve):
            for u, _, (hi, lo) in places():
                dve.wait_ge(hi_done, u + 1)
                nc.vector.tensor_tensor(lo, bank[u % 8][:, :], f32(hi), ALU.subtract).then_inc(done, 1)
            for i in range(2 * B):
                u = U_V + i
                dve.wait_ge(full, u + 1)
                nc.vector.tensor_copy(v2[:, i // 2, (i % 2) * 512:(i % 2 + 1) * 512],
                                      bank[u % 8][:, :]).then_inc(done, 1)


def differential_attention(nc, w, w_next, q2_d, k2_d, v2, shared, norm):
    with ExitStack() as ctx:
        def sb(name, shape, dt=F32):
            return ctx.enter_context(nc.sbuf_tensor(name, shape, dt))

        def sem(name):
            return ctx.enter_context(nc.semaphore(name))

        HALF = KB // 2
        RING = 4
        LAG_T, LAG_PV, LAG_ADD = 3, 4, 2
        ident, x1, wn, k2 = shared.ident, shared.x1, shared.Wo, shared.k2
        ident_b = sb("e_ident_b", [P, P], BF16)
        mask = sb("e_mask", [P, P])
        mask_b = sb("e_mask_b", [P, HG, P], BF16)
        woT = [sb(f"e_woT{i}", [P, KB, D], F32R) for i in range(2)]
        lam_in_sb = sb("e_lam_in", [1, 4, HEADS * HD])
        lam_p = sb("e_lam_p", [1, 2, HEADS * HD])
        lam_s = sb("e_lam_s", [1, 2, HEADS])
        lam_e = sb("e_lam_e", [1, 2, HEADS])
        lam_d = sb("e_lam_d", [1, HEADS])
        coef_row = sb("e_coef_row", [1, HEADS, 2])
        coef = sb("e_coef", [P, HEADS, 2])
        rs = sb("e_rs", [P, 1])
        q2 = sb("e_q2", [P, 2, HALF, 2, P], F32R)
        sm = sb("e_sm", [P, RING, HG, P])
        top = sb("e_top", [P, RING, HG])
        ntop = sb("e_ntop", [P, RING, HG])
        sums = sb("e_sums", [P, RING, HG])
        rsum = sb("e_rsum", [P, RING, HG])
        cf = sb("e_cf", [P, RING, HG])
        at = sb("e_at", [P, RING, 2, P])
        aT = sb("e_aT", [P, 2, 2, P])
        o_sb = sb("e_o", [P, W2])
        sq = sb("e_sq", [P, W2])
        ms = sb("e_ms", [P, HEADS])
        expo = sb("e_expo", [P, HEADS])
        root = sb("e_root", [P, HEADS])
        nt = sb("e_nt", [P, HEADS])
        on = sb("e_on", [P, W2])
        oT = [sb(f"e_oT{i}", [P, KB, P], F32R) for i in range(2)]
        psS = [ctx.enter_context(nc.psum_tensor(f"e_psS{i}", [P, 512], F32)) for i in range(RING)]
        psA = ctx.enter_context(nc.psum_tensor("e_psA", [P, 2, P], F32))
        psO = [ctx.enter_context(nc.psum_tensor(f"e_psO{i}", [P, 512], F32)) for i in range(2)]
        psW = ctx.enter_context(nc.psum_tensor("e_psW", [P, 512], F32))

        const = sem("e_const")
        lam_in = sem("e_lam_in_s")
        lam_step = sem("e_lam_step")
        lam_exp = sem("e_lam_exp")
        coef_ready = sem("e_coef_ready")
        qk_in = [sem(f"e_qk_in{i}") for i in range(2)]
        w_full = sem("e_w_full")
        w_hi = sem("e_w_hi")
        w_lo = sem("e_w_lo")
        s_full = sem("e_s_full")
        top_step = sem("e_top_step")
        exp_done = sem("e_exp_done")
        cf_step = sem("e_cf_step")
        mul_done = sem("e_mul_done")
        a_done = sem("e_a_done")
        a_full = sem("e_a_full")
        aT_done = sem("e_aT_done")
        pv_done = sem("e_pv_done")
        o_copied = sem("e_o_copied")
        o_step = sem("e_o_step")
        root_done = sem("e_root_done")
        on_done = sem("e_on_done")
        y_full = sem("e_y_full")
        x_done = sem("e_x_done")
        W_UNITS = KB
        O_STEPS = 6
        Y_OUT = {4: [0], 5: [1], 6: [2, 3]}
        Y_END = {0: [4, 5], 1: [6], 2: [7]}
        block = ctx.enter_context(nc.Block())

        def batches(engine, batch):
            batch(0, True, False, False, False)
            batch(1, True, True, False, False)
            batch(2, True, True, True, False)
            with engine.Fori(3, B) as b:
                batch(b, True, True, True, True)
            batch(B, False, True, True, True)
            batch(B + 1, False, False, True, True)
            batch(B + 2, False, False, False, True)

        def lagged(n, lag, front, back):
            if n >= lag:
                return (0, n - lag) if front else None
            return (-1, n - lag + KB) if back else None

        @block.sync
        def _(sp):
            for i, name in enumerate(("lq1", "lq2", "lk1", "lk2")):
                sp.dma_start(lam_in_sb[:, i, :], w[name].rearrange("(a h) d -> a (h d)", a=1)).then_inc(lam_in, 16)
            with nc.allow_non_contiguous_dma(reason="64 numbers"):
                for i in range(2):
                    sp.dma_start(rs[64 * i:64 * i + 64, :], w["rms_scale"].rearrange("(d a) -> d a", a=1)
                                 ).then_inc(lam_in, 16)
            def load(b, hf):
                sp.dma_start(f32(q2[:, hf, :, :, :]), f32(q2_d[b, hf, :, :, :, :])).then_inc(qk_in[hf], 16)
                for j in range(HG):
                    sp.dma_start(f32(k2[j * HD:(j + 1) * HD, hf, :, :, j, :]),
                                 f32(k2_d[b, hf, j * HD:(j + 1) * HD, :, :, :])).then_inc(qk_in[hf], 16)

            for hf in range(2):
                sp.wait_ge(const, hf + 1)
                load(0, hf)
            sp.wait_ge(w_full, W_UNITS)
            for r in range(2):
                sp.dma_start(shared.experts[:, r, :, :], w_next["expert_w"][r].rearrange("(k p) d -> p k d", p=P)
                             ).then_inc(shared.expert_in[r], 16)
            with sp.Fori(1, B) as b:
                for hf in range(2):
                    sp.wait_ge(s_full, b * KB + (HALF + hf * HALF - KB))
                    load(b, hf)

        @block.gpsimd
        def _(pool):
            for hf in range(2):
                nc.gpsimd.memset(f32(k2[:, hf, :, :, :, :]), 0.0).then_inc(const, 1)
            nc.gpsimd.memset(mask[:, :], 0.0).then_inc(const, 1)
            pool.wait_ge(const, 3)
            nc.gpsimd.affine_select(out=mask[:, :], in_=mask[:, :], compare_op=ALU.is_ge, fill=MASKED,
                                    base=0, pattern=[[-1, P]], channel_multiplier=1).then_inc(const, 1)
            nc.gpsimd.memset(expo[:, :], -0.5).then_inc(const, 1)
            pool.wait_ge(lam_step, 5)
            nc.gpsimd.partition_broadcast(coef[:, :, :].rearrange("p h s -> p (h s)"),
                                          coef_row[:, :, :].rearrange("p h s -> p (h s)"), P).then_inc(coef_ready, 1)
            pool.wait_ge(const, 5)

            def batch(b, front, back, out, end):
                for n in range(KB):
                    if back and n == KB - 1:
                        pool.wait_ge(o_step, b * O_STEPS)
                        normed(b, 0, out)
                    x = lagged(n, 1, front, back)
                    if x:
                        db, m = x
                        r = m % RING
                        pool.wait_ge(cf_step, b * (2 * KB) + (2 * KB * db + 2 * m + 2))
                        nc.gpsimd.tensor_tensor(
                            sm[:, r, :, :], sm[:, r, :, :],
                            cf[:, r, :].rearrange("p (j o) -> p j o", o=1).broadcast_to([P, HG, P]),
                            ALU.mult).then_inc(mul_done, 1)
                    if back and n == 5:
                        pool.wait_ge(o_step, b * O_STEPS + (3 - O_STEPS))
                        nc.gpsimd.tensor_tensor(root[:, :], ms[:, :], expo[:, :], ALU.pow).then_inc(root_done, 1)
                    if back and n == KB - 1:
                        normed(b, 1, out)

            def normed(b, i, out):
                if out:
                    pool.wait_ge(w_full, b * 2 + (W_UNITS + i + 1 - 4))
                nc.gpsimd.tensor_tensor(
                    on[:, i * 512:(i + 1) * 512].rearrange("p (h d) -> p h d", d=2 * HD),
                    o_sb[:, i * 512:(i + 1) * 512].rearrange("p (h d) -> p h d", d=2 * HD),
                    nt[:, i * 8:(i + 1) * 8].rearrange("p (h o) -> p h o", o=1).broadcast_to([P, 8, 2 * HD]),
                    ALU.mult).then_inc(on_done, 1)

            batches(pool, batch)

        @block.tensor
        def _(pe):
            pe.wait_ge(shared.Wo_in, 16)
            for k in range(KB):
                if k >= 4:
                    pe.wait_ge(w_lo, k - 3)
                for o in range(KD):
                    last = nc.tensor.transpose(psS[k % 4][:, o * P:(o + 1) * P], wn[:, o, k * P:(k + 1) * P],
                                               ident[:, :])
                last.then_inc(w_full, 1)
            pe.wait_ge(w_lo, W_UNITS)
            pe.wait_ge(lam_step, 8)

            def batch(b, front, back, out, end):
                for n in range(KB):
                    if front:
                        reached(pe, exp_done, b * KB + (n + 1 - RING))
                        nc.tensor.matmul(psS[n % RING][:, :], ident_b[:, :], mask_b[:, :, :], start=True, stop=False)
                        if n % HALF == 0:
                            pe.wait_ge(qk_in[n // HALF], b * (16 * 5) + 16 * 5)
                        product(nc, psS[n % RING][:, :], [q2[:, n // HALF, n % HALF, i, :] for i in range(2)],
                                [k2[:, n // HALF, n % HALF, i, :, :] for i in range(2)],
                                False, True).then_inc(s_full, 1)
                    x = lagged(n, LAG_T, front, back)
                    if x:
                        db, m = x
                        pe.wait_ge(a_done, b * KB + (KB * db + m + 1))
                        reached(pe, aT_done, b * KB + (KB * db + m))
                        for i in range(2):
                            last = nc.tensor.transpose(psA[:, i, :], at[:, m % RING, i, :], ident[:, :])
                        last.then_inc(a_full, 1)
                    x = lagged(n, LAG_PV, front, back)
                    if x:
                        db, m = x
                        pe.wait_ge(aT_done, b * KB + (KB * db + m + 1))
                        if m % HALF == 0:
                            reached(pe, o_copied, b * 2 + (2 * db + m // HALF - 1))
                            if out if m == 0 else end:
                                pe.wait_ge(w_lo, b * 2 + (W_UNITS + 2 * db + m // HALF + 1 - 4))
                        for i in range(2):
                            c = (m % HALF) * P + i * 2 * HD
                            last = nc.tensor.matmul(psO[m // HALF][:, c:c + 2 * HD], aT[:, m % 2, i, :],
                                                    v2[:, b + db, m * P + i * 2 * HD:m * P + (i + 1) * 2 * HD],
                                                    start=True, stop=True)
                        last.then_inc(pv_done, 1)
                    if out and n in (1, 5):
                        i = n // 4
                        pe.wait_ge(on_done, b * 2 + (i + 1 - 4))
                        if back:
                            pe.wait_ge(o_copied, b * 2 + (i + 1 - 2))
                        for j in range(4):
                            last = nc.tensor.transpose(psO[i][:, j * P:(j + 1) * P],
                                                       on[:, (4 * i + j) * P:(4 * i + j + 1) * P], ident[:, :])
                        last.then_inc(w_full, 1)
                    ks = Y_OUT.get(n, []) if out else []
                    if end:
                        ks = ks + Y_END.get(n, [])
                    for k in ks:
                        if k == 0:
                            pe.wait_ge(w_lo, b * 2 + (W_UNITS + 1 - 4))
                            reached(pe, x_done, b - 2)
                        if k == HALF:
                            pe.wait_ge(w_lo, b * 2 + (W_UNITS + 2 - 6))
                        last = product(nc, psW[:, :], [a[:, k, :] for a in oT], [a[:, k, :] for a in woT],
                                       k == 0, k == KB - 1)
                        if k in (HALF - 1, KB - 1):
                            last.then_inc(y_full, 1)

            batches(pe, batch)

        @block.scalar
        def _(act):
            for k in range(KB):
                act.wait_ge(w_full, k + 1)
                nc.scalar.activation(woT[0][:, k, :], psS[k % 4][:, :], ACT.Copy).then_inc(w_hi, 1)
            act.wait_ge(lam_step, 2)
            nc.scalar.activation(lam_e[:, :, :], lam_s[:, :, :], ACT.Exp).then_inc(lam_exp, 1)
            act.wait_ge(lam_step, 6)

            def batch(b, front, back, out, end):
                if not front and not back and out:
                    norm.scalar(act, 0)
                for n in range(KB):
                    if out and n in (2, 6):
                        i = n // 4
                        act.wait_ge(w_full, b * 2 + (W_UNITS + i + 1 - 4))
                        reached(act, y_full, b * 2 + (i + 1 - 6))
                        nc.scalar.activation(oT[0][:, 4 * i:4 * i + 4, :].rearrange("p k t -> p (k t)"), psO[i][:, :],
                                             ACT.Copy, scale=rs[:, 0:1]).then_inc(w_hi, 1)
                    x = lagged(n, LAG_T, front, back)
                    if x:
                        db, m = x
                        act.wait_ge(a_full, b * KB + (KB * db + m + 1))
                        reached(act, pv_done, b * KB + (KB * db + m - 1))
                        nc.scalar.activation(aT[:, m % 2, :, :], psA[:, :, :], ACT.Copy).then_inc(aT_done, 1)
                    if front:
                        act.wait_ge(top_step, b * (2 * KB) + (2 * n + 2))
                        reached(act, a_done, b * KB + (n + 1 - RING))
                        for j in range(HG):
                            last = nc.scalar.activation(sm[:, n % RING, j, :], psS[n % RING][:, j * P:(j + 1) * P],
                                                        ACT.Exp, bias=ntop[:, n % RING, j:j + 1], scale=SCALE,
                                                        accum_out=sums[:, n % RING, j:j + 1])
                        last.then_inc(exp_done, 1)
                    if back and n in (0, 4):
                        i = n // 4
                        part = slice(i * 512, (i + 1) * 512)
                        act.wait_ge(pv_done, b * KB + (HALF * (i + 1) - KB))
                        reached(act, on_done, b * 2 + (i + 1 - 4))
                        nc.scalar.activation(o_sb[:, part], psO[i][:, :], ACT.Copy)
                        nc.scalar.activation(sq[:, part], psO[i][:, :], ACT.Square).then_inc(o_copied, 1)

            batches(act, batch)

        @block.vector
        def _(dve):
            for k in range(KB):
                dve.wait_ge(w_hi, k + 1)
                nc.vector.tensor_tensor(woT[1][:, k, :], psS[k % 4][:, :], f32(woT[0][:, k, :]),
                                        ALU.subtract).then_inc(w_lo, 1)
            dve.wait_ge(lam_in, 16 * 6)
            nc.vector.tensor_tensor(lam_p[:, :, :], lam_in_sb[:, 0:2, :], lam_in_sb[:, 2:4, :],
                                    ALU.mult).then_inc(lam_step, 1)
            dve.wait_ge(lam_step, 1)
            nc.vector.tensor_reduce(lam_s[:, :, :], lam_p[:, :, :].rearrange("p i (h d) -> p i h d", d=HD),
                                    AX.X, ALU.add).then_inc(lam_step, 1)
            dve.wait_ge(lam_exp, 1)
            nc.vector.tensor_tensor(lam_d[:, :], lam_e[:, 1, :], lam_e[:, 0, :], ALU.subtract).then_inc(lam_step, 1)
            nc.vector.memset(coef_row[:, :, 0:1], 1.0).then_inc(lam_step, 1)
            dve.wait_ge(lam_step, 3)
            nc.vector.tensor_scalar(coef_row[:, :, 1], lam_d[:, :], -LAMBDA_INIT, None, ALU.add).then_inc(lam_step, 1)
            nc.vector.tensor_scalar(rs[:, :], rs[:, :], 1.0 - LAMBDA_INIT, None, ALU.mult).then_inc(lam_step, 1)
            dve.wait_ge(const, 4)
            nc.vector.tensor_copy(ident_b[:, :], ident[:, :]).then_inc(lam_step, 1)
            nc.vector.tensor_copy(mask_b[:, :, :], mask[:, :].rearrange("p (o n) -> p o n", o=1)
                                  .broadcast_to([P, HG, P])).then_inc(lam_step, 1)
            dve.wait_ge(coef_ready, 1)
            dve.wait_ge(lam_step, 6)

            def batch(b, front, back, out, end):
                if not front and not back and out:
                    norm.vector(dve, 0)
                for n in range(KB):
                    if front:
                        r = n % RING
                        dve.wait_ge(s_full, b * KB + (n + 1))
                        nc.vector.tensor_reduce(top[:, r, :], psS[r][:, :].rearrange("p (j k) -> p j k", j=HG),
                                                AX.X, ALU.max).then_inc(top_step, 1)
                        dve.wait_ge(top_step, b * (2 * KB) + (2 * n + 1))
                        nc.vector.tensor_scalar(ntop[:, r, :], top[:, r, :], -SCALE, None,
                                                ALU.mult).then_inc(top_step, 1)
                    x = lagged(n, 1, front, back)
                    if x:
                        db, m = x
                        r = m % RING
                        dve.wait_ge(exp_done, b * KB + (KB * db + m + 1))
                        nc.vector.reciprocal(rsum[:, r, :], sums[:, r, :]).then_inc(cf_step, 1)
                        dve.wait_ge(cf_step, b * (2 * KB) + (2 * KB * db + 2 * m + 1))
                        nc.vector.tensor_tensor(cf[:, r, :], rsum[:, r, :],
                                                coef[:, 2 * m:2 * m + 2, :].rearrange("p h s -> p (h s)"),
                                                ALU.mult).then_inc(cf_step, 1)
                    x = lagged(n, LAG_ADD, front, back)
                    if x:
                        db, m = x
                        r = m % RING
                        dve.wait_ge(mul_done, b * KB + (KB * db + m + 1))
                        reached(dve, a_full, b * KB + (KB * db + m + 1 - RING))
                        nc.vector.tensor_tensor(at[:, r, :, :], sm[:, r, 0:HG:2, :], sm[:, r, 1:HG:2, :],
                                                ALU.add).then_inc(a_done, 1)
                    if out and n in (2, 6):
                        i = n // 4
                        dve.wait_ge(w_hi, b * 2 + (W_UNITS + i + 1 - 4))
                        nc.vector.scalar_tensor_tensor(
                            out=oT[1][:, 4 * i:4 * i + 4, :].rearrange("p k t -> p (k t)"), in0=psO[i][:, :],
                            scalar=rs[:, 0:1], in1=f32(oT[0][:, 4 * i:4 * i + 4, :]).rearrange("p k t -> p (k t)"),
                            op0=ALU.mult, op1=ALU.subtract).then_inc(w_lo, 1)
                    o0 = b * O_STEPS
                    if back and n in (1, 5):
                        i = n // 4
                        dve.wait_ge(o_copied, b * 2 + (i + 1 - 2))
                        nc.vector.tensor_reduce(ms[:, i * 8:(i + 1) * 8], sq[:, i * 512:(i + 1) * 512]
                                                .rearrange("p (h d) -> p h d", d=2 * HD), AX.X,
                                                ALU.add).then_inc(o_step, 1)
                    if back and n == 5:
                        dve.wait_ge(o_step, o0 + (2 - O_STEPS))
                        nc.vector.tensor_scalar(ms[:, :], ms[:, :], 1.0 / (2 * HD), EPS, ALU.mult,
                                                ALU.add).then_inc(o_step, 1)
                    if end and n == 3:
                        dve.wait_ge(y_full, b * 2 - 4)
                        nc.vector.tensor_tensor(x1[:, b - 3, :], psW[:, :], x1[:, b - 3, :], ALU.add).then_inc(x_done, 1)
                        dve.wait_ge(x_done, b - 2)
                        norm.tile_stats(x1, b - 3)
                    if back and n == 6:
                        dve.wait_ge(root_done, b)
                        nc.vector.tensor_tensor(nt[:, :], root[:, :], root[:, :], ALU.mult).then_inc(o_step, 1)
                        dve.wait_ge(o_step, o0 + (4 - O_STEPS))
                        nc.vector.scalar_tensor_tensor(out=nt[:, :], in0=nt[:, :], scalar=-0.5, in1=ms[:, :],
                                                       op0=ALU.mult, op1=ALU.mult).then_inc(o_step, 1)
                        dve.wait_ge(o_step, o0 + (5 - O_STEPS))
                        nc.vector.scalar_tensor_tensor(out=nt[:, :], in0=nt[:, :], scalar=1.5, in1=root[:, :],
                                                       op0=ALU.add, op1=ALU.mult).then_inc(o_step, 1)

            batches(dve, batch)


def experts(nc, w, out, shared, norm):
    with ExitStack() as ctx:
        def sb(name, shape, dt=F32):
            return ctx.enter_context(nc.sbuf_tensor(name, shape, dt))

        def sem(name):
            return ctx.enter_context(nc.semaphore(name))

        ident, x2, wn, w_in = shared.ident, shared.x1, shared.experts, shared.expert_in
        xn = sb("f_xn", [P, B, D])
        xT = [sb(f"f_xT{i}", [P, KD, TOK], F32R) for i in range(2)]
        gw = sb("f_gw", [P, KD, NE])
        gws = [sb(f"f_gws{i}", [P, KD, NE], F32R) for i in range(2)]
        gb_row = sb("f_gb_row", [1, NE])
        gb = sb("f_gb", [P, NE])
        zT = sb("f_zT", [NE, TOK])
        z = sb("f_z", [P, B, NE])
        sel = sb("f_sel", [P, B, NE])
        r1 = sb("f_r1", [P, B])
        r2 = sb("f_r2", [P, B])
        gate = sb("f_gate", [P, NE, B])
        gateT = sb("f_gateT", [NE, TOK])
        eb = sb("f_eb", [NE, D])
        ws = [sb(f"f_ws{i}", [P, 2, KD, D], F32R) for i in range(2)]
        bank = [ctx.enter_context(nc.psum_tensor(f"f_ps{i}", [P, 512], F32)) for i in range(6)]
        psG = ctx.enter_context(nc.psum_tensor("f_psG", [P, 512], F32))
        s_in = sem("f_small_in")
        gb_ready = sem("f_gb_ready")
        normed = sem("f_normed")
        x_full = sem("f_x_full")
        x_hi = sem("f_x_hi")
        x_lo = sem("f_x_lo")
        gw_hi = sem("f_gw_hi")
        gw_lo = sem("f_gw_lo")
        zT_full = sem("f_zT_full")
        zT_done = sem("f_zT_done")
        z_full = sem("f_z_full")
        z_step = sem("f_z_step")
        z_exp = sem("f_z_exp")
        t_full = sem("f_t_full")
        t_done = sem("f_t_done")
        y_full = sem("f_y_full")
        y_done = sem("f_y_done")
        w_hi = sem("f_w_hi")
        w_lo = sem("f_w_lo")
        out_sem = sem("f_out")
        Z_STEPS = 12
        NBANK = len(bank)
        assert B * NE % 2 == 0
        block = ctx.enter_context(nc.Block())

        @block.sync
        def _(sp):
            def load_expert(i, r):
                sp.wait_ge(w_lo, i * 2 + r + 1)
                sp.dma_start(wn[:, r, :, :], w["expert_w"][i * 2 + r].rearrange("(k p) d -> p k d", p=P)
                             ).then_inc(w_in[r], 16)

            with nc.allow_non_contiguous_dma(reason="the gate's weights, 16 KB"):
                sp.dma_start(gw[:, :, :], w["gate_w"].rearrange("(k p) e -> p k e", p=P)).then_inc(s_in, 16)
            sp.dma_start(gb_row[:, :], w["gate_b"].rearrange("(a e) -> a e", a=1)).then_inc(s_in, 16)
            sp.dma_start(eb[:, :], w["expert_b"]).then_inc(s_in, 16)
            with sp.Fori(1, NE // 2) as i:
                for r in range(2):
                    load_expert(i, r)
            for t in range(B):
                sp.wait_ge(y_done, (1 + NE) * B + t + 1)
                sp.dma_start(out[t], x2[:, t, :]).then_inc(out_sem, 16)
            sp.wait_ge(out_sem, 16 * B)

        @block.gpsimd
        def _(pool):
            pool.sem_inc(w_lo, 2)
            pool.wait_ge(s_in, 48)
            nc.gpsimd.partition_broadcast(gb[:, :], gb_row[:, :], P).then_inc(gb_ready, 1)
            with pool.Fori(0, NE // 2) as i:
                for r in range(2):
                    pool.wait_ge(w_hi, i * 2 + (r + 1))
                    nc.gpsimd.tensor_tensor(ws[1][:, r, :, :], wn[:, r, :, :], f32(ws[0][:, r, :, :]),
                                            ALU.subtract).then_inc(w_lo, 1)

        @block.tensor
        def _(pe):
            u = 0
            for half in range(2):
                pe.wait_ge(normed, 4 * half + 4)
                u = transpose_units(nc, pe, bank, ident[:, :], xn[:, 4 * half:4 * half + 4, :], 4, u, x_full, x_lo)
            pe.wait_ge(x_lo, 8)
            pe.wait_ge(gw_lo, 1)
            for half in range(2):
                for k in range(KD):
                    last = product(nc, bank[2 + half][0:NE, :], [a[:, k, :] for a in gws],
                                   [a[:, k, half * 512:(half + 1) * 512] for a in xT], k == 0, k == KD - 1)
                last.then_inc(zT_full, 1)
            pe.wait_ge(zT_done, 2)
            for t in range(B):
                last = nc.tensor.transpose(psG[:, t * NE:(t + 1) * NE], zT[:, t * P:(t + 1) * P], ident[0:NE, 0:NE])
            last.then_inc(z_full, 1)
            with pe.Fori(0, NE // 2) as i:
                for r in range(2):
                    pe.wait_ge(w_lo, i * 2 + (r + 1 + 2))
                    for t in range(B):
                        n = r * B + t
                        pe.wait_ge(y_done, i * (2 * B) + (B + n - 4 + 1))
                        for k in range(KD):
                            last = product(nc, bank[n % 4][:, :], [a[:, k, t * P:(t + 1) * P] for a in xT],
                                           [a[:, r, k, :] for a in ws], k == 0, k == KD - 1)
                        last.then_inc(y_full, 1)
            for half in range(2):
                for t in range(4):
                    last = nc.tensor.transpose(bank[4 + half][0:NE, t * P:(t + 1) * P], gate[:, :, 4 * half + t],
                                               ident[:, :])
                last.then_inc(t_full, 1)
            for t in range(B):
                pe.wait_ge(y_done, (NE + 1) * B + t - 4 + 1)
                pe.wait_ge(t_done, t // 4 + 1)
                nc.tensor.matmul(bank[t % 4][:, :], gateT[:, t * P:(t + 1) * P], eb[:, :],
                                 start=True, stop=True).then_inc(y_full, 1)

        @block.scalar
        def _(act):
            norm.scalar(act, 1)

            def weights_hi(i, r):
                act.wait_ge(w_in[r], i * 16 + 16)
                act.wait_ge(y_full, i * (2 * B) + (r + 1) * B)
                nc.scalar.activation(ws[0][:, r, :, :].rearrange("p k d -> p (k d)"),
                                     wn[:, r, :, :].rearrange("p k d -> p (k d)"), ACT.Copy).then_inc(w_hi, 1)

            act.wait_ge(s_in, 48)
            nc.scalar.activation(gws[0][:, :, :], gw[:, :, :], ACT.Copy).then_inc(gw_hi, 1)
            for u in range(8):
                if u == 4:
                    weights_hi(0, 0)
                act.wait_ge(x_full, u + 1)
                half, k = u // 4, u % 4
                nc.scalar.activation(xT[0][:, k, half * 512:(half + 1) * 512], bank[u % NBANK][:, :],
                                     ACT.Copy).then_inc(x_hi, 1)
            for half in range(2):
                act.wait_ge(zT_full, half + 1)
                nc.scalar.activation(zT[:, half * 512:(half + 1) * 512], bank[2 + half][0:NE, :],
                                     ACT.Copy).then_inc(zT_done, 1)
            act.wait_ge(z_step, 3)
            nc.scalar.activation(z[:, :, :], z[:, :, :], ACT.Exp).then_inc(z_exp, 1)
            weights_hi(0, 1)
            with act.Fori(1, NE // 2) as i:
                for r in range(2):
                    weights_hi(i, r)
            for half in range(2):
                act.wait_ge(t_full, half + 1)
                nc.scalar.activation(gateT[:, half * 512:(half + 1) * 512], bank[4 + half][0:NE, :],
                                     ACT.Copy).then_inc(t_done, 1)

        @block.vector
        def _(dve):
            dve.sem_inc(y_full, 2 * B)
            dve.sem_inc(y_done, B)
            norm.done(dve, 0)
            for t in range(B // 2):
                norm.apply(x2[:, t, :], xn[:, t, :], t).then_inc(normed, 1)
            norm.vector(dve, 1)
            norm.done(dve, 1)
            for t in range(B // 2, B):
                norm.apply(x2[:, t, :], xn[:, t, :], t).then_inc(normed, 1)
            dve.wait_ge(gw_hi, 1)
            nc.vector.tensor_tensor(gws[1][:, :, :], gw[:, :, :], f32(gws[0][:, :, :]),
                                    ALU.subtract).then_inc(gw_lo, 1)
            for u in range(8):
                dve.wait_ge(x_hi, u + 1)
                half, k = u // 4, u % 4
                part = slice(half * 512, (half + 1) * 512)
                nc.vector.tensor_tensor(xT[1][:, k, part], bank[u % NBANK][:, :], f32(xT[0][:, k, part]),
                                        ALU.subtract).then_inc(x_lo, 1)

            def over_experts(row):
                return row[:, :].rearrange("p (t o) -> p t o", o=1).broadcast_to([P, B, NE])

            dve.wait_ge(z_full, 1)
            dve.wait_ge(gb_ready, 1)
            nc.vector.tensor_tensor(z[:, :, :], psG[:, 0:B * NE].rearrange("p (t e) -> p t e", t=B),
                                    gb[:, :].rearrange("p (o e) -> p o e", o=1).broadcast_to([P, B, NE]),
                                    ALU.add).then_inc(z_step, 1)
            dve.wait_ge(z_step, 1)
            nc.vector.tensor_reduce(r1[:, :], z[:, :, :], AX.X, ALU.max).then_inc(z_step, 1)
            dve.wait_ge(z_step, 2)
            nc.vector.tensor_tensor(z[:, :, :], z[:, :, :], over_experts(r1), ALU.subtract).then_inc(z_step, 1)
            dve.wait_ge(z_exp, 1)
            nc.vector.tensor_reduce(r1[:, :], z[:, :, :], AX.X, ALU.add).then_inc(z_step, 1)
            dve.wait_ge(z_step, 4)
            nc.vector.reciprocal(r2[:, :], r1[:, :]).then_inc(z_step, 1)
            dve.wait_ge(z_step, 5)
            nc.vector.tensor_tensor(z[:, :, :], z[:, :, :], over_experts(r2), ALU.mult).then_inc(z_step, 1)
            dve.wait_ge(z_step, 6)
            nc.vector.scalar_tensor_tensor(out=sel[:, :, :], in0=z[:, :, :], scalar=THRESHOLD, in1=z[:, :, :],
                                           op0=ALU.is_ge, op1=ALU.mult).then_inc(z_step, 1)
            dve.wait_ge(z_step, 7)
            nc.vector.tensor_reduce(r1[:, :], sel[:, :, :], AX.X, ALU.add).then_inc(z_step, 1)
            dve.wait_ge(z_step, 8)
            nc.vector.tensor_scalar(r2[:, :], r1[:, :], 0.0, None, ALU.is_equal).then_inc(z_step, 1)
            dve.wait_ge(z_step, 9)
            nc.vector.tensor_tensor(r2[:, :], r2[:, :], r1[:, :], ALU.add).then_inc(z_step, 1)
            dve.wait_ge(z_step, 10)
            nc.vector.reciprocal(r1[:, :], r2[:, :]).then_inc(z_step, 1)
            dve.wait_ge(z_step, 11)
            nc.vector.tensor_tensor(gate[:, :, :].rearrange("p e t -> p t e"), sel[:, :, :], over_experts(r1),
                                    ALU.mult).then_inc(z_step, 1)
            dve.wait_ge(z_step, Z_STEPS)
            with dve.Fori(0, NE // 2) as i:
                for r in range(2):
                    for t in range(B):
                        n = r * B + t
                        dve.wait_ge(y_full, i * (2 * B) + (2 * B + n + 1))
                        dve.wait_ge(y_done, i * (2 * B) + (n + 1))
                        nc.vector.scalar_tensor_tensor(out=x2[:, t, :], in0=bank[n % 4][:, :],
                                                       scalar=gate[:, i * 2 + r, t:t + 1], in1=x2[:, t, :],
                                                       op0=ALU.mult, op1=ALU.add).then_inc(y_done, 1)
            for t in range(B):
                dve.wait_ge(y_full, (2 + NE) * B + t + 1)
                dve.wait_ge(y_done, NE * B + t + 1)
                nc.vector.tensor_tensor(x2[:, t, :], bank[t % 4][:, :], x2[:, t, :], ALU.add).then_inc(y_done, 1)


def perceiver_layer(nc, x, ctx_in, wx, wa, wf, out):
    q_d = nc.dram_tensor("q_scratch", [G, B, P, 2, P], F32R).ap()
    o_d = nc.dram_tensor("o_scratch", [G, B, P, P], F32).ap()
    q2_d = nc.dram_tensor("q2_scratch", [B, 2, P, KB // 2, 2, P], F32R).ap()
    k2_d = nc.dram_tensor("k2_scratch", [B, 2, P, KB // 2, 2, P], F32R).ap()
    with ExitStack() as ctx:
        shared = Shared(nc, ctx)
        with ExitStack() as inner:
            wkT = [inner.enter_context(nc.sbuf_tensor(f"wkT{i}", [P, KD, D], F32R)) for i in range(2)]
            wvT = [inner.enter_context(nc.sbuf_tensor(f"wvT{i}", [P, KD, D], F32R)) for i in range(2)]
            cin = inner.enter_context(nc.sbuf_tensor("cin", [P, 2, 2, D], F32))
            queries_and_weights(nc, x, ctx_in, wx, q_d, wkT, wvT, cin, shared)
            cross_attention(nc, x, ctx_in, wx, q_d, o_d, wkT, wvT, cin, shared)
        norm = Norm(nc, ctx, "ffn_norm", ((0, B - 2), (B - 2, B)))
        with ExitStack() as inner:
            v2 = inner.enter_context(nc.sbuf_tensor("v2", [P, B, W2], F32))
            with ExitStack() as weights:
                wn = weights.enter_context(nc.sbuf_tensor("wn", [P, 2, KB, D], F32))
                output_projection(nc, wx, wa, o_d, wn, shared)
                self_projections(nc, wa, q2_d, k2_d, v2, wn, shared)
            differential_attention(nc, wa, wf, q2_d, k2_d, v2, shared, norm)
        experts(nc, wf, out, shared, norm)


_XATTN = ("wq", "bq", "wk", "bk", "wv", "bv", "wo", "bo")
_ATTN = ("Wq", "Wk", "Wv", "Wo", "lq1", "lk1", "lq2", "lk2", "rms_scale")
_FFN = ("gate_w", "gate_b", "expert_w", "expert_b")
_INS = (["x", "ctx_1024"] + [f"L0_xattn_{n}" for n in _XATTN] + [f"L0_attn_{n}" for n in _ATTN]
        + [f"L0_ffn_{n}" for n in _FFN])


def kernel(**inputs):
    import concourse.bacc as _bacc
    from concourse.bass_utils import run_bass_kernel_spmd as _run

    nc = _bacc.Bacc("TRN2", target_bir_lowering=False, num_devices=1)
    arrays, aps = {}, {}
    for name in _INS:
        a = np.ascontiguousarray(inputs[name])
        arrays[f"in_{name}"] = a
        aps[name] = nc.dram_tensor(f"in_{name}", a.shape, mybir.dt.from_np(a.dtype), kind="ExternalInput").ap()
    out = nc.dram_tensor("out_0", [B, P, D], F32, kind="ExternalOutput").ap()
    perceiver_layer(nc, aps["x"], aps["ctx_1024"], {n: aps[f"L0_xattn_{n}"] for n in _XATTN},
                    {n: aps[f"L0_attn_{n}"] for n in _ATTN}, {n: aps[f"L0_ffn_{n}"] for n in _FFN}, out)
    r = _run(nc, [arrays], core_ids=[0])
    return r.results[0]["out_0"]
```
